# Optimizing a Trainium2 kernel written in Bass

```python
import numpy as np
import jax
import jax.numpy as jnp

def _softmax(x, axis=-1):
    return jax.nn.softmax(x, axis=axis)

def _gelu(x):
    return jax.nn.gelu(x, approximate=True)

def _silu(x):
    return jax.nn.silu(x)

def _sigmoid(x):
    return jax.nn.sigmoid(x)

def _layernorm(x, axis=-1, eps=1e-05):
    m = jnp.mean(x, axis=axis, keepdims=True)
    v = jnp.var(x, axis=axis, keepdims=True)
    return (x - m) / jnp.sqrt(v + eps)

def _scatter_add(tgt, idx, src, axis=0):
    return tgt.at[idx].add(src)

def _segment_sum(src, seg, n):
    return jax.ops.segment_sum(src, seg, n)
kernel_name = 'mk_seq_postln_d1_jaxref_r4_a90ee1'

def setup_inputs(seed: int=0):
    np.random.seed(seed)
    _w = jnp.asarray

    def _L0_attn_setup():
        import jax, jax.numpy as jnp
        import numpy as np
        B, S, DM = (2, 512, 512)
        H, KVH, HD = (16, 4, 128)
        REP = H // KVH
        ROPE_BASE = 10000.0
        EPS = 1e-06

        def _rope_tables(seq_len, dim):
            inv_freq = 1.0 / ROPE_BASE ** (jnp.arange(0, dim, 2, dtype=jnp.float32) / dim)
            t = jnp.arange(seq_len, dtype=jnp.float32)
            freqs = jnp.outer(t, inv_freq)
            emb = jnp.concatenate([freqs, freqs], -1)
            return (jnp.cos(emb), jnp.sin(emb))

        def _rotate_half(x):
            d = x.shape[-1] // 2
            return jnp.concatenate([-x[..., d:], x[..., :d]], axis=-1)
        key = jax.random.key(seed)
        k0, k1, k2, k3, k4 = jax.random.split(key, 5)
        w = lambda k, o, i: jax.random.normal(k, (o, i), jnp.float32) * (1.0 / np.sqrt(i))
        return {'x': jax.random.normal(k0, (B, S, DM), jnp.float32), 'Wq': w(k1, H * HD, DM), 'Wk': w(k2, KVH * HD, DM), 'Wv': w(k3, KVH * HD, DM), 'Wo': w(k4, DM, H * HD)}
    _L0_attn_in = _L0_attn_setup()

    def _L0_ffn_setup():
        import jax, jax.numpy as jnp
        import numpy as np
        HIDDEN = 512
        INTER = 2048
        SCALE = 64.0

        def fwht(x):
            orig_shape = x.shape
            n = orig_shape[-1]
            x = x.reshape(-1, n)
            h = 1
            while h < n:
                x = x.reshape(-1, n // (2 * h), 2, h)
                a, b = (x[:, :, 0, :], x[:, :, 1, :])
                x = jnp.stack([a + b, a - b], axis=2).reshape(-1, n)
                h *= 2
            return (x / jnp.sqrt(jnp.asarray(n, x.dtype))).reshape(orig_shape)
        key = jax.random.key(seed)
        ks = jax.random.split(key, 8)
        inp = jax.random.normal(ks[0], (4, 512, HIDDEN), dtype=jnp.float32)
        SU_ug = jnp.where(jax.random.bernoulli(ks[1], 0.5, (HIDDEN,)), 1.0, -1.0).astype(jnp.float32)
        SU_dp = jnp.where(jax.random.bernoulli(ks[2], 0.5, (INTER,)), 1.0, -1.0).astype(jnp.float32)
        Wscale_ug = jax.random.uniform(ks[3], (2 * INTER,), jnp.float32, 0.5, 1.5)
        Wscale_dp = jax.random.uniform(ks[4], (HIDDEN,), jnp.float32, 0.5, 1.5)
        W_up = jax.random.normal(ks[5], (INTER, HIDDEN), dtype=jnp.float32) * 0.02
        W_gate = jax.random.normal(ks[6], (INTER, HIDDEN), dtype=jnp.float32) * 0.02
        W_down = jax.random.normal(ks[7], (HIDDEN, INTER), dtype=jnp.float32) * 0.02
        return {'input': inp, 'SU_ug': SU_ug, 'SU_dp': SU_dp, 'Wscale_ug': Wscale_ug, 'Wscale_dp': Wscale_dp, 'W_up': W_up, 'W_gate': W_gate, 'W_down': W_down}
    _L0_ffn_in = _L0_ffn_setup()
    _d = {'L0_attn_x': _L0_attn_in['x'], 'L0_attn_Wq': _L0_attn_in['Wq'], 'L0_attn_Wk': _L0_attn_in['Wk'], 'L0_attn_Wv': _L0_attn_in['Wv'], 'L0_attn_Wo': _L0_attn_in['Wo'], 'L0_ffn_SU_ug': _L0_ffn_in['SU_ug'], 'L0_ffn_SU_dp': _L0_ffn_in['SU_dp'], 'L0_ffn_Wscale_ug': _L0_ffn_in['Wscale_ug'], 'L0_ffn_Wscale_dp': _L0_ffn_in['Wscale_dp'], 'L0_ffn_W_up': _L0_ffn_in['W_up'], 'L0_ffn_W_gate': _L0_ffn_in['W_gate'], 'L0_ffn_W_down': _L0_ffn_in['W_down']}
    _x0 = _d['L0_attn_x']
    _d['L0_attn_x'] = jax.random.normal(jax.random.fold_in(jax.random.key(seed), 1), (1, 4096, 512), dtype=_x0.dtype)
    del _x0
    return _d

def reference(L0_attn_x, L0_attn_Wq, L0_attn_Wk, L0_attn_Wv, L0_attn_Wo, L0_ffn_SU_ug, L0_ffn_SU_dp, L0_ffn_Wscale_ug, L0_ffn_Wscale_dp, L0_ffn_W_up, L0_ffn_W_gate, L0_ffn_W_down):

    def _L0_attn_ref(x, Wq, Wk, Wv, Wo):
        import jax, jax.numpy as jnp
        import numpy as np
        B, S, DM = (2, 512, 512)
        H, KVH, HD = (16, 4, 128)
        REP = H // KVH
        ROPE_BASE = 10000.0
        EPS = 1e-06

        def _rope_tables(seq_len, dim):
            inv_freq = 1.0 / ROPE_BASE ** (jnp.arange(0, dim, 2, dtype=jnp.float32) / dim)
            t = jnp.arange(seq_len, dtype=jnp.float32)
            freqs = jnp.outer(t, inv_freq)
            emb = jnp.concatenate([freqs, freqs], -1)
            return (jnp.cos(emb), jnp.sin(emb))

        def _rotate_half(x):
            d = x.shape[-1] // 2
            return jnp.concatenate([-x[..., d:], x[..., :d]], axis=-1)
        bsz, seq_len, _ = x.shape
        q = (x @ Wq.T).reshape(bsz, seq_len, H, HD).transpose(0, 2, 1, 3)
        k = (x @ Wk.T).reshape(bsz, seq_len, KVH, HD).transpose(0, 2, 1, 3)
        v = (x @ Wv.T).reshape(bsz, seq_len, KVH, HD).transpose(0, 2, 1, 3)
        cos, sin = _rope_tables(seq_len, HD)
        cos, sin = (cos[None, None], sin[None, None])
        q = q * cos + _rotate_half(q) * sin
        k = k * cos + _rotate_half(k) * sin
        k = jnp.repeat(k, REP, axis=1)
        v = jnp.repeat(v, REP, axis=1)
        qf = jax.nn.elu(q) + 1.0
        kf = jax.nn.elu(k) + 1.0
        qf_t = qf.transpose(2, 0, 1, 3)
        kf_t = kf.transpose(2, 0, 1, 3)
        v_t = v.transpose(2, 0, 1, 3)

        def step(carry, inp):
            state, z = carry
            q_s, k_s, v_s = inp
            state = state + k_s[..., :, None] * v_s[..., None, :]
            z = z + k_s
            num = jnp.einsum('bhe,bhed->bhd', q_s, state)
            den = jnp.einsum('bhe,bhe->bh', q_s, z)[..., None] + EPS
            return ((state, z), num / den)
        init = (jnp.zeros((bsz, H, HD, HD), x.dtype), jnp.zeros((bsz, H, HD), x.dtype))
        _, out = jax.lax.scan(step, init, (qf_t, kf_t, v_t))
        out = out.transpose(1, 0, 2, 3).reshape(bsz, seq_len, H * HD)
        return out @ Wo.T

    def _L0_ffn_ref(input, SU_ug, SU_dp, Wscale_ug, Wscale_dp, W_up, W_gate, W_down):
        import jax, jax.numpy as jnp
        import numpy as np
        HIDDEN = 512
        INTER = 2048
        SCALE = 64.0

        def fwht(x):
            orig_shape = x.shape
            n = orig_shape[-1]
            x = x.reshape(-1, n)
            h = 1
            while h < n:
                x = x.reshape(-1, n // (2 * h), 2, h)
                a, b = (x[:, :, 0, :], x[:, :, 1, :])
                x = jnp.stack([a + b, a - b], axis=2).reshape(-1, n)
                h *= 2
            return (x / jnp.sqrt(jnp.asarray(n, x.dtype))).reshape(orig_shape)
        n = SU_ug.shape[0]
        x = input.reshape(-1, n)
        x = fwht(x * SU_ug) / SCALE
        x_up = x @ W_up.T * (Wscale_ug[:INTER] * SCALE)
        x_gate = x @ W_gate.T * (Wscale_ug[INTER:] * SCALE)
        x = jax.nn.silu(x_gate) * x_up
        x = fwht(x * SU_dp) / SCALE
        x = x @ W_down.T * (Wscale_dp * SCALE)
        return x.reshape(input.shape)
    x = L0_attn_x
    x = _layernorm(x + _L0_attn_ref(x, L0_attn_Wq, L0_attn_Wk, L0_attn_Wv, L0_attn_Wo), axis=-1)
    x = _layernorm(x + _L0_ffn_ref(x, L0_ffn_SU_ug, L0_ffn_SU_dp, L0_ffn_Wscale_ug, L0_ffn_Wscale_dp, L0_ffn_W_up, L0_ffn_W_gate, L0_ffn_W_down), axis=-1)
    return x

_drawn_inputs = setup_inputs


def setup_inputs(seed=0):
    import zlib

    import numpy as np

    out = dict(_drawn_inputs(seed))
    spreads = {}
    factors = {}
    for name, (base, spread) in spreads.items():
        noise = np.random.default_rng([zlib.crc32(name.encode()), seed]).standard_normal(out[name].shape)
        drawn = base * np.exp(spread * noise) if base else spread * noise
        out[name] = jnp.asarray(drawn.astype(out[name].dtype))
    for name, factor in factors.items():
        out[name] = (out[name] * factor).astype(out[name].dtype)
    return out
```

```python
from contextlib import ExitStack

import numpy as np

import concourse.bass as bass
from concourse import mybir

F32 = mybir.dt.float32
F32R = mybir.dt.float32r
ALU = mybir.AluOpType
ACT = mybir.ActivationFunctionType
AX_X = mybir.AxisListType.X

P = 128
T = 4096
D = 512
DC = D // P
H, KV, HD = 16, 4, 128
G = H // KV
MT = 512
NM = T // MT
CH = 128
NCH = MT // CH
F = 2048
FB = F // P
EPS = 1e-5

def f32(ap):
    return ap.bitcast(F32)




def tile_events():
    ev = [("J", 0, 0), ("V", 0), ("J", 0, 1), ("V", 1), ("J", 0, 2), ("J", 0, 3), ("J", 0, 4), ("V", 2), ("F", 0, 0),
          ("V", 3), ("F", 0, 1), ("T", 0), ("SC", 0)]
    for u in range(KV * NCH):
        g, c = divmod(u, NCH)
        after = [("SC", u + 1)] if u + 1 < KV * NCH else []
        n = g + 1
        if n == KV:
            ev += after
        elif c == 0:
            ev += [("J", n, 0)] + after + [("J", n, 1), ("J", n, 2)]
        elif c == 1:
            ev += [("J", n, 3)] + after + [("J", n, 4)]
        elif c == 2:
            ev += [("F", n, 0)] + after + [("F", n, 1)]
        else:
            ev += [("T", n)] + after
        ev.append(("U", u))
    return ev


EVENTS = tile_events()
NU = KV * NCH
JOBS = [e for e in EVENTS if e[0] in "JVT"]
NJ = len(JOBS)
NT = 3
NR = KV * (G + 1)
assert NJ % 2 == 0 and [e[1] for e in EVENTS if e[0] == "J"] == sorted(e[1] for e in EVENTS if e[0] == "J")


SLOTS = [e for e in EVENTS if e[0] in "JF"]


def feature_job_before(e, k):
    n = SLOTS.index(e) - k
    return SLOTS[n] if n >= 0 and SLOTS[n][0] == "J" else None


def job_index(e):
    return JOBS.index(e)


def rope_index(e):
    return e[1] * (G + 1) + e[2]


def phase_a(nc, xT, wq, wk, wv, cosT, sinT, consts, num_d, den_d):
    ctx = ExitStack()
    with ctx:
        def sb(name, shape, dt=F32, c=ctx):
            return c.enter_context(nc.sbuf_tensor(name, shape, dt))

        def sem(name):
            return ctx.enter_context(nc.semaphore(name))

        wqh, wql = sb("wqh", [P, H, DC, HD], F32R), sb("wql", [P, H, DC, HD], F32R)
        wkh, wkl = sb("wkh", [P, KV, DC, HD], F32R), sb("wkl", [P, KV, DC, HD], F32R)
        wvh, wvl = sb("wvh", [P, DC, KV * HD], F32R), sb("wvl", [P, DC, KV * HD], F32R)
        xh, xl = sb("xh", [P, DC, MT], F32R), sb("xl", [P, DC, MT], F32R)
        xst = sb("xst", [P, 2, MT])
        cosb, sinb = sb("cosb", [P, MT]), sb("sinb", [P, MT])
        Sh, Sl = sb("Sh", [P, HD], F32R), sb("Sl", [P, HD], F32R)
        Zt = sb("Zt", [P, NCH, P], F32R)
        ident = sb("ident", [P, P])
        ones0 = sb("ones0", [P, P], F32R)
        zall = sb("zall", [P, KV, NCH + 1])
        zs = sb("zs", [P, NCH])
        ones4 = sb("ones4", [P, NCH])
        pj = [ctx.enter_context(nc.psum_tensor(f"pj{i}", [P, MT], F32)) for i in range(2)]
        psc = [ctx.enter_context(nc.psum_tensor(f"psc{i}", [P, G * CH], F32)) for i in range(2)]
        pnum = [ctx.enter_context(nc.psum_tensor(f"pnum{i}", [P, G * CH], F32)) for i in range(2)]
        pden = ctx.enter_context(nc.psum_tensor("pden", [P, G * CH], F32))
        pst = ctx.enter_context(nc.psum_tensor("pst", [P, KV * HD], F32))

        w_in = [sem(f"w_in{i}") for i in range(6)]
        c_in, w_hi, w_lo, zeroed = sem("c_in"), sem("w_hi"), sem("w_lo"), sem("zeroed")
        xst_in = [sem("xst_in0"), sem("xst_in1")]
        x_hi, xt_ready = sem("x_hi"), sem("xt_ready")
        s_hi, s_lo = sem("s_hi"), sem("s_lo")
        cs_in = sem("cs_in")
        passed = sem("passed_a")
        job_done, bank_free = sem("job_done"), sem("bank_free")
        shifted, sin_done, rot_done = sem("shifted"), sem("sin_done"), sem("rot_done")
        relu_done, f_done, hi_done = sem("relu_done"), sem("f_done"), sem("hi_done")
        lo_done = sem("lo_done")
        v_hi, t_hi = sem("v_hi"), sem("t_hi")
        z_sum, z_move, z_scan, z_hi, z_lo = (sem("z_sum"), sem("z_move"), sem("z_scan"), sem("z_hi"), sem("z_lo"))
        sc_done, a_hi, a_ready = sem("sc_done"), sem("a_hi"), sem("a_ready")
        sc_free = sem("sc_free")
        num_done, den_done = sem("num_done"), sem("den_done")
        num_free = sem("num_free")
        den_free = sem("den_free")
        unit_done = sem("unit_done")
        num_out = [sem("num_out0"), sem("num_out1")]
        den_out = sem("den_out")
        pro = ExitStack()
        with pro:
            stage = sb("stage", [P, 6, 2048], F32, pro)
            parts = [(wq[:, 4 * i:4 * i + 4].rearrange("p h c e -> p (h c e)"),
                      wqh[:, 4 * i:4 * i + 4].rearrange("p h c e -> p (h c e)"),
                      wql[:, 4 * i:4 * i + 4].rearrange("p h c e -> p (h c e)")) for i in range(4)]
            parts = [(wk.rearrange("p h c e -> p (h c e)"), wkh[:].rearrange("p h c e -> p (h c e)"),
                      wkl[:].rearrange("p h c e -> p (h c e)"))] + parts[:1] + \
                    [(wv.rearrange("p c n -> p (c n)"), wvh[:].rearrange("p c n -> p (c n)"),
                      wvl[:].rearrange("p c n -> p (c n)"))] + parts[1:]
            block = pro.enter_context(nc.Block())

            @block.sync
            def _(sp):
                sp.dma_start(ident[:, :], consts[:, 0:P]).then_inc(c_in, 16)
                for q in range(2):
                    sp.dma_start(xst[:, q, :], xT[0, :, q, :]).then_inc(xst_in[q], 16)
                for i, (src, _, _) in enumerate(parts):
                    sp.dma_start(stage[:, i, :], src).then_inc(w_in[i], 16)
                    if i < 2:
                        sp.wait_ge(xt_ready, i + 1)
                        sp.dma_start(xst[:, i, :], xT[0, :, i + 2, :]).then_inc(xst_in[i], 16)
                sp.dma_start(cosb[:, :], cosT[:, 0:MT]).then_inc(cs_in, 16)
                sp.dma_start(sinb[:, :], sinT[:, 0:MT]).then_inc(cs_in, 16)
                sp.wait_ge(cs_in, 32)
                sp.wait_ge(c_in, 16)

            @block.gpsimd
            def _(pool):
                nc.gpsimd.memset(zall[:], 0.0)
                nc.gpsimd.memset(ones4[:], 1.0)
                nc.gpsimd.memset(f32(Sh[:]), 0.0).then_inc(zeroed, 1)
                nc.gpsimd.memset(f32(Sl[:]), 0.0).then_inc(s_lo, 1)
                nc.gpsimd.memset(f32(Zt[:]), 0.0).then_inc(zeroed, 1)
                nc.gpsimd.memset(f32(ones0[:]), 0.0).then_inc(zeroed, 1)
                pool.wait_ge(zeroed, 3)
                nc.gpsimd.memset(f32(ones0[:, 0:1]), 1.0).then_inc(zeroed, 1)
                for s, ahead in ((bank_free, 2), (sc_free, 2), (num_free, 2), (den_free, 1), (unit_done, 2),
                                 (lo_done, NT), (num_out[0], 16), (num_out[1], 16), (den_out, 16)):
                    nc.gpsimd.sem_inc(s, ahead)

            @block.scalar
            def _(act):
                for q in range(DC):
                    act.wait_ge(xst_in[q % 2], 16 * (q // 2 + 1))
                    nc.scalar.activation(xh[:, q, :], xst[:, q % 2, :], ACT.Copy).then_inc(x_hi, 1)
                for i, (_, hi, _) in enumerate(parts):
                    act.wait_ge(w_in[i], 16)
                    nc.scalar.activation(hi, stage[:, i, :], ACT.Copy).then_inc(w_hi, 1)

            @block.vector
            def _(dve):
                for q in range(DC):
                    dve.wait_ge(x_hi, q + 1)
                    nc.vector.tensor_tensor(xl[:, q, :], xst[:, q % 2, :], f32(xh[:, q, :]),
                                            ALU.subtract).then_inc(xt_ready, 1)
                for i, (_, hi, lo) in enumerate(parts):
                    dve.wait_ge(w_hi, i + 1)
                    nc.vector.tensor_tensor(lo, stage[:, i, :], f32(hi), ALU.subtract).then_inc(w_lo, 1)

            @block.tensor
            def _(pe):
                pe.wait_ge(zeroed, 2)
                nc.tensor.matmul(pst[:, :], Sh[:, :], Zt[:].rearrange("p c n -> p (c n)"), start=True, stop=True,
                                 skip_group_check=True).then_inc(w_lo, 1)

        Vh, Vl = sb("Vh", [P, NCH, KV * HD], F32R), sb("Vl", [P, NCH, KV * HD], F32R)
        Qh = [sb(f"Qh{i}", [P, G + 1, MT], F32R) for i in range(2)]
        Ql = [sb(f"Ql{i}", [P, G + 1, MT], F32R) for i in range(2)]
        Kth, Ktl = sb("Kth", [P, NCH, HD], F32R), sb("Ktl", [P, NCH, HD], F32R)
        Kf = sb("Kf", [P, MT])
        ta = [sb(f"ta{i}", [P, MT]) for i in range(NT)]
        tb = [sb(f"tb{i}", [P, MT]) for i in range(NT)]
        Ah = [sb(f"Ah{i}", [P, G, CH], F32R) for i in range(2)]
        Al = [sb(f"Al{i}", [P, G, CH], F32R) for i in range(2)]
        no = [sb(f"no{i}", [P, G, CH]) for i in range(2)]
        dn = sb("dn", [2, G * CH])

        block = ctx.enter_context(nc.Block())

        @block.tensor
        def _(pe):
            with pe.Fori(0, NM) as m:
                for e in EVENTS:
                    if e[0] in "JVT":
                        n = job_index(e)
                        bank = pj[n % 2]
                        pe.wait_ge(bank_free, m * NJ + n + 1)
                    if e[0] == "J":
                        g, i = e[1:]
                        wh, wl = (wkh[:, g], wkl[:, g]) if i == 0 else (wqh[:, G * g + i - 1], wql[:, G * g + i - 1])
                        if (g, i) == (0, 0):
                            pe.wait_ge(xt_ready, m * DC + DC)
                        k = 0
                        for c in range(DC):
                            for w, x in ((wh, xh), (wh, xl), (wl, xh)):
                                last = nc.tensor.matmul(bank[:, :], w[:, c, :], x[:, c, :], start=(k == 0), stop=(k == 11))
                                k += 1
                        last.then_inc(job_done, 1)
                    elif e[0] == "V":
                        tok = slice(e[1] * CH, (e[1] + 1) * CH)
                        k = 0
                        for c in range(DC):
                            for x, w in ((xh, wvh), (xh, wvl), (xl, wvh)):
                                last = nc.tensor.matmul(bank[:, :], x[:, c, tok], w[:, c, :], start=(k == 0), stop=(k == 11))
                                k += 1
                        last.then_inc(job_done, 1)
                    elif e[0] == "T":
                        g = e[1]
                        pe.wait_ge(f_done, m * NR + g * (G + 1) + 1)
                        for c in range(NCH):
                            last = nc.tensor.transpose(bank[:, c * CH:(c + 1) * CH], Kf[:, c * CH:(c + 1) * CH], ident[:, :])
                        last.then_inc(job_done, 1)
                    elif e[0] == "F":
                        pass
                    elif e[0] == "SC":
                        g, c = divmod(e[1], NCH)
                        u = e[1]
                        tok = slice(c * CH, (c + 1) * CH)
                        qh, ql = Qh[g % 2], Ql[g % 2]
                        pe.wait_ge(lo_done, m * NR + (g + 1) * (G + 1) + NT)
                        pe.wait_ge(sc_free, m * NU + u + 1)
                        out = psc[u % 2][:, :].rearrange("p (h t) -> p h t", h=G)
                        for k, (a, b) in enumerate(((qh, qh), (qh, ql), (ql, qh))):
                            last = nc.tensor.matmul(out, a[:, 0, tok], b[:, 1:, tok], start=(k == 0), stop=(k == 2))
                        last.then_inc(sc_done, 1)
                    else:
                        g, c = divmod(e[1], NCH)
                        u = e[1]
                        tok = slice(c * CH, (c + 1) * CH)
                        hd = slice(g * HD, (g + 1) * HD)
                        qh, ql = Qh[g % 2], Ql[g % 2]
                        num = pnum[u % 2][:, :].rearrange("p (h t) -> p h t", h=G)
                        den = pden[:, :].rearrange("p (h t) -> p h t", h=G)
                        ah, al = Ah[u % 2], Al[u % 2]
                        pe.wait_ge(num_free, m * NU + u + 1)
                        if g == 0:
                            pe.wait_ge(bank_free, m * NJ + job_index(("V", c)) + 3)
                        pe.wait_ge(a_ready, m * NU + u + 1)
                        for k, (a, b) in enumerate(((Vh, ah), (Vh, al), (Vl, ah))):
                            nc.tensor.matmul(num, a[:, c, hd], b[:, :, :], start=(k == 0), stop=False)
                        pe.wait_ge(den_free, m * NU + u + 1)
                        nc.tensor.matmul(den, ones0[:, :], ah[:, :, :], start=True, stop=False)
                        nc.tensor.matmul(den, ones0[:, :], al[:, :, :], start=False, stop=False)
                        pe.wait_ge(s_lo, m * NU + u + 1)
                        for k, (a, b) in enumerate(((Sh, qh), (Sh, ql), (Sl, qh))):
                            last = nc.tensor.matmul(num, a[:, :], b[:, 1:, tok], start=False, stop=(k == 2))
                        last.then_inc(num_done, 1)
                        if c == 0:
                            pe.wait_ge(z_lo, m * KV + g + 1)
                        nc.tensor.matmul(den, Zt[:, c, :], qh[:, 1:, tok], start=False, stop=False)
                        nc.tensor.matmul(den, Zt[:, c, :], ql[:, 1:, tok], start=False, stop=True).then_inc(den_done, 1)
                        if c == 0:
                            pe.wait_ge(bank_free, m * NJ + job_index(("T", g)) + 3)
                        for k, (a, b) in enumerate(((Kth, Vh), (Kth, Vl), (Ktl, Vh))):
                            last = nc.tensor.matmul(pst[:, hd], a[:, c, :], b[:, c, hd], start=False, stop=(k == 2),
                                                    skip_group_check=True)
                        last.then_inc(unit_done, 1)

        @block.scalar
        def _(act):
            def exp_relu(e, m):
                r = rope_index(e)
                act.wait_ge(rot_done, m * NR + r + 1)
                nc.scalar.activation(tb[r % NT][:, :], ta[r % NT][:, :], ACT.Exp)
                nc.scalar.activation(ta[r % NT][:, :], ta[r % NT][:, :], ACT.Relu).then_inc(relu_done, 1)

            def feature_hi(e, m):
                r = rope_index(e)
                g, i = e[1:]
                src = Kf if i == 0 else tb[r % NT]
                act.wait_ge(f_done, m * NR + r + 1)
                nc.scalar.activation(Qh[g % 2][:, i, :], src[:, :], ACT.Copy).then_inc(hi_done, 1)

            with act.Fori(0, NM) as m:
                for e in EVENTS:
                    if e[0] == "J":
                        r = rope_index(e)
                        bank = pj[job_index(e) % 2]
                        act.wait_ge(job_done, m * NJ + job_index(e) + 1)
                        act.wait_ge(lo_done, m * NR + r + 1)
                        nc.scalar.activation(tb[r % NT][0:64, :], bank[64:128, :], ACT.Copy)
                        nc.scalar.activation(tb[r % NT][64:128, :], bank[0:64, :], ACT.Copy).then_inc(shifted, 1)
                    if e[0] in "JF":
                        if feature_job_before(e, 2):
                            feature_hi(feature_job_before(e, 2), m)
                        if feature_job_before(e, 1):
                            exp_relu(feature_job_before(e, 1), m)
                    elif e[0] == "V":
                        act.wait_ge(job_done, m * NJ + job_index(e) + 1)
                        nc.scalar.activation(Vh[:, e[1], :], pj[job_index(e) % 2][:, :], ACT.Copy).then_inc(v_hi, 1)
                    elif e[0] == "T":
                        g = e[1]
                        act.wait_ge(job_done, m * NJ + job_index(e) + 1)
                        if g == 0:
                            nc.scalar.activation(Kth[:].rearrange("p c e -> p (c e)"), pj[job_index(e) % 2][:, :],
                                                 ACT.Copy).then_inc(t_hi, 1)
                            act.wait_ge(z_scan, m * KV + 1)
                            nc.scalar.activation(Zt[:, :, 0], zall[:, 0, 0:NCH], ACT.Copy).then_inc(z_hi, 1)
                    elif e[0] == "SC":
                        u = e[1]
                        act.wait_ge(sc_done, m * NU + u + 1)
                        act.wait_ge(unit_done, m * NU + u + 1)
                        nc.scalar.activation(Ah[u % 2][:].rearrange("p h t -> p (h t)"), psc[u % 2][:, :],
                                             ACT.Copy).then_inc(a_hi, 1)
                    else:
                        u = e[1]
                        g, c = divmod(u, NCH)
                        gn = ((u + 1) % NU) // NCH
                        act.wait_ge(unit_done, m * NU + u + 3)
                        nc.scalar.activation(Sh[:, :], pst[:, gn * HD:(gn + 1) * HD], ACT.Copy).then_inc(s_hi, 1)
                        if c == 3 and g + 1 < KV:
                            nc.scalar.activation(Kth[:].rearrange("p c e -> p (c e)"),
                                                 pj[job_index(("T", g + 1)) % 2][:, :], ACT.Copy).then_inc(t_hi, 1)
                            act.wait_ge(z_scan, m * KV + g + 2)
                            nc.scalar.activation(Zt[:, :, 0], zall[:, g + 1, 0:NCH], ACT.Copy).then_inc(z_hi, 1)
                        if g == KV - 1:
                            act.wait_ge(xst_in[c % 2], m * 32 + 16 * (c // 2) + 48)
                            nc.scalar.activation(xh[:, c, :], xst[:, c % 2, :], ACT.Copy).then_inc(x_hi, 1)

        @block.vector
        def _(dve):
            def rotate(e, m):
                r = rope_index(e)
                dve.wait_ge(sin_done, m * NR + r + 1)
                dve.wait_ge(bank_free, m * NJ + job_index(e) + 3)
                nc.vector.tensor_tensor(ta[r % NT][:, :], ta[r % NT][:, :], tb[r % NT][:, :], ALU.add).then_inc(rot_done, 1)

            def elu(e, m):
                r = rope_index(e)
                i = e[2]
                dve.wait_ge(relu_done, m * NR + r + 1)
                dst = Kf if i == 0 else tb[r % NT]
                nc.vector.scalar_tensor_tensor(out=dst[:, :], in0=tb[r % NT][:, :], scalar=1.0, in1=ta[r % NT][:, :],
                                               op0=ALU.min, op1=ALU.add).then_inc(f_done, 1)

            def keys_lo(g, m):
                dve.wait_ge(t_hi, m * KV + g + 1)
                bank = pj[job_index(("T", g)) % 2]
                nc.vector.tensor_tensor(Ktl[:].rearrange("p c e -> p (c e)"), bank[:, :],
                                        f32(Kth[:].rearrange("p c e -> p (c e)")), ALU.subtract).then_inc(bank_free, 1)
                dve.wait_ge(z_hi, m * KV + g + 1)
                nc.vector.tensor_tensor(Zt[:, :, 1], zall[:, g, 0:NCH], f32(Zt[:, :, 0]), ALU.subtract).then_inc(z_lo, 1)

            with dve.Fori(0, NM) as m:
                for e in EVENTS:
                    if e[0] in "JF" and feature_job_before(e, 1):
                        rotate(feature_job_before(e, 1), m)
                    if e[0] == "J":
                        r = rope_index(e)
                        if r == 0:
                            dve.wait_ge(cs_in, m * 32 + 32)
                        dve.wait_ge(shifted, m * NR + r + 1)
                        nc.vector.tensor_tensor(ta[r % NT][:, :], pj[job_index(e) % 2][:, :], cosb[:, :],
                                                ALU.mult).then_inc(bank_free, 1)
                    if e[0] in "JF":
                        if feature_job_before(e, 1):
                            elu(feature_job_before(e, 1), m)
                    elif e[0] == "V":
                        dve.wait_ge(v_hi, m * NCH + e[1] + 1)
                        nc.vector.tensor_tensor(Vl[:, e[1], :], pj[job_index(e) % 2][:, :], f32(Vh[:, e[1], :]),
                                                ALU.subtract).then_inc(bank_free, 1)
                    elif e[0] == "T":
                        g = e[1]
                        dve.wait_ge(f_done, m * NR + g * (G + 1) + 1)
                        nc.vector.tensor_reduce(zs[:, :], Kf[:, :].rearrange("p (c t) -> p c t", c=NCH), AX_X,
                                                ALU.add).then_inc(z_sum, 1)
                        nc.vector.tensor_copy(zall[:, g, 0:1], zall[:, g, NCH:NCH + 1]).then_inc(z_move, 1)
                        dve.wait_ge(z_sum, m * KV + g + 1)
                        dve.wait_ge(z_move, m * KV + g + 1)
                        nc.vector.tensor_tensor_scan(zall[:, g, 1:NCH + 1], ones4[:, :], zs[:, :], zall[:, g, 0:1],
                                                     ALU.mult, ALU.add).then_inc(z_scan, 1)
                        if g == 0:
                            keys_lo(0, m)
                    elif e[0] == "SC":
                        u = e[1]
                        dve.wait_ge(a_hi, m * NU + u + 1)
                        nc.vector.tensor_tensor(Al[u % 2][:].rearrange("p h t -> p (h t)"), psc[u % 2][:, :],
                                                f32(Ah[u % 2][:].rearrange("p h t -> p (h t)")),
                                                ALU.subtract).then_inc(sc_free, 1)
                    else:
                        u = e[1]
                        g, c = divmod(u, NCH)
                        gn = ((u + 1) % NU) // NCH
                        dve.wait_ge(s_hi, m * NU + u + 1)
                        nc.vector.tensor_tensor(Sl[:, :], pst[:, gn * HD:(gn + 1) * HD], f32(Sh[:, :]),
                                                ALU.subtract).then_inc(s_lo, 1)
                        if c == 3 and g + 1 < KV:
                            keys_lo(g + 1, m)
                        dve.wait_ge(num_done, m * NU + u + 1)
                        dve.wait_ge(num_out[u % 2], m * (8 * NU) + 16 * (u // 2) + 16)
                        nc.vector.tensor_copy(no[u % 2][:].rearrange("p h t -> p (h t)"),
                                              pnum[u % 2][:, :]).then_inc(num_free, 1)
                        dve.wait_ge(den_done, m * NU + u + 1)
                        dve.wait_ge(den_out, m * (16 * NU) + 16 * u + 16)
                        nc.vector.tensor_copy(dn[:, :], pden[0:2, :]).then_inc(den_free, 1)
                        if g == KV - 1:
                            dve.wait_ge(x_hi, m * DC + c + DC + 1)
                            nc.vector.tensor_tensor(xl[:, c, :], xst[:, c % 2, :], f32(xh[:, c, :]),
                                                    ALU.subtract).then_inc(xt_ready, 1)

        @block.gpsimd
        def _(pool):
            def feature_lo(e, m):
                r = rope_index(e)
                g, i = e[1:]
                src = Kf if i == 0 else tb[r % NT]
                pool.wait_ge(hi_done, m * NR + r + 1)
                nc.gpsimd.tensor_tensor(Ql[g % 2][:, i, :], src[:, :], f32(Qh[g % 2][:, i, :]),
                                        ALU.subtract).then_inc(lo_done, 1)

            with pool.Fori(0, NM) as m:
                for e in EVENTS:
                    if e[0] == "J":
                        r = rope_index(e)
                        if r == 0:
                            pool.wait_ge(cs_in, m * 32 + 32)
                        pool.wait_ge(shifted, m * NR + r + 1)
                        nc.gpsimd.tensor_tensor(tb[r % NT][:, :], tb[r % NT][:, :], sinb[:, :],
                                                ALU.mult).then_inc(sin_done, 1)
                    if e[0] in "JF":
                        if feature_job_before(e, 2):
                            feature_lo(feature_job_before(e, 2), m)
                    elif e[0] == "SC":
                        u = e[1]
                        pool.wait_ge(sc_free, m * NU + u + 3)
                        nc.gpsimd.sem_inc(passed, 1)
                        for n, a in enumerate((Ah[u % 2], Al[u % 2])):
                            ins = nc.gpsimd.affine_select(out=a[:, :, :], in_=a[:, :, :], compare_op=ALU.is_ge, fill=0.0,
                                                          base=0, pattern=[[0, G], [1, CH]], channel_multiplier=-1)
                        ins.then_inc(a_ready, 1)

        @block.sync
        def _(sp):
            with sp.Fori(0, NM) as m:
                nxt = (m + 1) % NM
                for q in range(2):
                    sp.wait_ge(xt_ready, m * DC + DC)
                    sp.dma_start(xst[:, q, :], xT[nxt, :, q, :]).then_inc(xst_in[q], 16)
                for u in range(NU):
                    g, c = divmod(u, NCH)
                    sp.wait_ge(num_free, m * NU + u + 3)
                    sp.dma_start(num_d[m * NCH + c, :, g * G:(g + 1) * G, :], no[u % 2][:, :, :]).then_inc(num_out[u % 2], 16)
                    sp.wait_ge(den_free, m * NU + u + 2)
                    sp.dma_start(den_d[:, m * NCH + c, g * G:(g + 1) * G, :],
                                 dn[:, :].rearrange("p (h t) -> p h t", h=G)).then_inc(den_out, 16)
                    if u == 11:
                        sp.wait_ge(sin_done, m * NR + NR)
                        sp.wait_ge(bank_free, m * NJ + job_index(("J", KV - 1, G)) + 3)
                        sp.dma_start(cosb[:, :], cosT[:, bass.ts(nxt, MT)]).then_inc(cs_in, 16)
                        sp.dma_start(sinb[:, :], sinT[:, bass.ts(nxt, MT)]).then_inc(cs_in, 16)
                    if u in (12, 13):
                        sp.wait_ge(xt_ready, m * DC + DC + u - 11)
                        sp.dma_start(xst[:, u - 12, :], xT[nxt, :, u - 10, :]).then_inc(xst_in[u - 12], 16)
            sp.wait_ge(num_out[0], NM * NU * 8 + 16)
            sp.wait_ge(num_out[1], NM * NU * 8 + 16)
            sp.wait_ge(den_out, NM * NU * 16 + 16)
            for q in range(2):
                sp.wait_ge(xst_in[q], 32 * (NM + 1))
            sp.wait_ge(cs_in, 32 * (NM + 1))


def phase_b(nc, x, wo, su, consts, num_d, den_d, rden_d, x1_d, x2_d):
    ctx = ExitStack()
    NC = T // CH
    with ctx:
        def sb(name, shape, dt=F32, c=ctx):
            return c.enter_context(nc.sbuf_tensor(name, shape, dt))

        def sem(name):
            return ctx.enter_context(nc.semaphore(name))

        woh, wol = sb("woh", [P, H, D], F32R), sb("wol", [P, H, D], F32R)
        nt = [sb(f"nt{i}", [P, H, CH]) for i in range(2)]
        rb = [sb(f"rb{i}", [P, H, CH]) for i in range(2)]
        xr = [sb(f"xr{i}", [P, D]) for i in range(2)]
        suc = sb("suc", [P, DC])
        identb, had, hadr = sb("identb", [P, P]), sb("had", [P, P]), sb("hadr", [P, P], F32R)
        neghalf = sb("neghalf", [P, 1])
        py = [ctx.enter_context(nc.psum_tensor(f"py{i}", [P, D], F32)) for i in range(2)]
        pt = [ctx.enter_context(nc.psum_tensor(f"pt{i}", [P, DC, CH], F32)) for i in range(2)]
        ph = [ctx.enter_context(nc.psum_tensor(f"ph{i}", [P, MT], F32)) for i in range(2)]
        x_v = x.rearrange("(n p) d -> n p d", p=CH)
        x1_v = x1_d.rearrange("(n p) d -> n p d", p=CH)

        passed, passed_sp = sem("passed_b"), sem("passed_b_sp")
        load_in = [sem("load_in0"), sem("load_in1")]
        o_done, o_hi, o_lo = sem("o_done"), sem("o_hi"), sem("o_lo")
        y_done = sem("y_done")
        r_done = sem("r_done")
        ln_step, rstd_done, x1_ready = sem("ln_step"), sem("rstd_done"), sem("x1_ready")
        x1_out = [sem("x1_out0"), sem("x1_out1")]
        tr_done = sem("tr_done")
        tr_free = sem("tr_free")
        bf_step, xs_hi, xs_lo = sem("bf_step"), sem("xs_hi"), sem("xs_lo")
        had_done = sem("had_done")
        had_free = sem("had_free")
        tile_had = sem("tile_had")
        x2_out = sem("x2_out")

        def load_chunk(sp, n, s):
            sp.dma_start(nt[s][:, :, :], num_d[n]).then_inc(load_in[s], 16)
            sp.dma_start(rb[s][:].rearrange("p h t -> p (h t)"),
                         rden_d[n:n + 1, :].broadcast_to([P, H * CH])
                         if isinstance(n, int) else rden_d[bass.ds(n, 1), :].broadcast_to([P, H * CH]))\
                .then_inc(load_in[s], 16)
            sp.dma_start(xr[s][:, :], x_v[n]).then_inc(load_in[s], 16)

        pro = ExitStack()
        with pro:
            w_in = [sem(f"wo_in{i}") for i in range(4)]
            c_in, w_hi, w_lo, d_in, d_step, d_out, set_up = (sem("cb_in"), sem("wo_hi"), sem("wo_lo"), sem("d_in"),
                                                             sem("d_step"), sem("d_out"), sem("set_up"))
            stage = sb("stage_b", [P, 4, 4 * D], F32, pro)
            da, db = sb("da", [P, D], F32, pro), sb("db", [P, D], F32, pro)
            block = pro.enter_context(nc.Block())

            @block.sync
            def _(sp):
                den_v = den_d.rearrange("a n h t -> a (n h t)").rearrange("a (p q) -> a p q", p=P)
                sp.dma_start(da[:, :], den_v[0]).then_inc(d_in, 16)
                sp.dma_start(db[:, :], den_v[1]).then_inc(d_in, 16)
                sp.dma_start(suc[:, :], su).then_inc(c_in, 16)
                sp.dma_start(identb[:, :], consts[:, 0:P]).then_inc(c_in, 16)
                sp.dma_start(had[:, :], consts[:, P:2 * P]).then_inc(c_in, 16)
                for i in range(4):
                    sp.dma_start(stage[:, i, :], wo[:, 4 * i:4 * i + 4].rearrange("p h n -> p (h n)")).then_inc(w_in[i], 16)
                sp.wait_ge(d_step, 3)
                rden_v = rden_d.rearrange("n k -> (n k)").rearrange("(p q) -> p q", p=P)
                sp.dma_start(rden_v, da[:, :]).then_inc(d_out, 16)
                sp.wait_ge(d_out, 16)
                for n in range(2):
                    load_chunk(sp, n, n)

            @block.gpsimd
            def _(pool):
                nc.gpsimd.memset(neghalf[:], -0.5)
                for s, ahead in ((y_done, 2), (r_done, 2), (tr_free, 2), (had_free, 2), (tile_had, 1), (x1_out[0], 16),
                                 (x1_out[1], 16), (x2_out, 16)):
                    nc.gpsimd.sem_inc(s, ahead)

            @block.scalar
            def _(act):
                for i in range(4):
                    act.wait_ge(w_in[i], 16)
                    nc.scalar.activation(woh[:, 4 * i:4 * i + 4].rearrange("p h n -> p (h n)"), stage[:, i, :],
                                         ACT.Copy).then_inc(w_hi, 1)

            @block.vector
            def _(dve):
                dve.wait_ge(d_in, 32)
                nc.vector.tensor_tensor(da[:, :], da[:, :], db[:, :], ALU.add).then_inc(d_step, 1)
                dve.wait_ge(d_step, 1)
                nc.vector.tensor_scalar_add(da[:, :], da[:, :], 1e-6).then_inc(d_step, 1)
                dve.wait_ge(d_step, 2)
                nc.vector.reciprocal(da[:, :], da[:, :]).then_inc(d_step, 1)
                dve.wait_ge(c_in, 48)
                nc.vector.tensor_copy(hadr[:, :], had[:, :]).then_inc(set_up, 1)
                for i in range(4):
                    dve.wait_ge(w_hi, i + 1)
                    hd = slice(4 * i, 4 * i + 4)
                    nc.vector.tensor_tensor(wol[:, hd].rearrange("p h n -> p (h n)"), stage[:, i, :],
                                            f32(woh[:, hd].rearrange("p h n -> p (h n)")),
                                            ALU.subtract).then_inc(w_lo, 1)

        oh = [sb(f"oh{i}", [P, H, CH], F32R) for i in range(2)]
        ol = [sb(f"ol{i}", [P, H, CH], F32R) for i in range(2)]
        x1 = [sb(f"x1{i}", [P, D]) for i in range(2)]
        stats, mv, ve, rstd = sb("stats", [P, 6]), sb("mv", [P, 2]), sb("ve", [P, 1]), sb("rstd", [P, 1])
        xs, xb = sb("xs", [P, DC, MT]), sb("xb", [P, DC, MT])
        xsh, xsl = sb("xsh", [P, DC, MT], F32R), sb("xsl", [P, DC, MT], F32R)
        x2 = sb("x2", [P, DC, MT])

        block = ctx.enter_context(nc.Block())

        def before(m, j):
            return (j - 1) % NCH, m * NCH + j - 1

        @block.tensor
        def _(pe):
            def tail(jp, n):
                s = jp % 2
                pe.wait_ge(x1_ready, n + 1)
                pe.wait_ge(tr_free, n + 1)
                for c in range(DC):
                    last = nc.tensor.transpose(pt[s][:, c, :], x1[s][:, c * P:(c + 1) * P], identb[:, :])
                last.then_inc(tr_done, 1)

            def transform(m1):
                pe.wait_ge(xs_lo, m1)
                for c in range(DC):
                    pe.wait_ge(had_free, m1 * DC - DC + c + 1)
                    nc.tensor.matmul(ph[c % 2][:, :], hadr[:, :], xsh[:, c, :], start=True, stop=False)
                    last = nc.tensor.matmul(ph[c % 2][:, :], hadr[:, :], xsl[:, c, :], start=False, stop=True)
                    last.then_inc(had_done, 1)

            def step(m, j, first):
                n = m * NCH + j
                s = j % 2
                pe.wait_ge(o_lo, n + 1)
                pe.wait_ge(r_done, n + 1)
                k = 0
                for h in range(H):
                    for a, b in ((oh, woh), (oh, wol), (ol, woh)):
                        last = nc.tensor.matmul(py[s][:, :], a[s][:, h, :], b[:, h, :], start=(k == 0), stop=(k == 3 * H - 1))
                        k += 1
                last.then_inc(y_done, 1)
                if j == 1 and not first:
                    transform(m)
                if j or not first:
                    tail(*before(m, j))

            for j in range(NCH):
                step(0, j, True)
            with pe.Fori(1, NM) as m:
                for j in range(NCH):
                    step(m, j, False)
            tail(NCH - 1, NC - 1)
            transform(NM)

        @block.scalar
        def _(act):
            def tail(jp, n, guard):
                s = jp % 2
                act.wait_ge(tr_done, n + 1)
                if jp == 0 and guard is not None:
                    act.wait_ge(xs_lo, guard)
                for c in range(DC):
                    last = nc.scalar.activation(xs[:, c, jp * CH:(jp + 1) * CH], pt[s][:, c, :], ACT.Copy,
                                                scale=suc[:, c:c + 1])
                last.then_inc(tr_free, 1)

            def split(m1):
                act.wait_ge(bf_step, m1 * 4)
                act.wait_ge(tile_had, m1)
                nc.scalar.activation(xsh[:].rearrange("p c t -> p (c t)"), xs[:].rearrange("p c t -> p (c t)"),
                                     ACT.Copy).then_inc(xs_hi, 1)

            def write_x2(m1, mt):
                act.wait_ge(x2_out, m1 * 16)
                for c in range(DC):
                    act.wait_ge(had_done, m1 * DC - DC + c + 1)
                    last = nc.scalar.activation(x2[:, c, :], ph[c % 2][:, :], ACT.Copy, scale=float(D) ** -0.5)
                    last.then_inc(had_free, 1)
                nc.scalar.sem_inc(tile_had, 1)
                act.wait_ge(had_free, m1 * DC + 2)
                act.dma_start(x2_d[mt], x2[:, :, :]).then_inc(x2_out, 16)

            def step(m, j, first):
                n = m * NCH + j
                s = j % 2
                act.wait_ge(o_done, n + 1)
                act.wait_ge(y_done, n + 1)
                nc.scalar.activation(oh[s][:].rearrange("p h t -> p (h t)"), nt[s][:].rearrange("p h t -> p (h t)"),
                                     ACT.Copy).then_inc(o_hi, 1)
                if j == 1 and not first:
                    write_x2(m, m - 1)
                if j or not first:
                    tail(*before(m, j), None if first else m)
                if j == 0 and not first:
                    split(m)

            for j in range(NCH):
                step(0, j, True)
            with act.Fori(1, NM) as m:
                for j in range(NCH):
                    step(m, j, False)
            tail(NCH - 1, NC - 1, None)
            split(NM)
            write_x2(NM, NM - 1)
            act.wait_ge(x2_out, 16 * NM + 16)

        @block.vector
        def _(dve):
            def tail(jp, n, m_of_n):
                s = jp % 2
                dve.wait_ge(y_done, n + 3)
                dve.wait_ge(x1_out[s], m_of_n * 32 + (jp // 2) * 16 + 16)
                nc.vector.tensor_tensor(x1[s][:, :], py[s][:, :], xr[s][:, :], ALU.add).then_inc(r_done, 1)
                dve.wait_ge(r_done, n + 3)
                nc.vector.bn_stats(stats[:, :], x1[s][:, :]).then_inc(ln_step, 1)
                dve.wait_ge(ln_step, n * 3 + 1)
                nc.vector.sem_inc(passed, 1)
                nc.vector.bn_aggr(mv[:, :], stats[:, :]).then_inc(ln_step, 1)
                dve.wait_ge(ln_step, n * 3 + 2)
                nc.vector.tensor_scalar_add(ve[:, :], mv[:, 1:2], EPS).then_inc(ln_step, 1)
                dve.wait_ge(rstd_done, n + 1)
                nc.vector.tensor_scalar(x1[s][:, :], x1[s][:, :], mv[:, 0:1], rstd[:, 0:1], ALU.subtract,
                                        ALU.mult).then_inc(x1_ready, 1)

            def butterflies(m1):
                dve.wait_ge(tr_free, m1 * NCH + 2)
                base = m1 * 4 - 4
                for k, (src, dst, v) in enumerate(((xs, xb, "p (a b) t -> p b a t"), (xb, xs, "p (b a) t -> p b a t"))):
                    i, o = src[:].rearrange(v, b=2), dst[:].rearrange(v, b=2)
                    if k:
                        dve.wait_ge(bf_step, base + 2)
                    nc.vector.tensor_tensor(o[:, 0], i[:, 0], i[:, 1], ALU.add).then_inc(bf_step, 1)
                    nc.vector.tensor_tensor(o[:, 1], i[:, 0], i[:, 1], ALU.subtract).then_inc(bf_step, 1)
                dve.wait_ge(xs_hi, m1)
                nc.vector.tensor_tensor(xsl[:].rearrange("p c t -> p (c t)"), xs[:].rearrange("p c t -> p (c t)"),
                                        f32(xsh[:].rearrange("p c t -> p (c t)")), ALU.subtract).then_inc(xs_lo, 1)

            def step(m, j, first):
                n = m * NCH + j
                s = j % 2
                dve.wait_ge(load_in[s], m * 96 + (j // 2) * 48 + 48)
                nc.vector.tensor_tensor(nt[s][:].rearrange("p h t -> p (h t)"), nt[s][:].rearrange("p h t -> p (h t)"),
                                        rb[s][:].rearrange("p h t -> p (h t)"), ALU.mult).then_inc(o_done, 1)
                dve.wait_ge(o_hi, n + 1)
                nc.vector.tensor_tensor(ol[s][:].rearrange("p h t -> p (h t)"), nt[s][:].rearrange("p h t -> p (h t)"),
                                        f32(oh[s][:].rearrange("p h t -> p (h t)")), ALU.subtract).then_inc(o_lo, 1)
                if j:
                    tail(*before(m, j), m)
                elif not first:
                    tail(*before(m, j), m - 1)
                    butterflies(m)

            for j in range(NCH):
                step(0, j, True)
            with dve.Fori(1, NM) as m:
                for j in range(NCH):
                    step(m, j, False)
            tail(NCH - 1, NC - 1, NM - 1)
            butterflies(NM)

        @block.gpsimd
        def _(pool):
            with pool.Fori(0, NM) as m:
                for j in range(NCH):
                    n = m * NCH + j
                    pool.wait_ge(ln_step, n * 3 + 3)
                    nc.gpsimd.tensor_tensor(rstd[:, :], ve[:, :], neghalf[:, :], ALU.pow).then_inc(rstd_done, 1)

        @block.sync
        def _(sp):
            with sp.Fori(0, NM) as m:
                for j in range(NCH):
                    n = m * NCH + j
                    s = j % 2
                    sp.wait_ge(r_done, n + 3)
                    nc.sync.sem_inc(passed_sp, 1)
                    sp.wait_ge(o_lo, n + 1)
                    nc.sync.sem_inc(passed_sp, 1)
                    load_chunk(sp, (n + 2) % NC, s)
                    sp.wait_ge(x1_ready, n + 1)
                    sp.dma_start(x1_v[n], x1[s][:, :]).then_inc(x1_out[s], 16)
            for s in range(2):
                sp.wait_ge(x1_out[s], NM * 32 + 16)
                sp.wait_ge(load_in[s], NM * 96 + 48)


def phase_f(nc, wd, sd, wsd, consts, wd_d):
    ctx = ExitStack()
    with ctx:
        def sb(name, shape, dt=F32):
            return ctx.enter_context(nc.sbuf_tensor(name, shape, dt))

        def sem(name):
            return ctx.enter_context(nc.semaphore(name))

        wa, wb = sb("wa", [P, FB, D]), sb("wb", [P, FB, D])
        fh, fl = sb("fh", [P, FB, D], F32R), sb("fl", [P, FB, D], F32R)
        hadf, hadfr = sb("hadf", [P, P]), sb("hadfr", [P, P], F32R)
        sdc, scb = sb("sdc", [P, FB]), sb("scb", [P, D])
        pf = [ctx.enter_context(nc.psum_tensor(f"pf{i}", [P, D], F32)) for i in range(4)]
        f_in, f_had, f_bf, f_hi, f_lo, f_mm, f_out, f_sd, f_w = (
            sem("f_in"), sem("f_had"), sem("f_bf"), sem("f_hi"), sem("f_lo"), sem("f_mm"), sem("f_out"), sem("f_sd"), sem("f_w"))
        block = ctx.enter_context(nc.Block())

        @block.sync
        def _(sp):
            for q in range(2):
                hf = slice(q * FB // 2, (q + 1) * FB // 2)
                sp.dma_start(wa[:, hf, :], wd[:, hf, :]).then_inc(f_in, 16)
            sp.dma_start(hadf[:, :], consts[:, P:2 * P]).then_inc(f_in, 16)
            sp.dma_start(sdc[:, :], sd).then_inc(f_in, 16)
            sp.dma_start(scb[:, :], wsd.broadcast_to([P, D])).then_inc(f_in, 16)
            sp.wait_ge(f_w, FB)
            sp.dma_start(wd_d[:, :, :], wb[:, :, :]).then_inc(f_out, 16)
            sp.wait_ge(f_out, 16)

        @block.scalar
        def _(act):
            for q in range(4):
                act.wait_ge(f_bf, 8)
                b = slice(4 * q, 4 * q + 4)
                nc.scalar.activation(fh[:, b].rearrange("p c n -> p (c n)"), wa[:, b].rearrange("p c n -> p (c n)"),
                                     ACT.Copy).then_inc(f_hi, 1)

        @block.vector
        def _(dve):
            dve.wait_ge(f_in, 80)
            nc.vector.tensor_copy(hadfr[:, :], hadf[:, :]).then_inc(f_had, 1)
            nc.vector.tensor_scalar_mul(sdc[:, :], sdc[:, :], float(F) ** -0.5).then_inc(f_sd, 1)
            src, dst = wa, wb
            for k, h in enumerate((1, 2, 4, 8)):
                i = src[:].rearrange("p (a b c) n -> p b a (c n)", b=2, c=h)
                o = dst[:].rearrange("p (a b c) n -> p b a (c n)", b=2, c=h)
                if k:
                    dve.wait_ge(f_bf, 2 * k)
                nc.vector.tensor_tensor(o[:, 0], i[:, 0], i[:, 1], ALU.add).then_inc(f_bf, 1)
                nc.vector.tensor_tensor(o[:, 1], i[:, 0], i[:, 1], ALU.subtract).then_inc(f_bf, 1)
                src, dst = dst, src
            for q in range(4):
                dve.wait_ge(f_hi, q + 1)
                b = slice(4 * q, 4 * q + 4)
                nc.vector.tensor_tensor(fl[:, b].rearrange("p c n -> p (c n)"), wa[:, b].rearrange("p c n -> p (c n)"),
                                        f32(fh[:, b].rearrange("p c n -> p (c n)")), ALU.subtract).then_inc(f_lo, 1)
            dve.wait_ge(f_sd, 1)
            for b in range(FB):
                dve.wait_ge(f_mm, b + 1)
                nc.vector.scalar_tensor_tensor(out=wb[:, b, :], in0=pf[b % 4][:, :], scalar=sdc[:, b:b + 1],
                                               in1=scb[:, :], op0=ALU.mult, op1=ALU.mult).then_inc(f_w, 1)

        @block.tensor
        def _(pe):
            pe.wait_ge(f_had, 1)
            for b in range(FB):
                if b % 4 == 0:
                    pe.wait_ge(f_lo, b // 4 + 1)
                if b >= 4:
                    pe.wait_ge(f_w, b - 3)
                nc.tensor.matmul(pf[b % 4][:, :], hadfr[:, :], fh[:, b, :], start=True, stop=False)
                nc.tensor.matmul(pf[b % 4][:, :], hadfr[:, :], fl[:, b, :], start=False, stop=True).then_inc(f_mm, 1)


def phase_c(nc, wg, wu, wsg, wsu, wd_d, x1_d, x2_d, out):
    ctx = ExitStack()
    with ctx:
        def sb(name, shape, dt=F32, c=ctx):
            return c.enter_context(nc.sbuf_tensor(name, shape, dt))

        def sem(name):
            return ctx.enter_context(nc.semaphore(name))

        wgh, wgl = sb("wgh", [P, FB, DC, P], F32R), sb("wgl", [P, FB, DC, P], F32R)
        wuh, wul = sb("wuh", [P, FB, DC, P], F32R), sb("wul", [P, FB, DC, P], F32R)
        wdf = sb("wdf", [P, FB, D])
        x2st = sb("x2st", [P, 2, MT])
        x2h, x2l = sb("x2h", [P, DC, MT], F32R), sb("x2l", [P, DC, MT], F32R)
        sg, su2 = sb("sg", [P, FB]), sb("su2", [P, FB])
        neghalf = sb("neghalfc", [P, 1])
        pgu = [ctx.enter_context(nc.psum_tensor(f"pgu{i}", [P, MT], F32)) for i in range(4)]
        pyc = [ctx.enter_context(nc.psum_tensor(f"pyc{i}", [P, D], F32)) for i in range(NCH)]
        x1_v = x1_d.rearrange("(n p) d -> n p d", p=CH)
        out_v = out.rearrange("(n p) d -> n p d", p=CH)

        passed = sem("passed_c")
        x2_in = [sem("x2_in0"), sem("x2_in1")]
        x2_hi, x2_lo = sem("x2_hi"), sem("x2_lo")
        gu_done = sem("gu_done")
        gu_free = sem("gu_free")
        tanh_done, h_hi = sem("tanh_done"), sem("h_hi")
        h_lo = sem("h_lo")
        wd_hi, wd_lo = sem("wd_hi"), sem("wd_lo")
        d_done = sem("down_done")
        yb_done = sem("yb_done")
        y_free = sem("y_free")
        lnc_step, rc_done, o_ready = sem("lnc_step"), sem("rc_done"), sem("o_ready")
        x1_in = [sem(f"x1_in{i}") for i in range(NCH)]
        o_out = [sem(f"o_out{i}") for i in range(NCH)]

        pro = ExitStack()
        with pro:
            stage = sb("stage_c", [P, 3, 4 * DC * P], F32, pro)
            w_in = [sem(f"wc_in{i}") for i in range(3)]
            w_hi, w_lo, c_in, c_step = sem("wc_hi"), sem("wc_lo"), sem("cc_in"), sem("c_step")
            parts = []
            for q in range(4):
                b = slice(4 * q, 4 * q + 4)
                for src, hi, lo in ((wg, wgh, wgl), (wu, wuh, wul)):
                    parts.append([a[:, b].rearrange("p f c n -> p (f c n)") for a in (src, hi, lo)])
            block = pro.enter_context(nc.Block())

            @block.sync
            def _(sp):
                for q in range(2):
                    sp.dma_start(x2st[:, q, :], x2_d[0, :, q, :]).then_inc(x2_in[q], 16)
                sp.dma_start(sg[:, :], wsg).then_inc(c_in, 16)
                sp.dma_start(su2[:, :], wsu).then_inc(c_in, 16)
                for i, (src, _, _) in enumerate(parts):
                    if i >= 3:
                        sp.wait_ge(w_lo, i - 2)
                    sp.dma_start(stage[:, i % 3, :], src).then_inc(w_in[i % 3], 16)
                    if i < 2:
                        sp.wait_ge(x2_lo, i + 1)
                        sp.dma_start(x2st[:, i, :], x2_d[0, :, i + 2, :]).then_inc(x2_in[i], 16)
                sp.dma_start(wdf[:, :, :], wd_d[:, :, :]).then_inc(c_in, 16)
                sp.wait_ge(c_in, 48)

            @block.gpsimd
            def _(pool):
                nc.gpsimd.memset(neghalf[:], -0.5)
                for s, ahead in ((gu_free, 4), (h_lo, 2), (d_done, 2), (y_free, 4)):
                    nc.gpsimd.sem_inc(s, ahead)

            @block.scalar
            def _(act):
                for q in range(DC):
                    act.wait_ge(x2_in[q % 2], 16 * (q // 2 + 1))
                    nc.scalar.activation(x2h[:, q, :], x2st[:, q % 2, :], ACT.Copy).then_inc(x2_hi, 1)
                for i, (_, hi, _) in enumerate(parts):
                    act.wait_ge(w_in[i % 3], 16 * (i // 3 + 1))
                    nc.scalar.activation(hi, stage[:, i % 3, :], ACT.Copy).then_inc(w_hi, 1)

            @block.vector
            def _(dve):
                for q in range(DC):
                    dve.wait_ge(x2_hi, q + 1)
                    nc.vector.tensor_tensor(x2l[:, q, :], x2st[:, q % 2, :], f32(x2h[:, q, :]),
                                            ALU.subtract).then_inc(x2_lo, 1)
                for i, (_, hi, lo) in enumerate(parts):
                    dve.wait_ge(w_hi, i + 1)
                    nc.vector.tensor_tensor(lo, stage[:, i % 3, :], f32(hi), ALU.subtract).then_inc(w_lo, 1)
                dve.wait_ge(c_in, 48)
                nc.vector.tensor_scalar_mul(sg[:, :], sg[:, :], 0.5).then_inc(c_step, 1)
                dve.wait_ge(c_step, 1)
                nc.vector.tensor_tensor(su2[:, :], su2[:, :], sg[:, :], ALU.mult).then_inc(c_step, 1)

        wdh, wdl = [sb(f"wdh{i}", [P, D], F32R) for i in range(2)], [sb(f"wdl{i}", [P, D], F32R) for i in range(2)]
        th = [sb(f"th{i}", [P, MT]) for i in range(2)]
        hh, hl = [sb(f"hh{i}", [P, MT], F32R) for i in range(2)], [sb(f"hl{i}", [P, MT], F32R) for i in range(2)]
        x1r = [sb(f"x1r{i}", [P, D]) for i in range(NCH)]
        stats, mv, ve, rstd = sb("statsc", [P, 6]), sb("mvc", [P, 2]), sb("vec", [P, 1]), sb("rstdc", [P, 1])

        block = ctx.enter_context(nc.Block())

        @block.tensor
        def _(pe):
            def project(f, up, m):
                n = m * 2 * FB + 2 * f + up
                bank = pgu[2 * (f % 2) + up]
                wh, wl = (wuh, wul) if up else (wgh, wgl)
                pe.wait_ge(gu_free, n + 1)
                k = 0
                for c in range(DC):
                    if f == 0 and not up:
                        pe.wait_ge(x2_lo, m * DC + c + 1)
                    for w, x in ((wh, x2h), (wh, x2l), (wl, x2h)):
                        last = nc.tensor.matmul(bank[:, :], w[:, f, c, :], x[:, c, :], start=(k == 0), stop=(k == 11))
                        k += 1
                last.then_inc(gu_done, 1)

            def down(f, m):
                s = f % 2
                pe.wait_ge(h_lo, m * FB + f + 3)
                pe.wait_ge(wd_lo, m * FB + f + 1)
                for t in range(NCH):
                    if f == 0:
                        pe.wait_ge(y_free, m * NCH + t + 1)
                    tok = slice(t * CH, (t + 1) * CH)
                    for k, (a, b) in enumerate(((hh, wdh), (hh, wdl), (hl, wdh))):
                        last = nc.tensor.matmul(pyc[t][:, :], a[s][:, tok], b[s][:, :], start=(f == 0 and k == 0),
                                                stop=(f == FB - 1 and k == 2))
                    if f == FB - 1 and t < NCH - 1:
                        last.then_inc(yb_done, 1)
                if f == FB - 1:
                    last.then_inc(yb_done, 1)
                else:
                    last.then_inc(d_done, 1)

            def tile(m, first):
                project(0, 0, m)
                if not first:
                    down(FB - 1, m - 1)
                project(0, 1, m)
                for f in range(1, FB):
                    project(f, 0, m)
                    project(f, 1, m)
                    down(f - 1, m)

            tile(0, True)
            with pe.Fori(1, NM) as m:
                tile(m, False)
            down(FB - 1, NM - 1)

        def used_before(eng, m, f):
            if f >= 2:
                eng.wait_ge(d_done, m * (FB - 1) + f - 1 + 2)
            elif f == 0:
                eng.wait_ge(d_done, m * (FB - 1) + 2)
            else:
                eng.wait_ge(yb_done, m * NCH)

        @block.scalar
        def _(act):
            def tile(m, first):
                for f in range(FB):
                    s = f % 2
                    n = m * 2 * FB + 2 * f
                    act.wait_ge(gu_done, n + 1)
                    act.wait_ge(h_lo, m * FB + f + 1)
                    nc.scalar.activation(th[s][:, :], pgu[2 * s][:, :], ACT.Tanh, scale=sg[:, f:f + 1]).then_inc(tanh_done, 1)
                    if f != 1 or not first:
                        used_before(act, m, f)
                    nc.scalar.activation(wdh[s][:, :], wdf[:, f, :], ACT.Copy).then_inc(wd_hi, 1)
                    if f == FB - 1:
                        for c in range(DC):
                            act.wait_ge(x2_in[c % 2], m * 32 + 16 * (c // 2) + 48)
                            act.wait_ge(gu_done, m * 2 * FB + 2 * FB)
                            nc.scalar.activation(x2h[:, c, :], x2st[:, c % 2, :], ACT.Copy).then_inc(x2_hi, 1)
                    act.wait_ge(gu_free, n + 2 + 4)
                    nc.scalar.activation(hh[s][:, :], th[s][:, :], ACT.Copy).then_inc(h_hi, 1)

            tile(0, True)
            with act.Fori(1, NM) as m:
                tile(m, False)

        @block.vector
        def _(dve):
            def residual(m, t):
                n = m * NCH + t
                dve.wait_ge(yb_done, n + 1)
                dve.wait_ge(x1_in[t], m * 16 + 16)
                nc.vector.tensor_tensor(x1r[t][:, :], pyc[t][:, :], x1r[t][:, :], ALU.add).then_inc(y_free, 1)

            def norm(m, t):
                n = m * NCH + t
                dve.wait_ge(y_free, n + 1 + 4)
                nc.vector.bn_stats(stats[:, :], x1r[t][:, :]).then_inc(lnc_step, 1)
                dve.wait_ge(lnc_step, n * 3 + 1)
                nc.vector.sem_inc(passed, 1)
                nc.vector.bn_aggr(mv[:, :], stats[:, :]).then_inc(lnc_step, 1)
                dve.wait_ge(lnc_step, n * 3 + 2)
                nc.vector.tensor_scalar_add(ve[:, :], mv[:, 1:2], EPS).then_inc(lnc_step, 1)
                dve.wait_ge(rc_done, n + 1)
                nc.vector.tensor_scalar(x1r[t][:, :], x1r[t][:, :], mv[:, 0:1], rstd[:, 0:1], ALU.subtract,
                                        ALU.mult).then_inc(o_ready, 1)

            def tile(m, first):
                for f in range(FB):
                    s = f % 2
                    n = m * 2 * FB + 2 * f
                    dve.wait_ge(tanh_done, m * FB + f + 1)
                    nc.vector.scalar_tensor_tensor(out=th[s][:, :], in0=th[s][:, :], scalar=1.0, in1=pgu[2 * s][:, :],
                                                   op0=ALU.add, op1=ALU.mult).then_inc(gu_free, 1)
                    dve.wait_ge(wd_hi, m * FB + f + 1)
                    nc.vector.tensor_tensor(wdl[s][:, :], wdf[:, f, :], f32(wdh[s][:, :]), ALU.subtract).then_inc(wd_lo, 1)
                    if f == 0 and not first:
                        for t in range(NCH):
                            residual(m - 1, t)
                    dve.wait_ge(gu_done, n + 2)
                    dve.wait_ge(gu_free, n + 1 + 4)
                    nc.vector.scalar_tensor_tensor(out=th[s][:, :], in0=pgu[2 * s + 1][:, :], scalar=su2[:, f:f + 1],
                                                   in1=th[s][:, :], op0=ALU.mult, op1=ALU.mult).then_inc(gu_free, 1)
                    if f == FB - 1:
                        for c in range(DC):
                            dve.wait_ge(x2_hi, m * DC + c + DC + 1)
                            nc.vector.tensor_tensor(x2l[:, c, :], x2st[:, c % 2, :], f32(x2h[:, c, :]),
                                                    ALU.subtract).then_inc(x2_lo, 1)
                    dve.wait_ge(h_hi, m * FB + f + 1)
                    nc.vector.tensor_tensor(hl[s][:, :], th[s][:, :], f32(hh[s][:, :]), ALU.subtract).then_inc(h_lo, 1)
                    if f < NCH and not first:
                        norm(m - 1, f)

            tile(0, True)
            with dve.Fori(1, NM) as m:
                tile(m, False)
            for t in range(NCH):
                residual(NM - 1, t)
                norm(NM - 1, t)

        @block.gpsimd
        def _(pool):
            with pool.Fori(0, NM) as m:
                for t in range(NCH):
                    pool.wait_ge(lnc_step, m * (3 * NCH) + 3 * t + 3)
                    nc.gpsimd.tensor_tensor(rstd[:, :], ve[:, :], neghalf[:, :], ALU.pow).then_inc(rc_done, 1)

        @block.sync
        def _(sp):
            def write_out(m, t):
                sp.wait_ge(o_ready, m * NCH + t + 1)
                sp.dma_start(out_v[m * NCH + t], x1r[t][:, :]).then_inc(o_out[t], 16)

            def load_x2(m, q):
                sp.wait_ge(x2_lo, m * DC + DC + max(q - 1, 0))
                sp.dma_start(x2st[:, q % 2, :], x2_d[(m + 1) % NM, :, q, :]).then_inc(x2_in[q % 2], 16)

            def tile(m, first):
                for q in range(2):
                    load_x2(m, q)
                if not first:
                    for t in range(NCH):
                        write_out(m - 1, t)
                for t in range(NCH):
                    if not first:
                        sp.wait_ge(o_out[t], m * 16)
                    sp.dma_start(x1r[t][:, :], x1_v[m * NCH + t]).then_inc(x1_in[t], 16)
                for q in range(2, DC):
                    load_x2(m, q)

            tile(0, True)
            with sp.Fori(1, NM) as m:
                tile(m, False)
            for t in range(NCH):
                write_out(NM - 1, t)
            for t in range(NCH):
                sp.wait_ge(o_out[t], 16 * NM)
            for q in range(2):
                sp.wait_ge(x2_in[q], 32 * (NM + 1))


def kernel(L0_attn_x, L0_attn_Wq, L0_attn_Wk, L0_attn_Wv, L0_attn_Wo, L0_ffn_SU_ug, L0_ffn_SU_dp,
           L0_ffn_Wscale_ug, L0_ffn_Wscale_dp, L0_ffn_W_up, L0_ffn_W_gate, L0_ffn_W_down):
    import concourse.bacc as bacc
    from concourse.bass_utils import run_bass_kernel_spmd

    lay = np.ascontiguousarray
    x = np.asarray(L0_attn_x).reshape(T, D)

    def cols(v, n):
        return lay(np.asarray(v).reshape(n, P).T)

    inv_freq = (np.float32(1.0) / np.power(np.float32(10000.0), np.arange(0, HD, 2, dtype=np.float32) / np.float32(HD)))
    freqs = np.outer(np.arange(T, dtype=np.float32), inv_freq.astype(np.float32)).T
    cos, sin = np.cos(freqs), np.sin(freqs)
    had = np.ones((1, 1), np.float32)
    while had.shape[0] < P:
        had = np.block([[had, had], [had, -had]])
    arrays = {
        "xT": lay(x.reshape(NM, MT, DC, P).transpose(0, 3, 2, 1)),
        "x": lay(x),
        "wq": lay(np.asarray(L0_attn_Wq).reshape(H, HD, DC, P).transpose(3, 0, 2, 1)),
        "wk": lay(np.asarray(L0_attn_Wk).reshape(KV, HD, DC, P).transpose(3, 0, 2, 1)),
        "wv": lay(np.asarray(L0_attn_Wv).reshape(KV * HD, DC, P).transpose(2, 1, 0)),
        "wo": lay(np.asarray(L0_attn_Wo).reshape(D, H, HD).transpose(2, 1, 0)),
        "wg": lay(np.asarray(L0_ffn_W_gate).reshape(FB, P, DC, P).transpose(3, 0, 2, 1)),
        "wu": lay(np.asarray(L0_ffn_W_up).reshape(FB, P, DC, P).transpose(3, 0, 2, 1)),
        "wd": lay(np.asarray(L0_ffn_W_down).reshape(D, FB, P).transpose(2, 1, 0)),
        "su": cols(L0_ffn_SU_ug, DC),
        "sd": cols(L0_ffn_SU_dp, FB),
        "wsu": cols(np.asarray(L0_ffn_Wscale_ug)[:F], FB),
        "wsg": cols(np.asarray(L0_ffn_Wscale_ug)[F:], FB),
        "wsd": lay(np.asarray(L0_ffn_Wscale_dp).reshape(1, D)),
        "cosT": lay(np.concatenate([cos, cos]).astype(np.float32)),
        "sinT": lay(np.concatenate([-sin, sin]).astype(np.float32)),
        "consts": lay(np.concatenate([np.eye(P, dtype=np.float32), had], axis=1)),
    }
    nc = bacc.Bacc("TRN2", target_bir_lowering=False, num_devices=1, dynamic_dma_scratch_size=1024)
    a = {}
    feed = {}
    for name, v in arrays.items():
        feed[f"in_{name}"] = v
        a[name] = nc.dram_tensor(f"in_{name}", v.shape, F32, kind="ExternalInput").ap()
    out = nc.dram_tensor("out", [T, D], F32, kind="ExternalOutput").ap()

    def scratch(name, shape):
        return nc.dram_tensor(name, shape, F32).ap()

    num_d = scratch("num_scratch", [T // CH, P, H, CH])
    den_d = scratch("den_scratch", [2, T // CH, H, CH])
    rden_d = scratch("rden_scratch", [T // CH, H * CH])
    x1_d = scratch("x1_scratch", [T, D])
    x2_d = scratch("x2_scratch", [NM, P, DC, MT])
    wd_d = scratch("wd_scratch", [P, FB, D])
    phase_f(nc, a["wd"], a["sd"], a["wsd"], a["consts"], wd_d)
    phase_a(nc, a["xT"], a["wq"], a["wk"], a["wv"], a["cosT"], a["sinT"], a["consts"], num_d, den_d)
    phase_b(nc, a["x"], a["wo"], a["su"], a["consts"], num_d, den_d, rden_d, x1_d, x2_d)
    phase_c(nc, a["wg"], a["wu"], a["wsg"], a["wsu"], wd_d, x1_d, x2_d, out)
    r = run_bass_kernel_spmd(nc, [feed], core_ids=[0])
    return r.results[0]["out"].reshape(1, T, D)
```

```python
from contextlib import ExitStack

import numpy as np

import concourse.bass as bass
from concourse import mybir

F32 = mybir.dt.float32
F32R = mybir.dt.float32r
ALU = mybir.AluOpType
ACT = mybir.ActivationFunctionType
AX_X = mybir.AxisListType.X

P = 128
T = 4096
D = 512
DC = D // P
H, KV, HD = 16, 4, 128
G = H // KV
MT = 512
NM = T // MT
CH = 128
NCH = MT // CH
F = 2048
FB = F // P
EPS = 1e-5

def f32(ap):
    return ap.bitcast(F32)




def tile_events():
    ev = [("J", 0, 0), ("V", 0), ("J", 0, 1), ("V", 1), ("J", 0, 2), ("J", 0, 3), ("J", 0, 4), ("V", 2), ("F", 0, 0),
          ("V", 3), ("F", 0, 1), ("T", 0), ("SC", 0)]
    for u in range(KV * NCH):
        g, c = divmod(u, NCH)
        after = [("SC", u + 1)] if u + 1 < KV * NCH else []
        n = g + 1
        if n == KV:
            ev += after
        elif c == 0:
            ev += [("J", n, 0)] + after + [("J", n, 1), ("J", n, 2)]
        elif c == 1:
            ev += [("J", n, 3)] + after + [("J", n, 4)]
        elif c == 2:
            ev += [("F", n, 0)] + after + [("F", n, 1)]
        else:
            ev += [("T", n)] + after
        ev.append(("U", u))
    return ev


EVENTS = tile_events()
NU = KV * NCH
JOBS = [e for e in EVENTS if e[0] in "JVT"]
NJ = len(JOBS)
NT = 3
NR = KV * (G + 1)
assert NJ % 2 == 0 and [e[1] for e in EVENTS if e[0] == "J"] == sorted(e[1] for e in EVENTS if e[0] == "J")


SLOTS = [e for e in EVENTS if e[0] in "JF"]


def feature_job_before(e, k):
    n = SLOTS.index(e) - k
    return SLOTS[n] if n >= 0 and SLOTS[n][0] == "J" else None


def job_index(e):
    return JOBS.index(e)


def rope_index(e):
    return e[1] * (G + 1) + e[2]


def phase_a(nc, xT, wq, wk, wv, cosT, sinT, consts, num_d, den_d):
    ctx = ExitStack()
    with ctx:
        def sb(name, shape, dt=F32, c=ctx):
            return c.enter_context(nc.sbuf_tensor(name, shape, dt))

        def sem(name):
            return ctx.enter_context(nc.semaphore(name))

        wqh, wql = sb("wqh", [P, H, DC, HD], F32R), sb("wql", [P, H, DC, HD], F32R)
        wkh, wkl = sb("wkh", [P, KV, DC, HD], F32R), sb("wkl", [P, KV, DC, HD], F32R)
        wvh, wvl = sb("wvh", [P, DC, KV * HD], F32R), sb("wvl", [P, DC, KV * HD], F32R)
        xh, xl = sb("xh", [P, DC, MT], F32R), sb("xl", [P, DC, MT], F32R)
        xst = sb("xst", [P, 2, MT])
        cosb, sinb = sb("cosb", [P, MT]), sb("sinb", [P, MT])
        Sh, Sl = sb("Sh", [P, HD], F32R), sb("Sl", [P, HD], F32R)
        Zt = sb("Zt", [P, NCH, P], F32R)
        ident = sb("ident", [P, P])
        ones0 = sb("ones0", [P, P], F32R)
        zall = sb("zall", [P, KV, NCH + 1])
        zs = sb("zs", [P, NCH])
        ones4 = sb("ones4", [P, NCH])
        pj = [ctx.enter_context(nc.psum_tensor(f"pj{i}", [P, MT], F32)) for i in range(2)]
        psc = [ctx.enter_context(nc.psum_tensor(f"psc{i}", [P, G * CH], F32)) for i in range(2)]
        pnum = [ctx.enter_context(nc.psum_tensor(f"pnum{i}", [P, G * CH], F32)) for i in range(2)]
        pden = ctx.enter_context(nc.psum_tensor("pden", [P, G * CH], F32))
        pst = ctx.enter_context(nc.psum_tensor("pst", [P, KV * HD], F32))

        w_in = [sem(f"w_in{i}") for i in range(6)]
        c_in, w_hi, w_lo, zeroed = sem("c_in"), sem("w_hi"), sem("w_lo"), sem("zeroed")
        xst_in = [sem("xst_in0"), sem("xst_in1")]
        x_hi, xt_ready = sem("x_hi"), sem("xt_ready")
        s_hi, s_lo = sem("s_hi"), sem("s_lo")
        cs_in = sem("cs_in")
        passed = sem("passed_a")
        job_done, bank_free = sem("job_done"), sem("bank_free")
        shifted, sin_done, rot_done = sem("shifted"), sem("sin_done"), sem("rot_done")
        relu_done, f_done, hi_done = sem("relu_done"), sem("f_done"), sem("hi_done")
        lo_done = sem("lo_done")
        v_hi, t_hi = sem("v_hi"), sem("t_hi")
        z_sum, z_move, z_scan, z_hi, z_lo = (sem("z_sum"), sem("z_move"), sem("z_scan"), sem("z_hi"), sem("z_lo"))
        sc_done, a_hi, a_ready = sem("sc_done"), sem("a_hi"), sem("a_ready")
        sc_free = sem("sc_free")
        num_done, den_done = sem("num_done"), sem("den_done")
        num_free = sem("num_free")
        den_free = sem("den_free")
        unit_done = sem("unit_done")
        num_out = [sem("num_out0"), sem("num_out1")]
        den_out = sem("den_out")
        pro = ExitStack()
        with pro:
            stage = sb("stage", [P, 6, 2048], F32, pro)
            parts = [(wq[:, 4 * i:4 * i + 4].rearrange("p h c e -> p (h c e)"),
                      wqh[:, 4 * i:4 * i + 4].rearrange("p h c e -> p (h c e)"),
                      wql[:, 4 * i:4 * i + 4].rearrange("p h c e -> p (h c e)")) for i in range(4)]
            parts = [(wk.rearrange("p h c e -> p (h c e)"), wkh[:].rearrange("p h c e -> p (h c e)"),
                      wkl[:].rearrange("p h c e -> p (h c e)"))] + parts[:1] + \
                    [(wv.rearrange("p c n -> p (c n)"), wvh[:].rearrange("p c n -> p (c n)"),
                      wvl[:].rearrange("p c n -> p (c n)"))] + parts[1:]
            block = pro.enter_context(nc.Block())

            @block.sync
            def _(sp):
                sp.dma_start(ident[:, :], consts[:, 0:P]).then_inc(c_in, 16)
                for q in range(2):
                    sp.dma_start(xst[:, q, :], xT[0, :, q, :]).then_inc(xst_in[q], 16)
                for i, (src, _, _) in enumerate(parts):
                    sp.dma_start(stage[:, i, :], src).then_inc(w_in[i], 16)
                    if i < 2:
                        sp.wait_ge(xt_ready, i + 1)
                        sp.dma_start(xst[:, i, :], xT[0, :, i + 2, :]).then_inc(xst_in[i], 16)
                sp.dma_start(cosb[:, :], cosT[:, 0:MT]).then_inc(cs_in, 16)
                sp.dma_start(sinb[:, :], sinT[:, 0:MT]).then_inc(cs_in, 16)
                sp.wait_ge(cs_in, 32)
                sp.wait_ge(c_in, 16)

            @block.gpsimd
            def _(pool):
                nc.gpsimd.memset(zall[:], 0.0)
                nc.gpsimd.memset(ones4[:], 1.0)
                nc.gpsimd.memset(f32(Sh[:]), 0.0).then_inc(zeroed, 1)
                nc.gpsimd.memset(f32(Sl[:]), 0.0).then_inc(s_lo, 1)
                nc.gpsimd.memset(f32(Zt[:]), 0.0).then_inc(zeroed, 1)
                nc.gpsimd.memset(f32(ones0[:]), 0.0).then_inc(zeroed, 1)
                pool.wait_ge(zeroed, 3)
                nc.gpsimd.memset(f32(ones0[:, 0:1]), 1.0).then_inc(zeroed, 1)
                for s, ahead in ((bank_free, 2), (sc_free, 2), (num_free, 2), (den_free, 1), (unit_done, 2),
                                 (lo_done, NT), (num_out[0], 16), (num_out[1], 16), (den_out, 16)):
                    nc.gpsimd.sem_inc(s, ahead)

            @block.scalar
            def _(act):
                for q in range(DC):
                    act.wait_ge(xst_in[q % 2], 16 * (q // 2 + 1))
                    nc.scalar.activation(xh[:, q, :], xst[:, q % 2, :], ACT.Copy).then_inc(x_hi, 1)
                for i, (_, hi, _) in enumerate(parts):
                    act.wait_ge(w_in[i], 16)
                    nc.scalar.activation(hi, stage[:, i, :], ACT.Copy).then_inc(w_hi, 1)

            @block.vector
            def _(dve):
                for q in range(DC):
                    dve.wait_ge(x_hi, q + 1)
                    nc.vector.tensor_tensor(xl[:, q, :], xst[:, q % 2, :], f32(xh[:, q, :]),
                                            ALU.subtract).then_inc(xt_ready, 1)
                for i, (_, hi, lo) in enumerate(parts):
                    dve.wait_ge(w_hi, i + 1)
                    nc.vector.tensor_tensor(lo, stage[:, i, :], f32(hi), ALU.subtract).then_inc(w_lo, 1)

            @block.tensor
            def _(pe):
                pe.wait_ge(zeroed, 2)
                nc.tensor.matmul(pst[:, :], Sh[:, :], Zt[:].rearrange("p c n -> p (c n)"), start=True, stop=True,
                                 skip_group_check=True).then_inc(w_lo, 1)

        Vh, Vl = sb("Vh", [P, NCH, KV * HD], F32R), sb("Vl", [P, NCH, KV * HD], F32R)
        Qh = [sb(f"Qh{i}", [P, G + 1, MT], F32R) for i in range(2)]
        Ql = [sb(f"Ql{i}", [P, G + 1, MT], F32R) for i in range(2)]
        Kth, Ktl = sb("Kth", [P, NCH, HD], F32R), sb("Ktl", [P, NCH, HD], F32R)
        Kf = sb("Kf", [P, MT])
        ta = [sb(f"ta{i}", [P, MT]) for i in range(NT)]
        tb = [sb(f"tb{i}", [P, MT]) for i in range(NT)]
        Ah = [sb(f"Ah{i}", [P, G, CH], F32R) for i in range(2)]
        Al = [sb(f"Al{i}", [P, G, CH], F32R) for i in range(2)]
        no = [sb(f"no{i}", [P, G, CH]) for i in range(2)]
        dn = sb("dn", [2, G * CH])

        block = ctx.enter_context(nc.Block())

        @block.tensor
        def _(pe):
            with pe.Fori(0, NM) as m:
                for e in EVENTS:
                    if e[0] in "JVT":
                        n = job_index(e)
                        bank = pj[n % 2]
                        pe.wait_ge(bank_free, m * NJ + n + 1)
                    if e[0] == "J":
                        g, i = e[1:]
                        wh, wl = (wkh[:, g], wkl[:, g]) if i == 0 else (wqh[:, G * g + i - 1], wql[:, G * g + i - 1])
                        if (g, i) == (0, 0):
                            pe.wait_ge(xt_ready, m * DC + DC)
                        k = 0
                        for c in range(DC):
                            for w, x in ((wh, xh), (wh, xl), (wl, xh)):
                                last = nc.tensor.matmul(bank[:, :], w[:, c, :], x[:, c, :], start=(k == 0), stop=(k == 11))
                                k += 1
                        last.then_inc(job_done, 1)
                    elif e[0] == "V":
                        tok = slice(e[1] * CH, (e[1] + 1) * CH)
                        k = 0
                        for c in range(DC):
                            for x, w in ((xh, wvh), (xh, wvl), (xl, wvh)):
                                last = nc.tensor.matmul(bank[:, :], x[:, c, tok], w[:, c, :], start=(k == 0), stop=(k == 11))
                                k += 1
                        last.then_inc(job_done, 1)
                    elif e[0] == "T":
                        g = e[1]
                        pe.wait_ge(f_done, m * NR + g * (G + 1) + 1)
                        for c in range(NCH):
                            last = nc.tensor.transpose(bank[:, c * CH:(c + 1) * CH], Kf[:, c * CH:(c + 1) * CH], ident[:, :])
                        last.then_inc(job_done, 1)
                    elif e[0] == "F":
                        pass
                    elif e[0] == "SC":
                        g, c = divmod(e[1], NCH)
                        u = e[1]
                        tok = slice(c * CH, (c + 1) * CH)
                        qh, ql = Qh[g % 2], Ql[g % 2]
                        pe.wait_ge(lo_done, m * NR + (g + 1) * (G + 1) + NT)
                        pe.wait_ge(sc_free, m * NU + u + 1)
                        out = psc[u % 2][:, :].rearrange("p (h t) -> p h t", h=G)
                        for k, (a, b) in enumerate(((qh, qh), (qh, ql), (ql, qh))):
                            last = nc.tensor.matmul(out, a[:, 0, tok], b[:, 1:, tok], start=(k == 0), stop=(k == 2))
                        last.then_inc(sc_done, 1)
                    else:
                        g, c = divmod(e[1], NCH)
                        u = e[1]
                        tok = slice(c * CH, (c + 1) * CH)
                        hd = slice(g * HD, (g + 1) * HD)
                        qh, ql = Qh[g % 2], Ql[g % 2]
                        num = pnum[u % 2][:, :].rearrange("p (h t) -> p h t", h=G)
                        den = pden[:, :].rearrange("p (h t) -> p h t", h=G)
                        ah, al = Ah[u % 2], Al[u % 2]
                        pe.wait_ge(num_free, m * NU + u + 1)
                        if g == 0:
                            pe.wait_ge(bank_free, m * NJ + job_index(("V", c)) + 3)
                        pe.wait_ge(a_ready, m * NU + u + 1)
                        for k, (a, b) in enumerate(((Vh, ah), (Vh, al), (Vl, ah))):
                            nc.tensor.matmul(num, a[:, c, hd], b[:, :, :], start=(k == 0), stop=False)
                        pe.wait_ge(den_free, m * NU + u + 1)
                        nc.tensor.matmul(den, ones0[:, :], ah[:, :, :], start=True, stop=False)
                        nc.tensor.matmul(den, ones0[:, :], al[:, :, :], start=False, stop=False)
                        pe.wait_ge(s_lo, m * NU + u + 1)
                        for k, (a, b) in enumerate(((Sh, qh), (Sh, ql), (Sl, qh))):
                            last = nc.tensor.matmul(num, a[:, :], b[:, 1:, tok], start=False, stop=(k == 2))
                        last.then_inc(num_done, 1)
                        if c == 0:
                            pe.wait_ge(z_lo, m * KV + g + 1)
                        nc.tensor.matmul(den, Zt[:, c, :], qh[:, 1:, tok], start=False, stop=False)
                        nc.tensor.matmul(den, Zt[:, c, :], ql[:, 1:, tok], start=False, stop=True).then_inc(den_done, 1)
                        if c == 0:
                            pe.wait_ge(bank_free, m * NJ + job_index(("T", g)) + 3)
                        for k, (a, b) in enumerate(((Kth, Vh), (Kth, Vl), (Ktl, Vh))):
                            last = nc.tensor.matmul(pst[:, hd], a[:, c, :], b[:, c, hd], start=False, stop=(k == 2),
                                                    skip_group_check=True)
                        last.then_inc(unit_done, 1)

        @block.scalar
        def _(act):
            def exp_relu(e, m):
                r = rope_index(e)
                act.wait_ge(rot_done, m * NR + r + 1)
                nc.scalar.activation(tb[r % NT][:, :], ta[r % NT][:, :], ACT.Exp)
                nc.scalar.activation(ta[r % NT][:, :], ta[r % NT][:, :], ACT.Relu).then_inc(relu_done, 1)

            def feature_hi(e, m):
                r = rope_index(e)
                g, i = e[1:]
                src = Kf if i == 0 else tb[r % NT]
                act.wait_ge(f_done, m * NR + r + 1)
                nc.scalar.activation(Qh[g % 2][:, i, :], src[:, :], ACT.Copy).then_inc(hi_done, 1)

            with act.Fori(0, NM) as m:
                for e in EVENTS:
                    if e[0] == "J":
                        r = rope_index(e)
                        bank = pj[job_index(e) % 2]
                        act.wait_ge(job_done, m * NJ + job_index(e) + 1)
                        act.wait_ge(lo_done, m * NR + r + 1)
                        nc.scalar.activation(tb[r % NT][0:64, :], bank[64:128, :], ACT.Copy)
                        nc.scalar.activation(tb[r % NT][64:128, :], bank[0:64, :], ACT.Copy).then_inc(shifted, 1)
                    if e[0] in "JF":
                        if feature_job_before(e, 2):
                            feature_hi(feature_job_before(e, 2), m)
                        if feature_job_before(e, 1):
                            exp_relu(feature_job_before(e, 1), m)
                    elif e[0] == "V":
                        act.wait_ge(job_done, m * NJ + job_index(e) + 1)
                        nc.scalar.activation(Vh[:, e[1], :], pj[job_index(e) % 2][:, :], ACT.Copy).then_inc(v_hi, 1)
                    elif e[0] == "T":
                        g = e[1]
                        act.wait_ge(job_done, m * NJ + job_index(e) + 1)
                        if g == 0:
                            nc.scalar.activation(Kth[:].rearrange("p c e -> p (c e)"), pj[job_index(e) % 2][:, :],
                                                 ACT.Copy).then_inc(t_hi, 1)
                            act.wait_ge(z_scan, m * KV + 1)
                            nc.scalar.activation(Zt[:, :, 0], zall[:, 0, 0:NCH], ACT.Copy).then_inc(z_hi, 1)
                    elif e[0] == "SC":
                        u = e[1]
                        act.wait_ge(sc_done, m * NU + u + 1)
                        act.wait_ge(unit_done, m * NU + u + 1)
                        nc.scalar.activation(Ah[u % 2][:].rearrange("p h t -> p (h t)"), psc[u % 2][:, :],
                                             ACT.Copy).then_inc(a_hi, 1)
                    else:
                        u = e[1]
                        g, c = divmod(u, NCH)
                        gn = ((u + 1) % NU) // NCH
                        act.wait_ge(unit_done, m * NU + u + 3)
                        nc.scalar.activation(Sh[:, :], pst[:, gn * HD:(gn + 1) * HD], ACT.Copy).then_inc(s_hi, 1)
                        if c == 3 and g + 1 < KV:
                            nc.scalar.activation(Kth[:].rearrange("p c e -> p (c e)"),
                                                 pj[job_index(("T", g + 1)) % 2][:, :], ACT.Copy).then_inc(t_hi, 1)
                            act.wait_ge(z_scan, m * KV + g + 2)
                            nc.scalar.activation(Zt[:, :, 0], zall[:, g + 1, 0:NCH], ACT.Copy).then_inc(z_hi, 1)
                        if g == KV - 1:
                            act.wait_ge(xst_in[c % 2], m * 32 + 16 * (c // 2) + 48)
                            nc.scalar.activation(xh[:, c, :], xst[:, c % 2, :], ACT.Copy).then_inc(x_hi, 1)

        @block.vector
        def _(dve):
            def rotate(e, m):
                r = rope_index(e)
                dve.wait_ge(sin_done, m * NR + r + 1)
                dve.wait_ge(bank_free, m * NJ + job_index(e) + 3)
                nc.vector.tensor_tensor(ta[r % NT][:, :], ta[r % NT][:, :], tb[r % NT][:, :], ALU.add).then_inc(rot_done, 1)

            def elu(e, m):
                r = rope_index(e)
                i = e[2]
                dve.wait_ge(relu_done, m * NR + r + 1)
                dst = Kf if i == 0 else tb[r % NT]
                nc.vector.scalar_tensor_tensor(out=dst[:, :], in0=tb[r % NT][:, :], scalar=1.0, in1=ta[r % NT][:, :],
                                               op0=ALU.min, op1=ALU.add).then_inc(f_done, 1)

            def keys_lo(g, m):
                dve.wait_ge(t_hi, m * KV + g + 1)
                bank = pj[job_index(("T", g)) % 2]
                nc.vector.tensor_tensor(Ktl[:].rearrange("p c e -> p (c e)"), bank[:, :],
                                        f32(Kth[:].rearrange("p c e -> p (c e)")), ALU.subtract).then_inc(bank_free, 1)
                dve.wait_ge(z_hi, m * KV + g + 1)
                nc.vector.tensor_tensor(Zt[:, :, 1], zall[:, g, 0:NCH], f32(Zt[:, :, 0]), ALU.subtract).then_inc(z_lo, 1)

            with dve.Fori(0, NM) as m:
                for e in EVENTS:
                    if e[0] in "JF" and feature_job_before(e, 1):
                        rotate(feature_job_before(e, 1), m)
                    if e[0] == "J":
                        r = rope_index(e)
                        if r == 0:
                            dve.wait_ge(cs_in, m * 32 + 32)
                        dve.wait_ge(shifted, m * NR + r + 1)
                        nc.vector.tensor_tensor(ta[r % NT][:, :], pj[job_index(e) % 2][:, :], cosb[:, :],
                                                ALU.mult).then_inc(bank_free, 1)
                    if e[0] in "JF":
                        if feature_job_before(e, 1):
                            elu(feature_job_before(e, 1), m)
                    elif e[0] == "V":
                        dve.wait_ge(v_hi, m * NCH + e[1] + 1)
                        nc.vector.tensor_tensor(Vl[:, e[1], :], pj[job_index(e) % 2][:, :], f32(Vh[:, e[1], :]),
                                                ALU.subtract).then_inc(bank_free, 1)
                    elif e[0] == "T":
                        g = e[1]
                        dve.wait_ge(f_done, m * NR + g * (G + 1) + 1)
                        nc.vector.tensor_reduce(zs[:, :], Kf[:, :].rearrange("p (c t) -> p c t", c=NCH), AX_X,
                                                ALU.add).then_inc(z_sum, 1)
                        nc.vector.tensor_copy(zall[:, g, 0:1], zall[:, g, NCH:NCH + 1]).then_inc(z_move, 1)
                        dve.wait_ge(z_sum, m * KV + g + 1)
                        dve.wait_ge(z_move, m * KV + g + 1)
                        nc.vector.tensor_tensor_scan(zall[:, g, 1:NCH + 1], ones4[:, :], zs[:, :], zall[:, g, 0:1],
                                                     ALU.mult, ALU.add).then_inc(z_scan, 1)
                        if g == 0:
                            keys_lo(0, m)
                    elif e[0] == "SC":
                        u = e[1]
                        dve.wait_ge(a_hi, m * NU + u + 1)
                        nc.vector.tensor_tensor(Al[u % 2][:].rearrange("p h t -> p (h t)"), psc[u % 2][:, :],
                                                f32(Ah[u % 2][:].rearrange("p h t -> p (h t)")),
                                                ALU.subtract).then_inc(sc_free, 1)
                    else:
                        u = e[1]
                        g, c = divmod(u, NCH)
                        gn = ((u + 1) % NU) // NCH
                        dve.wait_ge(s_hi, m * NU + u + 1)
                        nc.vector.tensor_tensor(Sl[:, :], pst[:, gn * HD:(gn + 1) * HD], f32(Sh[:, :]),
                                                ALU.subtract).then_inc(s_lo, 1)
                        if c == 3 and g + 1 < KV:
                            keys_lo(g + 1, m)
                        dve.wait_ge(num_done, m * NU + u + 1)
                        dve.wait_ge(num_out[u % 2], m * (8 * NU) + 16 * (u // 2) + 16)
                        nc.vector.tensor_copy(no[u % 2][:].rearrange("p h t -> p (h t)"),
                                              pnum[u % 2][:, :]).then_inc(num_free, 1)
                        dve.wait_ge(den_done, m * NU + u + 1)
                        dve.wait_ge(den_out, m * (16 * NU) + 16 * u + 16)
                        nc.vector.tensor_copy(dn[:, :], pden[0:2, :]).then_inc(den_free, 1)
                        if g == KV - 1:
                            dve.wait_ge(x_hi, m * DC + c + DC + 1)
                            nc.vector.tensor_tensor(xl[:, c, :], xst[:, c % 2, :], f32(xh[:, c, :]),
                                                    ALU.subtract).then_inc(xt_ready, 1)

        @block.gpsimd
        def _(pool):
            def feature_lo(e, m):
                r = rope_index(e)
                g, i = e[1:]
                src = Kf if i == 0 else tb[r % NT]
                pool.wait_ge(hi_done, m * NR + r + 1)
                nc.gpsimd.tensor_tensor(Ql[g % 2][:, i, :], src[:, :], f32(Qh[g % 2][:, i, :]),
                                        ALU.subtract).then_inc(lo_done, 1)

            with pool.Fori(0, NM) as m:
                for e in EVENTS:
                    if e[0] == "J":
                        r = rope_index(e)
                        if r == 0:
                            pool.wait_ge(cs_in, m * 32 + 32)
                        pool.wait_ge(shifted, m * NR + r + 1)
                        nc.gpsimd.tensor_tensor(tb[r % NT][:, :], tb[r % NT][:, :], sinb[:, :],
                                                ALU.mult).then_inc(sin_done, 1)
                    if e[0] in "JF":
                        if feature_job_before(e, 2):
                            feature_lo(feature_job_before(e, 2), m)
                    elif e[0] == "SC":
                        u = e[1]
                        pool.wait_ge(sc_free, m * NU + u + 3)
                        nc.gpsimd.sem_inc(passed, 1)
                        for n, a in enumerate((Ah[u % 2], Al[u % 2])):
                            ins = nc.gpsimd.affine_select(out=a[:, :, :], in_=a[:, :, :], compare_op=ALU.is_ge, fill=0.0,
                                                          base=0, pattern=[[0, G], [1, CH]], channel_multiplier=-1)
                        ins.then_inc(a_ready, 1)

        @block.sync
        def _(sp):
            with sp.Fori(0, NM) as m:
                nxt = (m + 1) % NM
                for q in range(2):
                    sp.wait_ge(xt_ready, m * DC + DC)
                    sp.dma_start(xst[:, q, :], xT[nxt, :, q, :]).then_inc(xst_in[q], 16)
                for u in range(NU):
                    g, c = divmod(u, NCH)
                    sp.wait_ge(num_free, m * NU + u + 3)
                    sp.dma_start(num_d[m * NCH + c, :, g * G:(g + 1) * G, :], no[u % 2][:, :, :]).then_inc(num_out[u % 2], 16)
                    sp.wait_ge(den_free, m * NU + u + 2)
                    sp.dma_start(den_d[:, m * NCH + c, g * G:(g + 1) * G, :],
                                 dn[:, :].rearrange("p (h t) -> p h t", h=G)).then_inc(den_out, 16)
                    if u == 11:
                        sp.wait_ge(sin_done, m * NR + NR)
                        sp.wait_ge(bank_free, m * NJ + job_index(("J", KV - 1, G)) + 3)
                        sp.dma_start(cosb[:, :], cosT[:, bass.ts(nxt, MT)]).then_inc(cs_in, 16)
                        sp.dma_start(sinb[:, :], sinT[:, bass.ts(nxt, MT)]).then_inc(cs_in, 16)
                    if u in (12, 13):
                        sp.wait_ge(xt_ready, m * DC + DC + u - 11)
                        sp.dma_start(xst[:, u - 12, :], xT[nxt, :, u - 10, :]).then_inc(xst_in[u - 12], 16)
            sp.wait_ge(num_out[0], NM * NU * 8 + 16)
            sp.wait_ge(num_out[1], NM * NU * 8 + 16)
            sp.wait_ge(den_out, NM * NU * 16 + 16)
            for q in range(2):
                sp.wait_ge(xst_in[q], 32 * (NM + 1))
            sp.wait_ge(cs_in, 32 * (NM + 1))


def phase_b(nc, x, wo, su, consts, num_d, den_d, rden_d, x1_d, x2_d):
    ctx = ExitStack()
    NC = T // CH
    WP = 4
    with ctx:
        def sb(name, shape, dt=F32):
            return ctx.enter_context(nc.sbuf_tensor(name, shape, dt))

        def sem(name):
            return ctx.enter_context(nc.semaphore(name))

        woh, wol = sb("woh", [P, H, D], F32R), sb("wol", [P, H, D], F32R)
        stage = [sb(f"stage_b{i}", [P, H // WP, D]) for i in range(2)]
        da, db = sb("da", [P, T * H // P]), sb("db", [P, T * H // P])
        nt = [sb(f"nt{i}", [P, H, CH]) for i in range(2)]
        rrow = [sb(f"rrow{i}", [1, H * CH]) for i in range(2)]
        rb = [sb(f"rb{i}", [P, H * CH]) for i in range(2)]
        xr = [sb(f"xr{i}", [P, D]) for i in range(2)]
        oh = [sb(f"oh{i}", [P, H, CH], F32R) for i in range(2)]
        ol = [sb(f"ol{i}", [P, H, CH], F32R) for i in range(2)]
        x1 = [sb(f"x1{i}", [P, D]) for i in range(2)]
        stats, mv, ve, rstd = sb("stats", [P, 6]), sb("mv", [P, 2]), sb("ve", [P, 1]), sb("rstd", [P, 1])
        xs, xb, xc = sb("xs", [P, DC, MT]), sb("xb", [P, DC, MT]), sb("xc", [P, DC, MT])
        xsh, xsl = sb("xsh", [P, DC, MT], F32R), sb("xsl", [P, DC, MT], F32R)
        x2 = sb("x2", [P, DC, MT])
        suc = sb("suc", [P, DC])
        identb, had, hadr = sb("identb", [P, P]), sb("had", [P, P]), sb("hadr", [P, P], F32R)
        neghalf = sb("neghalf", [P, 1])
        py = [ctx.enter_context(nc.psum_tensor(f"py{i}", [P, D], F32)) for i in range(2)]
        pt = [ctx.enter_context(nc.psum_tensor(f"pt{i}", [P, DC, CH], F32)) for i in range(2)]
        ph = [ctx.enter_context(nc.psum_tensor(f"ph{i}", [P, MT], F32)) for i in range(DC)]
        x_v = x.rearrange("(n p) d -> n p d", p=CH)
        x1_v = x1_d.rearrange("(n p) d -> n p d", p=CH)

        passed, passed_sp = sem("passed_b"), sem("passed_b_sp")
        w_in = [sem("wo_in0"), sem("wo_in1")]
        id_in, had_in, su_in, had_ready = sem("id_in"), sem("had_in"), sem("su_in"), sem("had_ready")
        w_hi, w_lo = sem("wo_hi"), sem("wo_lo")
        d_in, d_step, d_out = sem("d_in"), sem("d_step"), sem("d_out")
        nt_in = [sem("nt_in0"), sem("nt_in1")]
        row_in = [sem("row_in0"), sem("row_in1")]
        xr_in = [sem("xr_in0"), sem("xr_in1")]
        rb_done = sem("rb_done")
        o_done, o_hi, o_lo = sem("o_done"), sem("o_hi"), sem("o_lo")
        y_done = sem("y_done")
        r_done = sem("r_done")
        ln_step, rstd_done, x1_ready = sem("ln_step"), sem("rstd_done"), sem("x1_ready")
        x1_out = [sem("x1_out0"), sem("x1_out1")]
        tr_done = sem("tr_done")
        tr_free = sem("tr_free")
        bf_step, xs_hi = sem("bf_step"), sem("xs_hi")
        xs_lo = sem("xs_lo")
        had_done = sem("had_done")
        had_free = sem("had_free")
        x2_out = sem("x2_out")

        def heads(a, i):
            return a[:, i * (H // WP):(i + 1) * (H // WP)].rearrange("p h n -> p (h n)")

        def load_numerators(sp, n, s):
            row = rden_d[n:n + 1, :] if isinstance(n, int) else rden_d[bass.ds(n, 1), :]
            sp.dma_start(rrow[s][:, :], row).then_inc(row_in[s], 16)
            sp.dma_start(nt[s][:, :, :], num_d[n]).then_inc(nt_in[s], 16)

        block = ctx.enter_context(nc.Block())

        def before(m, j, k):
            return (j - k) % NCH, m * NCH + j - k

        @block.tensor
        def _(pe):
            def transposes(jp, n):
                s = jp % 2
                pe.wait_ge(x1_ready, n + 1)
                pe.wait_ge(tr_free, n + 1)
                for c in range(DC):
                    last = nc.tensor.transpose(pt[s][:, c, :], x1[s][:, c * P:(c + 1) * P], identb[:, :])
                last.then_inc(tr_done, 1)

            def transform(m1):
                pe.wait_ge(xs_lo, m1 + 1)
                pe.wait_ge(had_free, m1 * DC)
                for c in range(DC):
                    nc.tensor.matmul(ph[c][:, :], hadr[:, :], xsh[:, c, :], start=True, stop=False)
                    last = nc.tensor.matmul(ph[c][:, :], hadr[:, :], xsl[:, c, :], start=False, stop=True)
                    last.then_inc(had_done, 1)

            def step(m, j, first):
                n = m * NCH + j
                s = j % 2
                pe.wait_ge(o_lo, n + 1)
                pe.wait_ge(r_done, n + 1)
                k = 0
                for h in range(H):
                    if first and j == 0 and h % (H // WP) == 0:
                        pe.wait_ge(w_lo, h // (H // WP) + 1)
                    for a, b in ((oh, woh), (oh, wol), (ol, woh)):
                        last = nc.tensor.matmul(py[s][:, :], a[s][:, h, :], b[:, h, :], start=(k == 0), stop=(k == 3 * H - 1))
                        k += 1
                    if h == H // 2:
                        if j or not first:
                            transposes(*before(m, j, 1))
                        if j == 2 and not first:
                            transform(m)
                last.then_inc(y_done, 1)

            pe.wait_ge(id_in, 16)
            pe.wait_ge(had_ready, 1)
            for j in range(NCH):
                step(0, j, True)
            with pe.Fori(1, NM) as m:
                for j in range(NCH):
                    step(m, j, False)
            transposes(NCH - 1, NC - 1)
            transform(NM)

        @block.scalar
        def _(act):
            def columns(jp, n, stage1):
                s = jp % 2
                act.wait_ge(tr_done, n + 1)
                if stage1 is not None:
                    act.wait_ge(bf_step, stage1)
                for c in range(DC):
                    last = nc.scalar.activation(xs[:, c, jp * CH:(jp + 1) * CH], pt[s][:, c, :], ACT.Copy,
                                                scale=suc[:, c:c + 1])
                last.then_inc(tr_free, 1)

            def split(m1):
                act.wait_ge(bf_step, m1 * 4)
                act.wait_ge(had_free, m1 * DC)
                nc.scalar.activation(xsh[:].rearrange("p c t -> p (c t)"), xc[:].rearrange("p c t -> p (c t)"),
                                     ACT.Copy).then_inc(xs_hi, 1)

            def write_x2(m1, mt):
                act.wait_ge(x2_out, m1 * 16)
                for c in range(DC):
                    act.wait_ge(had_done, m1 * DC - DC + c + 1)
                    last = nc.scalar.activation(x2[:, c, :], ph[c][:, :], ACT.Copy, scale=float(D) ** -0.5)
                    last.then_inc(had_free, 1)
                act.wait_ge(had_free, m1 * DC + DC)
                act.dma_start(x2_d[mt], x2[:, :, :]).then_inc(x2_out, 16)

            def weights_hi(i):
                act.wait_ge(w_in[i % 2], 16 * (i // 2) + 16)
                nc.scalar.activation(heads(woh, i), stage[i % 2][:].rearrange("p h n -> p (h n)"), ACT.Copy).then_inc(w_hi, 1)

            def step(m, j, first):
                n = m * NCH + j
                s = j % 2
                act.wait_ge(o_done, n + 1)
                act.wait_ge(y_done, n + 1)
                nc.scalar.activation(oh[s][:].rearrange("p h t -> p (h t)"), nt[s][:].rearrange("p h t -> p (h t)"),
                                     ACT.Copy).then_inc(o_hi, 1)
                if j == 2 and not first:
                    split(m)
                if j >= 2 or not first:
                    columns(*before(m, j, 2), m * 4 - 2 if j == 2 and not first else None)
                if j == 3 and not first:
                    write_x2(m, m - 1)

            for i in range(WP):
                weights_hi(i)
                if i == 1:
                    step(0, 0, True)
            act.wait_ge(su_in, 16)
            for j in range(1, NCH):
                step(0, j, True)
            with act.Fori(1, NM) as m:
                for j in range(NCH):
                    step(m, j, False)
            for k in (2, 1):
                columns(NCH - k, NC - k, None)
            split(NM)
            write_x2(NM, NM - 1)
            act.wait_ge(x2_out, 16 * NM + 16)

        @block.vector
        def _(dve):
            def norm(jp, n, m_of_n):
                s = jp % 2
                dve.wait_ge(y_done, n + 3)
                dve.wait_ge(x1_out[s], m_of_n * 32 + (jp // 2) * 16)
                dve.wait_ge(xr_in[s], m_of_n * 32 + (jp // 2) * 16 + 16)
                nc.vector.tensor_tensor(x1[s][:, :], py[s][:, :], xr[s][:, :], ALU.add).then_inc(r_done, 1)
                dve.wait_ge(r_done, n + 3)
                nc.vector.bn_stats(stats[:, :], x1[s][:, :]).then_inc(ln_step, 1)
                dve.wait_ge(ln_step, n * 3 + 1)
                nc.vector.sem_inc(passed, 1)
                nc.vector.bn_aggr(mv[:, :], stats[:, :]).then_inc(ln_step, 1)
                dve.wait_ge(ln_step, n * 3 + 2)
                nc.vector.tensor_scalar_add(ve[:, :], mv[:, 1:2], EPS).then_inc(ln_step, 1)
                dve.wait_ge(rstd_done, n + 1)
                nc.vector.tensor_scalar(x1[s][:, :], x1[s][:, :], mv[:, 0:1], rstd[:, 0:1], ALU.subtract,
                                        ALU.mult).then_inc(x1_ready, 1)

            def butterflies(m1):
                dve.wait_ge(tr_free, m1 * NCH + 2)
                base = m1 * 4 - 4
                for k, (src, dst, v) in enumerate(((xs, xb, "p (a b) t -> p b a t"), (xb, xc, "p (b a) t -> p b a t"))):
                    i, o = src[:].rearrange(v, b=2), dst[:].rearrange(v, b=2)
                    if k:
                        dve.wait_ge(bf_step, base + 2)
                        dve.wait_ge(xs_lo, m1)
                    nc.vector.tensor_tensor(o[:, 0], i[:, 0], i[:, 1], ALU.add).then_inc(bf_step, 1)
                    nc.vector.tensor_tensor(o[:, 1], i[:, 0], i[:, 1], ALU.subtract).then_inc(bf_step, 1)

            def weights_lo(i):
                dve.wait_ge(w_hi, i + 1)
                nc.vector.tensor_tensor(heads(wol, i), stage[i % 2][:].rearrange("p h n -> p (h n)"), f32(heads(woh, i)),
                                        ALU.subtract).then_inc(w_lo, 1)

            def divide(m, j):
                n = m * NCH + j
                s = j % 2
                dve.wait_ge(nt_in[s], m * 32 + (j // 2) * 16 + 16)
                dve.wait_ge(rb_done, n + 1)
                nc.vector.tensor_tensor(nt[s][:].rearrange("p h t -> p (h t)"), nt[s][:].rearrange("p h t -> p (h t)"),
                                        rb[s][:, :], ALU.mult).then_inc(o_done, 1)

            def lower_part(m, j):
                n = m * NCH + j
                s = j % 2
                dve.wait_ge(o_hi, n + 1)
                nc.vector.tensor_tensor(ol[s][:].rearrange("p h t -> p (h t)"), nt[s][:].rearrange("p h t -> p (h t)"),
                                        f32(oh[s][:].rearrange("p h t -> p (h t)")), ALU.subtract).then_inc(o_lo, 1)

            def step(m, j, first):
                divide(m, j)
                if j >= 2 or not first:
                    norm(*before(m, j, 2), m if j >= 2 else m - 1)
                lower_part(m, j)
                if j == 1 and not first:
                    butterflies(m)

            dve.wait_ge(d_in, 32)
            nc.vector.tensor_tensor(da[:, :], da[:, :], db[:, :], ALU.add).then_inc(d_step, 1)
            dve.wait_ge(d_step, 1)
            nc.vector.tensor_scalar_add(da[:, :], da[:, :], 1e-6).then_inc(d_step, 1)
            dve.wait_ge(d_step, 2)
            nc.vector.reciprocal(da[:, :], da[:, :]).then_inc(d_step, 1)
            dve.wait_ge(had_in, 16)
            nc.vector.tensor_copy(hadr[:, :], had[:, :]).then_inc(had_ready, 1)
            for i in range(WP):
                weights_lo(i)
                if i == 1:
                    step(0, 0, True)
            for j in range(1, NCH):
                step(0, j, True)
            with dve.Fori(1, NM) as m:
                for j in range(NCH):
                    step(m, j, False)
            for k in (2, 1):
                norm(NCH - k, NC - k, NM - 1)
            butterflies(NM)

        @block.gpsimd
        def _(pool):
            def inverse_root(n):
                pool.wait_ge(ln_step, n * 3 + 3)
                nc.gpsimd.tensor_tensor(rstd[:, :], ve[:, :], neghalf[:, :], ALU.pow).then_inc(rstd_done, 1)

            def columns_lo(m1):
                pool.wait_ge(xs_hi, m1)
                nc.gpsimd.tensor_tensor(xsl[:].rearrange("p c t -> p (c t)"), xc[:].rearrange("p c t -> p (c t)"),
                                        f32(xsh[:].rearrange("p c t -> p (c t)")), ALU.subtract).then_inc(xs_lo, 1)

            def step(m, j, first):
                n = m * NCH + j
                s = j % 2
                pool.wait_ge(row_in[s], m * 32 + (j // 2) * 16 + 16)
                if j >= 2 or not first:
                    pool.wait_ge(o_done, n - 1)
                nc.gpsimd.sem_inc(passed_sp, 1)
                nc.gpsimd.partition_broadcast(rb[s][:, :], rrow[s][:, :]).then_inc(rb_done, 1)
                if j >= 2 or not first:
                    inverse_root(before(m, j, 2)[1])
                if j == 2 and not first:
                    columns_lo(m)

            for s, ahead in ((y_done, 2), (r_done, 2), (tr_free, 2), (had_free, DC), (xs_lo, 1), (x2_out, 16)):
                nc.gpsimd.sem_inc(s, ahead)
            nc.gpsimd.memset(neghalf[:], -0.5).then_inc(passed_sp, 1)
            pool.wait_ge(passed_sp, 1)
            for j in range(NCH):
                step(0, j, True)
            with pool.Fori(1, NM) as m:
                for j in range(NCH):
                    step(m, j, False)
            for k in (2, 1):
                inverse_root(NC - k)
            columns_lo(NM)

        @block.sync
        def _(sp):
            def load_weights(i):
                sp.dma_start(stage[i % 2][:, :, :], wo[:, i * (H // WP):(i + 1) * (H // WP)]).then_inc(w_in[i % 2], 16)

            def write_x1(jp, n):
                sp.wait_ge(x1_ready, n + 1)
                sp.dma_start(x1_v[n], x1[jp % 2][:, :]).then_inc(x1_out[jp % 2], 16)

            def step(m, j, first):
                n = m * NCH + j
                s = j % 2
                sp.wait_ge(o_lo, n + 1)
                load_numerators(sp, (n + 2) % NC, s)
                if j >= 2 or not first:
                    sp.wait_ge(r_done, n + 1)
                sp.dma_start(xr[s][:, :], x_v[n]).then_inc(xr_in[s], 16)
                if j >= 2 or not first:
                    write_x1(*before(m, j, 2))

            den_v = den_d.rearrange("a n h t -> a (n h t)").rearrange("a (p q) -> a p q", p=P)
            sp.dma_start(da[:, :], den_v[0]).then_inc(d_in, 16)
            sp.dma_start(db[:, :], den_v[1]).then_inc(d_in, 16)
            load_weights(0)
            sp.wait_ge(d_step, 3)
            sp.dma_start(rden_d.rearrange("n k -> (n k)").rearrange("(p q) -> p q", p=P), da[:, :]).then_inc(d_out, 16)
            sp.dma_start(identb[:, :], consts[:, 0:P]).then_inc(id_in, 16)
            sp.dma_start(had[:, :], consts[:, P:2 * P]).then_inc(had_in, 16)
            sp.dma_start(suc[:, :], su).then_inc(su_in, 16)
            sp.wait_ge(d_out, 16)
            load_numerators(sp, 0, 0)
            load_weights(1)
            load_numerators(sp, 1, 1)
            for i in range(2, WP):
                sp.wait_ge(w_lo, i - 1)
                load_weights(i)
            for j in range(NCH):
                step(0, j, True)
            with sp.Fori(1, NM) as m:
                for j in range(NCH):
                    step(m, j, False)
            for k in (2, 1):
                write_x1(NCH - k, NC - k)
            for s in range(2):
                sp.wait_ge(x1_out[s], NM * 32)
                sp.wait_ge(nt_in[s], NM * 32 + 16)
                sp.wait_ge(row_in[s], NM * 32 + 16)


def phase_f(nc, wd, sd, wsd, consts, wd_d):
    ctx = ExitStack()
    with ctx:
        def sb(name, shape, dt=F32):
            return ctx.enter_context(nc.sbuf_tensor(name, shape, dt))

        def sem(name):
            return ctx.enter_context(nc.semaphore(name))

        wa, wb = sb("wa", [P, FB, D]), sb("wb", [P, FB, D])
        fh, fl = sb("fh", [P, FB, D], F32R), sb("fl", [P, FB, D], F32R)
        hadf, hadfr = sb("hadf", [P, P]), sb("hadfr", [P, P], F32R)
        sdc, scb = sb("sdc", [P, FB]), sb("scb", [P, D])
        pf = [ctx.enter_context(nc.psum_tensor(f"pf{i}", [P, D], F32)) for i in range(4)]
        f_in, f_had, f_bf, f_hi, f_lo, f_mm, f_out, f_sd, f_w = (
            sem("f_in"), sem("f_had"), sem("f_bf"), sem("f_hi"), sem("f_lo"), sem("f_mm"), sem("f_out"), sem("f_sd"), sem("f_w"))
        block = ctx.enter_context(nc.Block())

        @block.sync
        def _(sp):
            for q in range(2):
                hf = slice(q * FB // 2, (q + 1) * FB // 2)
                sp.dma_start(wa[:, hf, :], wd[:, hf, :]).then_inc(f_in, 16)
            sp.dma_start(hadf[:, :], consts[:, P:2 * P]).then_inc(f_in, 16)
            sp.dma_start(sdc[:, :], sd).then_inc(f_in, 16)
            sp.dma_start(scb[:, :], wsd.broadcast_to([P, D])).then_inc(f_in, 16)
            sp.wait_ge(f_w, FB)
            sp.dma_start(wd_d[:, :, :], wb[:, :, :]).then_inc(f_out, 16)
            sp.wait_ge(f_out, 16)

        @block.scalar
        def _(act):
            for q in range(4):
                act.wait_ge(f_bf, 8)
                b = slice(4 * q, 4 * q + 4)
                nc.scalar.activation(fh[:, b].rearrange("p c n -> p (c n)"), wa[:, b].rearrange("p c n -> p (c n)"),
                                     ACT.Copy).then_inc(f_hi, 1)

        @block.vector
        def _(dve):
            dve.wait_ge(f_in, 80)
            nc.vector.tensor_copy(hadfr[:, :], hadf[:, :]).then_inc(f_had, 1)
            nc.vector.tensor_scalar_mul(sdc[:, :], sdc[:, :], float(F) ** -0.5).then_inc(f_sd, 1)
            src, dst = wa, wb
            for k, h in enumerate((1, 2, 4, 8)):
                i = src[:].rearrange("p (a b c) n -> p b a (c n)", b=2, c=h)
                o = dst[:].rearrange("p (a b c) n -> p b a (c n)", b=2, c=h)
                if k:
                    dve.wait_ge(f_bf, 2 * k)
                nc.vector.tensor_tensor(o[:, 0], i[:, 0], i[:, 1], ALU.add).then_inc(f_bf, 1)
                nc.vector.tensor_tensor(o[:, 1], i[:, 0], i[:, 1], ALU.subtract).then_inc(f_bf, 1)
                src, dst = dst, src
            for q in range(4):
                dve.wait_ge(f_hi, q + 1)
                b = slice(4 * q, 4 * q + 4)
                nc.vector.tensor_tensor(fl[:, b].rearrange("p c n -> p (c n)"), wa[:, b].rearrange("p c n -> p (c n)"),
                                        f32(fh[:, b].rearrange("p c n -> p (c n)")), ALU.subtract).then_inc(f_lo, 1)
            dve.wait_ge(f_sd, 1)
            for b in range(FB):
                dve.wait_ge(f_mm, b + 1)
                nc.vector.scalar_tensor_tensor(out=wb[:, b, :], in0=pf[b % 4][:, :], scalar=sdc[:, b:b + 1],
                                               in1=scb[:, :], op0=ALU.mult, op1=ALU.mult).then_inc(f_w, 1)

        @block.tensor
        def _(pe):
            pe.wait_ge(f_had, 1)
            for b in range(FB):
                if b % 4 == 0:
                    pe.wait_ge(f_lo, b // 4 + 1)
                if b >= 4:
                    pe.wait_ge(f_w, b - 3)
                nc.tensor.matmul(pf[b % 4][:, :], hadfr[:, :], fh[:, b, :], start=True, stop=False)
                nc.tensor.matmul(pf[b % 4][:, :], hadfr[:, :], fl[:, b, :], start=False, stop=True).then_inc(f_mm, 1)


def phase_c(nc, wg, wu, wsg, wsu, wd_d, x1_d, x2_d, out):
    ctx = ExitStack()
    with ctx:
        def sb(name, shape, dt=F32, c=ctx):
            return c.enter_context(nc.sbuf_tensor(name, shape, dt))

        def sem(name):
            return ctx.enter_context(nc.semaphore(name))

        wgh, wgl = sb("wgh", [P, FB, DC, P], F32R), sb("wgl", [P, FB, DC, P], F32R)
        wuh, wul = sb("wuh", [P, FB, DC, P], F32R), sb("wul", [P, FB, DC, P], F32R)
        wdf = sb("wdf", [P, FB, D])
        x2st = sb("x2st", [P, 2, MT])
        x2h, x2l = sb("x2h", [P, DC, MT], F32R), sb("x2l", [P, DC, MT], F32R)
        sg, su2 = sb("sg", [P, FB]), sb("su2", [P, FB])
        neghalf = sb("neghalfc", [P, 1])
        pgu = [ctx.enter_context(nc.psum_tensor(f"pgu{i}", [P, MT], F32)) for i in range(4)]
        pyc = [ctx.enter_context(nc.psum_tensor(f"pyc{i}", [P, D], F32)) for i in range(NCH)]
        x1_v = x1_d.rearrange("(n p) d -> n p d", p=CH)
        out_v = out.rearrange("(n p) d -> n p d", p=CH)

        passed = sem("passed_c")
        x2_in = [sem("x2_in0"), sem("x2_in1")]
        x2_hi, x2_lo = sem("x2_hi"), sem("x2_lo")
        gu_done = sem("gu_done")
        gu_free = sem("gu_free")
        tanh_done, h_hi = sem("tanh_done"), sem("h_hi")
        h_lo = sem("h_lo")
        wd_hi, wd_lo = sem("wd_hi"), sem("wd_lo")
        d_done = sem("down_done")
        yb_done = sem("yb_done")
        y_free = sem("y_free")
        lnc_step, rc_done, o_ready = sem("lnc_step"), sem("rc_done"), sem("o_ready")
        x1_in = [sem(f"x1_in{i}") for i in range(NCH)]
        o_out = [sem(f"o_out{i}") for i in range(NCH)]

        pro = ExitStack()
        with pro:
            stage = sb("stage_c", [P, 3, 4 * DC * P], F32, pro)
            w_in = [sem(f"wc_in{i}") for i in range(3)]
            w_hi, w_lo, c_in, c_step = sem("wc_hi"), sem("wc_lo"), sem("cc_in"), sem("c_step")
            parts = []
            for q in range(4):
                b = slice(4 * q, 4 * q + 4)
                for src, hi, lo in ((wg, wgh, wgl), (wu, wuh, wul)):
                    parts.append([a[:, b].rearrange("p f c n -> p (f c n)") for a in (src, hi, lo)])
            block = pro.enter_context(nc.Block())

            @block.sync
            def _(sp):
                for q in range(2):
                    sp.dma_start(x2st[:, q, :], x2_d[0, :, q, :]).then_inc(x2_in[q], 16)
                sp.dma_start(sg[:, :], wsg).then_inc(c_in, 16)
                sp.dma_start(su2[:, :], wsu).then_inc(c_in, 16)
                for i, (src, _, _) in enumerate(parts):
                    if i >= 3:
                        sp.wait_ge(w_lo, i - 2)
                    sp.dma_start(stage[:, i % 3, :], src).then_inc(w_in[i % 3], 16)
                    if i < 2:
                        sp.wait_ge(x2_lo, i + 1)
                        sp.dma_start(x2st[:, i, :], x2_d[0, :, i + 2, :]).then_inc(x2_in[i], 16)
                sp.dma_start(wdf[:, :, :], wd_d[:, :, :]).then_inc(c_in, 16)
                sp.wait_ge(c_in, 48)

            @block.gpsimd
            def _(pool):
                nc.gpsimd.memset(neghalf[:], -0.5)
                for s, ahead in ((gu_free, 4), (h_lo, 2), (d_done, 2), (y_free, 4)):
                    nc.gpsimd.sem_inc(s, ahead)

            @block.scalar
            def _(act):
                for q in range(DC):
                    act.wait_ge(x2_in[q % 2], 16 * (q // 2 + 1))
                    nc.scalar.activation(x2h[:, q, :], x2st[:, q % 2, :], ACT.Copy).then_inc(x2_hi, 1)
                for i, (_, hi, _) in enumerate(parts):
                    act.wait_ge(w_in[i % 3], 16 * (i // 3 + 1))
                    nc.scalar.activation(hi, stage[:, i % 3, :], ACT.Copy).then_inc(w_hi, 1)

            @block.vector
            def _(dve):
                for q in range(DC):
                    dve.wait_ge(x2_hi, q + 1)
                    nc.vector.tensor_tensor(x2l[:, q, :], x2st[:, q % 2, :], f32(x2h[:, q, :]),
                                            ALU.subtract).then_inc(x2_lo, 1)
                for i, (_, hi, lo) in enumerate(parts):
                    dve.wait_ge(w_hi, i + 1)
                    nc.vector.tensor_tensor(lo, stage[:, i % 3, :], f32(hi), ALU.subtract).then_inc(w_lo, 1)
                dve.wait_ge(c_in, 48)
                nc.vector.tensor_scalar_mul(sg[:, :], sg[:, :], 0.5).then_inc(c_step, 1)
                dve.wait_ge(c_step, 1)
                nc.vector.tensor_tensor(su2[:, :], su2[:, :], sg[:, :], ALU.mult).then_inc(c_step, 1)

        wdh, wdl = [sb(f"wdh{i}", [P, D], F32R) for i in range(2)], [sb(f"wdl{i}", [P, D], F32R) for i in range(2)]
        th = [sb(f"th{i}", [P, MT]) for i in range(2)]
        hh, hl = [sb(f"hh{i}", [P, MT], F32R) for i in range(2)], [sb(f"hl{i}", [P, MT], F32R) for i in range(2)]
        x1r = [sb(f"x1r{i}", [P, D]) for i in range(NCH)]
        stats, mv, ve, rstd = sb("statsc", [P, 6]), sb("mvc", [P, 2]), sb("vec", [P, 1]), sb("rstdc", [P, 1])

        block = ctx.enter_context(nc.Block())

        @block.tensor
        def _(pe):
            def project(f, up, m):
                n = m * 2 * FB + 2 * f + up
                bank = pgu[2 * (f % 2) + up]
                wh, wl = (wuh, wul) if up else (wgh, wgl)
                pe.wait_ge(gu_free, n + 1)
                k = 0
                for c in range(DC):
                    if f == 0 and not up:
                        pe.wait_ge(x2_lo, m * DC + c + 1)
                    for w, x in ((wh, x2h), (wh, x2l), (wl, x2h)):
                        last = nc.tensor.matmul(bank[:, :], w[:, f, c, :], x[:, c, :], start=(k == 0), stop=(k == 11))
                        k += 1
                last.then_inc(gu_done, 1)

            def down(f, m):
                s = f % 2
                pe.wait_ge(h_lo, m * FB + f + 3)
                pe.wait_ge(wd_lo, m * FB + f + 1)
                for t in range(NCH):
                    if f == 0:
                        pe.wait_ge(y_free, m * NCH + t + 1)
                    tok = slice(t * CH, (t + 1) * CH)
                    for k, (a, b) in enumerate(((hh, wdh), (hh, wdl), (hl, wdh))):
                        last = nc.tensor.matmul(pyc[t][:, :], a[s][:, tok], b[s][:, :], start=(f == 0 and k == 0),
                                                stop=(f == FB - 1 and k == 2))
                    if f == FB - 1 and t < NCH - 1:
                        last.then_inc(yb_done, 1)
                if f == FB - 1:
                    last.then_inc(yb_done, 1)
                else:
                    last.then_inc(d_done, 1)

            def tile(m, first):
                project(0, 0, m)
                if not first:
                    down(FB - 1, m - 1)
                project(0, 1, m)
                for f in range(1, FB):
                    project(f, 0, m)
                    project(f, 1, m)
                    down(f - 1, m)

            tile(0, True)
            with pe.Fori(1, NM) as m:
                tile(m, False)
            down(FB - 1, NM - 1)

        def used_before(eng, m, f):
            if f >= 2:
                eng.wait_ge(d_done, m * (FB - 1) + f - 1 + 2)
            elif f == 0:
                eng.wait_ge(d_done, m * (FB - 1) + 2)
            else:
                eng.wait_ge(yb_done, m * NCH)

        @block.scalar
        def _(act):
            def tile(m, first):
                for f in range(FB):
                    s = f % 2
                    n = m * 2 * FB + 2 * f
                    act.wait_ge(gu_done, n + 1)
                    act.wait_ge(h_lo, m * FB + f + 1)
                    nc.scalar.activation(th[s][:, :], pgu[2 * s][:, :], ACT.Tanh, scale=sg[:, f:f + 1]).then_inc(tanh_done, 1)
                    if f != 1 or not first:
                        used_before(act, m, f)
                    nc.scalar.activation(wdh[s][:, :], wdf[:, f, :], ACT.Copy).then_inc(wd_hi, 1)
                    if f == FB - 1:
                        for c in range(DC):
                            act.wait_ge(x2_in[c % 2], m * 32 + 16 * (c // 2) + 48)
                            act.wait_ge(gu_done, m * 2 * FB + 2 * FB)
                            nc.scalar.activation(x2h[:, c, :], x2st[:, c % 2, :], ACT.Copy).then_inc(x2_hi, 1)
                    act.wait_ge(gu_free, n + 2 + 4)
                    nc.scalar.activation(hh[s][:, :], th[s][:, :], ACT.Copy).then_inc(h_hi, 1)

            tile(0, True)
            with act.Fori(1, NM) as m:
                tile(m, False)

        @block.vector
        def _(dve):
            def residual(m, t):
                n = m * NCH + t
                dve.wait_ge(yb_done, n + 1)
                dve.wait_ge(x1_in[t], m * 16 + 16)
                nc.vector.tensor_tensor(x1r[t][:, :], pyc[t][:, :], x1r[t][:, :], ALU.add).then_inc(y_free, 1)

            def norm(m, t):
                n = m * NCH + t
                dve.wait_ge(y_free, n + 1 + 4)
                nc.vector.bn_stats(stats[:, :], x1r[t][:, :]).then_inc(lnc_step, 1)
                dve.wait_ge(lnc_step, n * 3 + 1)
                nc.vector.sem_inc(passed, 1)
                nc.vector.bn_aggr(mv[:, :], stats[:, :]).then_inc(lnc_step, 1)
                dve.wait_ge(lnc_step, n * 3 + 2)
                nc.vector.tensor_scalar_add(ve[:, :], mv[:, 1:2], EPS).then_inc(lnc_step, 1)
                dve.wait_ge(rc_done, n + 1)
                nc.vector.tensor_scalar(x1r[t][:, :], x1r[t][:, :], mv[:, 0:1], rstd[:, 0:1], ALU.subtract,
                                        ALU.mult).then_inc(o_ready, 1)

            def tile(m, first):
                for f in range(FB):
                    s = f % 2
                    n = m * 2 * FB + 2 * f
                    dve.wait_ge(tanh_done, m * FB + f + 1)
                    nc.vector.scalar_tensor_tensor(out=th[s][:, :], in0=th[s][:, :], scalar=1.0, in1=pgu[2 * s][:, :],
                                                   op0=ALU.add, op1=ALU.mult).then_inc(gu_free, 1)
                    dve.wait_ge(wd_hi, m * FB + f + 1)
                    nc.vector.tensor_tensor(wdl[s][:, :], wdf[:, f, :], f32(wdh[s][:, :]), ALU.subtract).then_inc(wd_lo, 1)
                    if f == 0 and not first:
                        for t in range(NCH):
                            residual(m - 1, t)
                    dve.wait_ge(gu_done, n + 2)
                    dve.wait_ge(gu_free, n + 1 + 4)
                    nc.vector.scalar_tensor_tensor(out=th[s][:, :], in0=pgu[2 * s + 1][:, :], scalar=su2[:, f:f + 1],
                                                   in1=th[s][:, :], op0=ALU.mult, op1=ALU.mult).then_inc(gu_free, 1)
                    if f == FB - 1:
                        for c in range(DC):
                            dve.wait_ge(x2_hi, m * DC + c + DC + 1)
                            nc.vector.tensor_tensor(x2l[:, c, :], x2st[:, c % 2, :], f32(x2h[:, c, :]),
                                                    ALU.subtract).then_inc(x2_lo, 1)
                    dve.wait_ge(h_hi, m * FB + f + 1)
                    nc.vector.tensor_tensor(hl[s][:, :], th[s][:, :], f32(hh[s][:, :]), ALU.subtract).then_inc(h_lo, 1)
                    if f < NCH and not first:
                        norm(m - 1, f)

            tile(0, True)
            with dve.Fori(1, NM) as m:
                tile(m, False)
            for t in range(NCH):
                residual(NM - 1, t)
                norm(NM - 1, t)

        @block.gpsimd
        def _(pool):
            with pool.Fori(0, NM) as m:
                for t in range(NCH):
                    pool.wait_ge(lnc_step, m * (3 * NCH) + 3 * t + 3)
                    nc.gpsimd.tensor_tensor(rstd[:, :], ve[:, :], neghalf[:, :], ALU.pow).then_inc(rc_done, 1)

        @block.sync
        def _(sp):
            def write_out(m, t):
                sp.wait_ge(o_ready, m * NCH + t + 1)
                sp.dma_start(out_v[m * NCH + t], x1r[t][:, :]).then_inc(o_out[t], 16)

            def load_x2(m, q):
                sp.wait_ge(x2_lo, m * DC + DC + max(q - 1, 0))
                sp.dma_start(x2st[:, q % 2, :], x2_d[(m + 1) % NM, :, q, :]).then_inc(x2_in[q % 2], 16)

            def tile(m, first):
                for q in range(2):
                    load_x2(m, q)
                if not first:
                    for t in range(NCH):
                        write_out(m - 1, t)
                for t in range(NCH):
                    if not first:
                        sp.wait_ge(o_out[t], m * 16)
                    sp.dma_start(x1r[t][:, :], x1_v[m * NCH + t]).then_inc(x1_in[t], 16)
                for q in range(2, DC):
                    load_x2(m, q)

            tile(0, True)
            with sp.Fori(1, NM) as m:
                tile(m, False)
            for t in range(NCH):
                write_out(NM - 1, t)
            for t in range(NCH):
                sp.wait_ge(o_out[t], 16 * NM)
            for q in range(2):
                sp.wait_ge(x2_in[q], 32 * (NM + 1))


def kernel(L0_attn_x, L0_attn_Wq, L0_attn_Wk, L0_attn_Wv, L0_attn_Wo, L0_ffn_SU_ug, L0_ffn_SU_dp,
           L0_ffn_Wscale_ug, L0_ffn_Wscale_dp, L0_ffn_W_up, L0_ffn_W_gate, L0_ffn_W_down):
    import concourse.bacc as bacc
    from concourse.bass_utils import run_bass_kernel_spmd

    lay = np.ascontiguousarray
    x = np.asarray(L0_attn_x).reshape(T, D)

    def cols(v, n):
        return lay(np.asarray(v).reshape(n, P).T)

    inv_freq = (np.float32(1.0) / np.power(np.float32(10000.0), np.arange(0, HD, 2, dtype=np.float32) / np.float32(HD)))
    freqs = np.outer(np.arange(T, dtype=np.float32), inv_freq.astype(np.float32)).T
    cos, sin = np.cos(freqs), np.sin(freqs)
    had = np.ones((1, 1), np.float32)
    while had.shape[0] < P:
        had = np.block([[had, had], [had, -had]])
    arrays = {
        "xT": lay(x.reshape(NM, MT, DC, P).transpose(0, 3, 2, 1)),
        "x": lay(x),
        "wq": lay(np.asarray(L0_attn_Wq).reshape(H, HD, DC, P).transpose(3, 0, 2, 1)),
        "wk": lay(np.asarray(L0_attn_Wk).reshape(KV, HD, DC, P).transpose(3, 0, 2, 1)),
        "wv": lay(np.asarray(L0_attn_Wv).reshape(KV * HD, DC, P).transpose(2, 1, 0)),
        "wo": lay(np.asarray(L0_attn_Wo).reshape(D, H, HD).transpose(2, 1, 0)),
        "wg": lay(np.asarray(L0_ffn_W_gate).reshape(FB, P, DC, P).transpose(3, 0, 2, 1)),
        "wu": lay(np.asarray(L0_ffn_W_up).reshape(FB, P, DC, P).transpose(3, 0, 2, 1)),
        "wd": lay(np.asarray(L0_ffn_W_down).reshape(D, FB, P).transpose(2, 1, 0)),
        "su": cols(L0_ffn_SU_ug, DC),
        "sd": cols(L0_ffn_SU_dp, FB),
        "wsu": cols(np.asarray(L0_ffn_Wscale_ug)[:F], FB),
        "wsg": cols(np.asarray(L0_ffn_Wscale_ug)[F:], FB),
        "wsd": lay(np.asarray(L0_ffn_Wscale_dp).reshape(1, D)),
        "cosT": lay(np.concatenate([cos, cos]).astype(np.float32)),
        "sinT": lay(np.concatenate([-sin, sin]).astype(np.float32)),
        "consts": lay(np.concatenate([np.eye(P, dtype=np.float32), had], axis=1)),
    }
    nc = bacc.Bacc("TRN2", target_bir_lowering=False, num_devices=1, dynamic_dma_scratch_size=1024)
    a = {}
    feed = {}
    for name, v in arrays.items():
        feed[f"in_{name}"] = v
        a[name] = nc.dram_tensor(f"in_{name}", v.shape, F32, kind="ExternalInput").ap()
    out = nc.dram_tensor("out", [T, D], F32, kind="ExternalOutput").ap()

    def scratch(name, shape):
        return nc.dram_tensor(name, shape, F32).ap()

    num_d = scratch("num_scratch", [T // CH, P, H, CH])
    den_d = scratch("den_scratch", [2, T // CH, H, CH])
    rden_d = scratch("rden_scratch", [T // CH, H * CH])
    x1_d = scratch("x1_scratch", [T, D])
    x2_d = scratch("x2_scratch", [NM, P, DC, MT])
    wd_d = scratch("wd_scratch", [P, FB, D])
    phase_f(nc, a["wd"], a["sd"], a["wsd"], a["consts"], wd_d)
    phase_a(nc, a["xT"], a["wq"], a["wk"], a["wv"], a["cosT"], a["sinT"], a["consts"], num_d, den_d)
    phase_b(nc, a["x"], a["wo"], a["su"], a["consts"], num_d, den_d, rden_d, x1_d, x2_d)
    phase_c(nc, a["wg"], a["wu"], a["wsg"], a["wsu"], wd_d, x1_d, x2_d, out)
    r = run_bass_kernel_spmd(nc, [feed], core_ids=[0])
    return r.results[0]["out"].reshape(1, T, D)
```

```python
from contextlib import ExitStack

import numpy as np

import concourse.bass as bass
from concourse import mybir

F32 = mybir.dt.float32
F32R = mybir.dt.float32r
ALU = mybir.AluOpType
ACT = mybir.ActivationFunctionType
AX_X = mybir.AxisListType.X

P = 128
T = 4096
D = 512
DC = D // P
H, KV, HD = 16, 4, 128
G = H // KV
MT = 512
NM = T // MT
CH = 128
NCH = MT // CH
F = 2048
FB = F // P
EPS = 1e-5


def f32(ap):
    return ap.bitcast(F32)




ORDER_PE = """
C00 J11 C01 J12 U00 C02 C03 D04 J13 U01 J14 D11 U02 J20 D12 J21 U03 D13 T1 C10 J22 C11 C12 J23 U10 D14
J24 U11 C13 D21 J30 U12 D22 J31 U13 T2 D23 C20 C21 J32 C22 U20 D24 J33 J34 U21 C23 D31 U22 T3 D32 U23
J00' D33 C30 C31 J01' D34 C32 C33 J02' U30 J03' U31 V0' U32 D01' J04' V1' J10' V2' D02' U33 T0' V3' D03'
"""

ORDER_REST = """
A00 E10 S11 L10 A01 R11 E11 O00 S12 Y0 L11 A02 N00 P11 R12 N01 A03 E12 S13 S14 P12 L12 R13 R14 O01 E13
L13 N02 P13 E14 L14 S20 S21 N03 P14 R20 O02 O03 A10 K1 S22 A11 R21 R22 E20 E21 L20 O10 E22 L21 P21 N10 Y1
S23 A12 S24 N11 O11 L22 P22 A13 R23 R24 E23 E24 O12 S30 L23 P23 L24 N12 R30 S31 O13 N13 P24 K2 A20 R31
L30 E30 E31 S32 A21 P31 R32 O20 L31 E32 Y2 S33 N20 A22 X0' X1' X2' S34 N21 A23 P32 L32 R33 R34 O21 E33
N22 L33 O22 X3' P33 E34 L34 K3 P34 S00' N23 A30 A31 S01' R00' O23 R01' E00' O30 N30 A32 S02' L00' L01'
E01' P01' R02' Y3 O31 N31 S03' A33 W0' R03' E02' E03' S04' P02' W1' L02' L03' R04' O32 S10' N32 W2' E04'
P03' K0' L04' O33 R10' N33 W3' P04'
"""


def events_in(order):
    return [(w[0], int(w[1]), int((w[2:].rstrip("'")) or 0), int(w[-1] == "'")) for w in order.split()]


EVENTS = events_in(ORDER_PE) + events_in(ORDER_REST)
NU = KV * NCH
JOBS = [e for e in EVENTS if e[0] in "JVT"]
BANK_READS = {"S": "J", "W": "V", "K": "T"}
NJ = len(JOBS)
NJ0 = len([e for e in JOBS if e[3]])
NT = 3
XS = 3
NR = KV * (G + 1)
assert NJ % 2 == 0 and all(e[3] for e in JOBS[NJ - NJ0:])
assert [(BANK_READS[e[0]],) + e[1:] for e in EVENTS if e[0] in BANK_READS] == JOBS


def job_place(kind, a, b=0):
    for d in (0, 1):
        if (kind, a, b, d) in JOBS:
            return JOBS.index((kind, a, b, d)), d


def job_number(kind, a, b, m, d):
    k, early = job_place(kind, a, b)
    return m * NJ + ((d - early) * NJ + NJ0 + k)


def job_bank(kind, a, b=0):
    return (NJ0 + job_place(kind, a, b)[0]) % 2


def rope_number(e, m):
    return m * NR + (e[3] * NR + e[1] * (G + 1) + e[2])


def slot_free(e, m):
    r = e[1] * (G + 1) + e[2]
    back = NT if r >= NR % NT else NR % NT
    tile, last = divmod(r - back, NR)
    g, i = divmod(last, G + 1)
    return rope_number(e, m) + (1 + NT - back), m * H + ((e[3] + tile) * H + g * G + i + NT)


def product_number(e, m):
    return m * H + (e[3] * H + e[1] * G + e[2] - 1)


def phase_a(nc, xT, wq, wk, wv, cosT, sinT, consts, wd, sd, wsd, num_d, den_d, wd_d):
    ctx = ExitStack()
    with ctx:
        def sb(name, shape, dt=F32, c=ctx):
            return c.enter_context(nc.sbuf_tensor(name, shape, dt))

        def sem(name):
            return ctx.enter_context(nc.semaphore(name))

        wqh, wql = sb("wqh", [P, H, DC, HD], F32R), sb("wql", [P, H, DC, HD], F32R)
        wkh, wkl = sb("wkh", [P, KV, DC, HD], F32R), sb("wkl", [P, KV, DC, HD], F32R)
        wvh, wvl = sb("wvh", [P, DC, KV * HD], F32R), sb("wvl", [P, DC, KV * HD], F32R)
        xh, xl = sb("xh", [P, DC, MT], F32R), sb("xl", [P, DC, MT], F32R)
        xst = sb("xst", [P, XS, MT])
        cosb, sinb = sb("cosb", [P, MT]), sb("sinb", [P, MT])
        Sh, Sl = sb("Sh", [P, HD], F32R), sb("Sl", [P, HD], F32R)
        ident = sb("ident", [P, P])
        onesd = sb("onesd", [P, G, G], F32R)
        carry = sb("carry", [P, KV])
        pj = [ctx.enter_context(nc.psum_tensor(f"pj{i}", [P, MT], F32)) for i in range(2)]
        psc = [ctx.enter_context(nc.psum_tensor(f"psc{i}", [P, G * CH], F32)) for i in range(2)]
        pnum = [ctx.enter_context(nc.psum_tensor(f"pnum{i}", [P, G * CH], F32)) for i in range(2)]
        pden = ctx.enter_context(nc.psum_tensor("pden", [P, G * CH], F32))
        pst = ctx.enter_context(nc.psum_tensor("pst", [P, KV * HD], F32))

        w_in = [sem(f"w_in{i}") for i in range(6)]
        c_in, w_hi, zeroed = sem("c_in"), sem("w_hi"), sem("zeroed")
        xst_in = [sem(f"xst_in{i}") for i in range(DC)]
        x_hi, xt_ready = sem("x_hi"), sem("xt_ready")
        s_hi, s_lo = sem("s_hi"), sem("s_lo")
        cs_in = sem("cs_in")
        passed = sem("passed_a")
        job_done, bank_free = sem("job_done"), sem("bank_free")
        shifted, sin_done, rot_done = sem("shifted"), sem("sin_done"), sem("rot_done")
        relu_done, f_done, hi_done = sem("relu_done"), sem("f_done"), sem("hi_done")
        lo_done = sem("lo_done")
        v_hi, t_hi = sem("v_hi"), sem("t_hi")
        z_scan, z_carry, product, p_hi = sem("z_scan"), sem("z_carry"), sem("product"), sem("p_hi")
        p_lo = sem("p_lo")
        d_done = sem("head_den_done")
        sc_done, a_hi, a_ready = sem("sc_done"), sem("a_hi"), sem("a_ready")
        sc_free = sem("sc_free")
        num_done = sem("num_done")
        num_free = sem("num_free")
        den_free = sem("den_free")
        unit_done = sem("unit_done")
        num_out = [sem("num_out0"), sem("num_out1")]
        den_out = sem("den_out")
        pro = ExitStack()
        with pro:
            NS, NQ, QC = 3, 4, D // 4
            stage = sb("stage", [P, NS, 2048], F32, pro)
            fa = [sb(f"fa{i}", [P, FB, QC], F32, pro) for i in range(2)]
            fb = sb("fb", [P, FB, QC], F32, pro)
            fh = [sb(f"fh{i}", [P, FB, QC], F32R, pro) for i in range(2)]
            fl = [sb(f"fl{i}", [P, FB, QC], F32R, pro) for i in range(2)]
            fo = sb("fo", [P, FB, QC], F32, pro)
            hadf = sb("hadf", [P, P], F32, pro)
            hadp, hadn = sb("hadp", [P, P], F32R, pro), sb("hadn", [P, P], F32R, pro)
            sdc, scb = sb("sdc", [P, FB], F32, pro), sb("scb", [P, D], F32, pro)
            pf = pj + psc + pnum
            f_in = [pro.enter_context(nc.semaphore(f"f_in{i}")) for i in range(2)]
            w_lo = [pro.enter_context(nc.semaphore(f"w_lo{i}")) for i in range(NS)]
            had_in, sd_in, had_ready, sd_ready, f_bf, f_hi, f_lo, f_mm, f_w, f_out, state_zero = (
                pro.enter_context(nc.semaphore(n)) for n in
                ("had_in_f", "sd_in", "had_ready_f", "sd_ready", "f_bf", "f_hi", "f_lo", "f_mm", "f_w", "f_out", "state_zero"))
            parts = [(wq[:, 4 * i:4 * i + 4].rearrange("p h c e -> p (h c e)"),
                      wqh[:, 4 * i:4 * i + 4].rearrange("p h c e -> p (h c e)"),
                      wql[:, 4 * i:4 * i + 4].rearrange("p h c e -> p (h c e)")) for i in range(4)]
            parts = [(wk.rearrange("p h c e -> p (h c e)"), wkh[:].rearrange("p h c e -> p (h c e)"),
                      wkl[:].rearrange("p h c e -> p (h c e)"))] + parts[:1] + \
                    [(wv.rearrange("p c n -> p (c n)"), wvh[:].rearrange("p c n -> p (c n)"),
                      wvl[:].rearrange("p c n -> p (c n)"))] + parts[1:]
            block = pro.enter_context(nc.Block())

            def cols(q):
                return slice(q * QC, (q + 1) * QC)

            def flat(a):
                return a.rearrange("p b n -> p (b n)")

            def weights_lo(eng, ops, i):
                eng.wait_ge(w_hi, i + 1)
                ops.tensor_tensor(parts[i][2], stage[:, i % NS, :], f32(parts[i][1]), ALU.subtract).then_inc(w_lo[i % NS], 1)

            @block.sync
            def _(sp):
                def load_down(q):
                    if q >= 2:
                        sp.wait_ge(f_lo, q - 1)
                    sp.dma_start(fa[q % 2][:, :, :], wd[:, :, cols(q)]).then_inc(f_in[q % 2], 16)

                def load_weights(i):
                    if i >= NS:
                        sp.wait_ge(w_lo[i % NS], i // NS)
                    sp.dma_start(stage[:, i % NS, :], parts[i][0]).then_inc(w_in[i], 16)

                def store_down(q):
                    sp.wait_ge(f_w, FB * (q + 1))
                    sp.dma_start(wd_d[:, :, cols(q)], fo[:, :, :]).then_inc(f_out, 16)

                load_down(0)
                sp.dma_start(hadf[:, :], consts[:, P:2 * P]).then_inc(had_in, 16)
                load_weights(0)
                load_down(1)
                sp.dma_start(sdc[:, :], sd).then_inc(sd_in, 16)
                sp.dma_start(scb[:, :], wsd.broadcast_to([P, D])).then_inc(sd_in, 16)
                sp.dma_start(ident[:, :], consts[:, 0:P]).then_inc(c_in, 16)
                load_weights(1)
                load_weights(2)
                load_down(2)
                load_weights(3)
                load_down(3)
                store_down(0)
                load_weights(4)
                store_down(1)
                load_weights(5)
                for c in range(XS):
                    sp.dma_start(xst[:, c, :], xT[0, :, c, :]).then_inc(xst_in[c], 16)
                sp.dma_start(cosb[:, :], cosT[:, 0:MT]).then_inc(cs_in, 16)
                sp.dma_start(sinb[:, :], sinT[:, 0:MT]).then_inc(cs_in, 16)
                for q in range(2, NQ):
                    store_down(q)
                sp.wait_ge(f_out, 16 * NQ)
                sp.wait_ge(cs_in, 32)
                sp.wait_ge(c_in, 16)

            @block.gpsimd
            def _(pool):
                nc.gpsimd.memset(carry[:], 0.0)
                nc.gpsimd.memset(f32(Sh[:]), 0.0).then_inc(zeroed, 1)
                nc.gpsimd.memset(f32(Sl[:]), 0.0).then_inc(s_lo, 1)
                nc.gpsimd.memset(f32(xh[:, 0, :]), 0.0).then_inc(zeroed, 1)
                nc.gpsimd.memset(f32(onesd[:]), 0.0).then_inc(zeroed, 1)
                pool.wait_ge(zeroed, 3)
                for i in range(G):
                    nc.gpsimd.memset(f32(onesd[:, i, i:i + 1]), 1.0).then_inc(zeroed, 1)
                for s, ahead in ((bank_free, 2), (sc_free, 2), (num_free, 2), (den_free, 1), (unit_done, 2),
                                 (lo_done, NT), (p_lo, NT), (d_done, 1), (num_out[0], 16), (num_out[1], 16), (den_out, 16)):
                    nc.gpsimd.sem_inc(s, ahead)
                for q in range(NQ):
                    pool.wait_ge(f_hi, q + 1)
                    nc.gpsimd.tensor_tensor(flat(fl[q % 2][:]), flat(fa[q % 2][:]), f32(flat(fh[q % 2][:])),
                                            ALU.subtract).then_inc(f_lo, 1)
                    if q >= 2:
                        weights_lo(pool, nc.gpsimd, q + 2)

            @block.scalar
            def _(act):
                act.wait_ge(had_in, 16)
                nc.scalar.activation(hadn[:, :], hadf[:, :], ACT.Copy, scale=-1.0).then_inc(had_ready, 1)
                i = 0
                for q in range(NQ):
                    act.wait_ge(f_bf, 4 * q + 4)
                    if q >= 2:
                        act.wait_ge(f_mm, NQ * (q - 1))
                    nc.scalar.activation(flat(fh[q % 2][:]), flat(fa[q % 2][:]), ACT.Copy).then_inc(f_hi, 1)
                    for _ in range((1, 2, 2, 1)[q]):
                        act.wait_ge(w_in[i], 16)
                        nc.scalar.activation(parts[i][1], stage[:, i % NS, :], ACT.Copy).then_inc(w_hi, 1)
                        i += 1

            @block.vector
            def _(dve):
                def butterflies(q):
                    dve.wait_ge(f_in[q % 2], 16 * (q // 2) + 16)
                    src, dst = fa[q % 2], fb
                    for k, h in enumerate((1, 2)):
                        i = src[:].rearrange("p (a b c) n -> p b a (c n)", b=2, c=h)
                        o = dst[:].rearrange("p (a b c) n -> p b a (c n)", b=2, c=h)
                        if q or k:
                            dve.wait_ge(f_bf, 4 * q + 2 * k)
                        nc.vector.tensor_tensor(o[:, 0], i[:, 0], i[:, 1], ALU.add).then_inc(f_bf, 1)
                        nc.vector.tensor_tensor(o[:, 1], i[:, 0], i[:, 1], ALU.subtract).then_inc(f_bf, 1)
                        src, dst = dst, src

                def scale(q):
                    if q:
                        dve.wait_ge(f_out, 16 * q)
                    for b in range(FB):
                        k = NQ * q + b // 4
                        if b % 4 == 0:
                            dve.wait_ge(f_mm, k + 1)
                        nc.vector.scalar_tensor_tensor(out=fo[:, b, :], in0=pf[k % 6][:, (b % 4) * QC:(b % 4 + 1) * QC],
                                                       scalar=sdc[:, b:b + 1], in1=scb[:, cols(q)], op0=ALU.mult,
                                                       op1=ALU.mult).then_inc(f_w, 1)

                dve.wait_ge(had_in, 16)
                nc.vector.tensor_copy(hadp[:, :], hadf[:, :]).then_inc(had_ready, 1)
                for q in range(NQ):
                    butterflies(q)
                    weights_lo(dve, nc.vector, q)
                    if q == 0:
                        dve.wait_ge(sd_in, 32)
                        nc.vector.tensor_scalar_mul(sdc[:, :], sdc[:, :], float(F) ** -0.5).then_inc(sd_ready, 1)
                        dve.wait_ge(sd_ready, 1)
                    else:
                        scale(q - 1)
                scale(NQ - 1)

            @block.tensor
            def _(pe):
                pe.wait_ge(zeroed, 2)
                nc.tensor.matmul(pst[:, :], Sh[:, :], xh[:, 0, :], start=True, stop=True,
                                 skip_group_check=True).then_inc(state_zero, 1)
                pe.wait_ge(had_ready, 2)
                for q in range(NQ):
                    pe.wait_ge(f_lo, q + 1)
                    for o in range(4):
                        k = NQ * q + o
                        if k >= 6:
                            pe.wait_ge(f_w, 4 * (k - 6) + 4)
                        n = 0
                        for i in range(4):
                            w = hadn if bin(o & i).count("1") % 2 else hadp
                            for f in (fh[q % 2], fl[q % 2]):
                                last = nc.tensor.matmul(pf[k % 6][:, :], w[:, :], flat(f[:, 4 * i:4 * i + 4]), start=(n == 0),
                                                        stop=(n == 7))
                                n += 1
                        last.then_inc(f_mm, 1)

        Vh, Vl = sb("Vh", [P, NCH, KV * HD], F32R), sb("Vl", [P, NCH, KV * HD], F32R)
        Qh = [sb(f"Qh{i}", [P, G + 1, MT], F32R) for i in range(2)]
        Ql = [sb(f"Ql{i}", [P, G + 1, MT], F32R) for i in range(2)]
        Kth = [sb(f"Kth{i}", [P, NCH, HD], F32R) for i in range(2)]
        Ktl = [sb(f"Ktl{i}", [P, NCH, HD], F32R) for i in range(2)]
        Kf = sb("Kf", [P, MT])
        ta = [sb(f"ta{i}", [P, MT]) for i in range(NT)]
        tb = [sb(f"tb{i}", [P, MT]) for i in range(NT)]
        Ah = [sb(f"Ah{i}", [P, G, CH], F32R) for i in range(2)]
        Al = [sb(f"Al{i}", [P, G, CH], F32R) for i in range(2)]
        no = [sb(f"no{i}", [P, G, CH]) for i in range(2)]
        Ph, Pl = sb("Ph", [P, MT], F32R), sb("Pl", [P, MT], F32R)
        zc = sb("zc", [P, MT])
        dn = sb("dn", [G, MT])

        block = ctx.enter_context(nc.Block())

        def bodies(eng, body):
            body(-1, [e for e in EVENTS if e[3] == 1])
            with eng.Fori(0, NM - 1) as m:
                body(m, EVENTS)
            body(NM - 1, [e for e in EVENTS if e[3] == 0])

        def is_start(m):
            return isinstance(m, int) and m < 0

        @block.tensor
        def _(pe):
            def body(m, events):
                for kind, g, c, d in events:
                    if kind in "JVT":
                        bank = pj[job_bank(kind, g, c)]
                        pe.wait_ge(bank_free, job_number(kind, g, c, m, d) + 1)
                    u = g * NCH + c
                    tok = slice(c * CH, (c + 1) * CH)
                    hd = slice(g * HD, (g + 1) * HD)
                    qh, ql = Qh[g % 2], Ql[g % 2]
                    if kind == "J":
                        wh, wl = (wkh[:, g], wkl[:, g]) if c == 0 else (wqh[:, G * g + c - 1], wql[:, G * g + c - 1])
                        k = 0
                        for b in range(DC):
                            if (g, c) == (0, 0):
                                pe.wait_ge(xt_ready, m * DC + (d * DC + b + 1))
                            for w, x in ((wh, xh), (wh, xl), (wl, xh)):
                                last = nc.tensor.matmul(bank[:, :], w[:, b, :], x[:, b, :], start=(k == 0), stop=(k == 11))
                                k += 1
                        last.then_inc(job_done, 1)
                    elif kind == "V":
                        tok = slice(g * CH, (g + 1) * CH)
                        k = 0
                        for b in range(DC):
                            for x, w in ((xh, wvh), (xh, wvl), (xl, wvh)):
                                last = nc.tensor.matmul(bank[:, :], x[:, b, tok], w[:, b, :], start=(k == 0), stop=(k == 11))
                                k += 1
                        last.then_inc(job_done, 1)
                    elif kind == "T":
                        pe.wait_ge(f_done, rope_number((kind, g, 0, d), m) + 1)
                        for q in range(NCH):
                            last = nc.tensor.transpose(bank[:, q * CH:(q + 1) * CH], Kf[:, q * CH:(q + 1) * CH], ident[:, :])
                        last.then_inc(job_done, 1)
                    elif kind == "C":
                        pe.wait_ge(lo_done, m * NR + ((g + 1) * (G + 1) + NT))
                        pe.wait_ge(sc_free, m * NU + u + 1)
                        out = psc[u % 2][:, :].rearrange("p (h t) -> p h t", h=G)
                        for k, (a, b) in enumerate(((qh, qh), (qh, ql), (ql, qh))):
                            last = nc.tensor.matmul(out, a[:, 0, tok], b[:, 1:, tok], start=(k == 0), stop=(k == 2))
                        last.then_inc(sc_done, 1)
                    elif kind == "U":
                        num = pnum[u % 2][:, :].rearrange("p (h t) -> p h t", h=G)
                        ah, al = Ah[u % 2], Al[u % 2]
                        pe.wait_ge(num_free, m * NU + u + 1)
                        if g == 0:
                            pe.wait_ge(bank_free, job_number("V", c, 0, m, 0) + 3)
                        pe.wait_ge(a_ready, m * NU + u + 1)
                        for k, (a, b) in enumerate(((Vh, ah), (Vh, al), (Vl, ah))):
                            nc.tensor.matmul(num, a[:, c, hd], b[:, :, :], start=(k == 0), stop=False)
                        pe.wait_ge(s_lo, m * NU + u + 1)
                        for k, (a, b) in enumerate(((Sh, qh), (Sh, ql), (Sl, qh))):
                            last = nc.tensor.matmul(num, a[:, :], b[:, 1:, tok], start=False, stop=(k == 2))
                        last.then_inc(num_done, 1)
                        if c == 0:
                            pe.wait_ge(bank_free, job_number("T", g, 0, m, 0) + 3)
                        kh, kl = Kth[g % 2], Ktl[g % 2]
                        for k, (a, b) in enumerate(((kh, Vh), (kh, Vl), (kl, Vh))):
                            last = nc.tensor.matmul(pst[:, hd], a[:, c, :], b[:, c, hd], start=False, stop=(k == 2),
                                                    skip_group_check=True)
                        last.then_inc(unit_done, 1)
                    elif kind == "D":
                        pe.wait_ge(p_lo, product_number((kind, g, c, d), m) + (1 + NT))
                        if c == 1:
                            pe.wait_ge(den_free, m * KV + (d * KV + g + 1))
                        nc.tensor.matmul(pden[0:G, :], onesd[:, c - 1, :], Ph[:, :], start=(c == 1), stop=False)
                        nc.tensor.matmul(pden[0:G, :], onesd[:, c - 1, :], Pl[:, :], start=False,
                                         stop=(c == G)).then_inc(d_done, 1)

            bodies(pe, body)

        @block.scalar
        def _(act):
            def body(m, events):
                for e in events:
                    kind, g, c, d = e
                    u = g * NCH + c
                    if kind in BANK_READS:
                        bank = pj[job_bank(BANK_READS[kind], g, c)]
                        act.wait_ge(job_done, job_number(BANK_READS[kind], g, c, m, d) + 1)
                    if kind == "S":
                        s = (g * (G + 1) + c) % NT
                        if not (is_start(m) and g * (G + 1) + c < NT):
                            act.wait_ge(lo_done, slot_free(e, m)[0])
                            act.wait_ge(p_lo, slot_free(e, m)[1])
                        nc.scalar.activation(tb[s][0:64, :], bank[64:128, :], ACT.Copy)
                        nc.scalar.activation(tb[s][64:128, :], bank[0:64, :], ACT.Copy).then_inc(shifted, 1)
                    elif kind == "R":
                        s = (g * (G + 1) + c) % NT
                        act.wait_ge(rot_done, rope_number(e, m) + 1)
                        nc.scalar.activation(tb[s][:, :], ta[s][:, :], ACT.Exp)
                        nc.scalar.activation(ta[s][:, :], ta[s][:, :], ACT.Relu).then_inc(relu_done, 1)
                    elif kind == "L":
                        src = Kf if c == 0 else tb[(g * (G + 1) + c) % NT]
                        act.wait_ge(f_done, rope_number(e, m) + 1)
                        nc.scalar.activation(Qh[g % 2][:, c, :], src[:, :], ACT.Copy).then_inc(hi_done, 1)
                    elif kind == "W":
                        if not is_start(m):
                            act.wait_ge(unit_done, m * NU + ((KV - 1) * NCH + g + 3))
                        nc.scalar.activation(Vh[:, g, :], bank[:, :], ACT.Copy).then_inc(v_hi, 1)
                    elif kind == "K":
                        nc.scalar.activation(Kth[g % 2][:].rearrange("p c e -> p (c e)"), bank[:, :],
                                             ACT.Copy).then_inc(t_hi, 1)
                    elif kind == "P":
                        act.wait_ge(product, product_number(e, m) + 1)
                        act.wait_ge(d_done, product_number(e, m) + 1)
                        nc.scalar.activation(Ph[:, :], ta[(g * (G + 1) + c) % NT][:, :], ACT.Copy).then_inc(p_hi, 1)
                    elif kind == "X":
                        act.wait_ge(xst_in[g], m * 16 + 32)
                        if not is_start(m):
                            act.wait_ge(job_done, job_number("J", KV - 1, G, m, 0) + 1)
                        nc.scalar.activation(xh[:, g, :], xst[:, g % XS, :], ACT.Copy).then_inc(x_hi, 1)
                    elif kind == "A":
                        act.wait_ge(sc_done, m * NU + u + 1)
                        act.wait_ge(unit_done, m * NU + u + 1)
                        nc.scalar.activation(Ah[u % 2][:].rearrange("p h t -> p (h t)"), psc[u % 2][:, :],
                                             ACT.Copy).then_inc(a_hi, 1)
                    elif kind == "N":
                        gn = ((u + 1) % NU) // NCH
                        act.wait_ge(unit_done, m * NU + u + 3)
                        nc.scalar.activation(Sh[:, :], pst[:, gn * HD:(gn + 1) * HD], ACT.Copy).then_inc(s_hi, 1)

            bodies(act, body)

        @block.vector
        def _(dve):
            def body(m, events):
                for e in events:
                    kind, g, c, d = e
                    u = g * NCH + c
                    s = (g * (G + 1) + c) % NT
                    if kind in BANK_READS:
                        bank = pj[job_bank(BANK_READS[kind], g, c)]
                    if kind == "S":
                        if (g, c) == (0, 0):
                            dve.wait_ge(cs_in, m * 32 + (d * 32 + 32))
                        dve.wait_ge(shifted, rope_number(e, m) + 1)
                        nc.vector.tensor_tensor(ta[s][:, :], bank[:, :], cosb[:, :], ALU.mult).then_inc(bank_free, 1)
                    elif kind == "R":
                        dve.wait_ge(sin_done, rope_number(e, m) + 1)
                        dve.wait_ge(bank_free, job_number("J", g, c, m, d) + 3)
                        nc.vector.tensor_tensor(ta[s][:, :], ta[s][:, :], tb[s][:, :], ALU.add).then_inc(rot_done, 1)
                    elif kind == "E":
                        dve.wait_ge(relu_done, rope_number(e, m) + 1)
                        dst = Kf if c == 0 else tb[s]
                        nc.vector.scalar_tensor_tensor(out=dst[:, :], in0=tb[s][:, :], scalar=1.0, in1=ta[s][:, :],
                                                       op0=ALU.min, op1=ALU.add).then_inc(f_done, 1)
                        dve.wait_ge(f_done, rope_number(e, m) + 1)
                        if c == 0:
                            z = m * KV + (d * KV + g + 1)
                            nc.vector.tensor_tensor_scan(zc[:, :], Kf[:, :], Kf[:, :], carry[:, g:g + 1], ALU.add,
                                                         ALU.max).then_inc(z_scan, 1)
                            dve.wait_ge(z_scan, z)
                            nc.vector.tensor_copy(carry[:, g:g + 1], zc[:, MT - 1:MT]).then_inc(z_carry, 1)
                        else:
                            dve.wait_ge(z_scan, m * KV + (d * KV + g + 1))
                            nc.vector.tensor_tensor(ta[s][:, :], tb[s][:, :], zc[:, :], ALU.mult).then_inc(product, 1)
                    elif kind == "W":
                        dve.wait_ge(v_hi, m * NCH + (NCH + g + 1))
                        nc.vector.tensor_tensor(Vl[:, g, :], bank[:, :], f32(Vh[:, g, :]),
                                                ALU.subtract).then_inc(bank_free, 1)
                    elif kind == "K":
                        z = m * KV + (d * KV + g + 1)
                        dve.wait_ge(t_hi, z)
                        nc.vector.tensor_tensor(Ktl[g % 2][:].rearrange("p c e -> p (c e)"), bank[:, :],
                                                f32(Kth[g % 2][:].rearrange("p c e -> p (c e)")),
                                                ALU.subtract).then_inc(bank_free, 1)
                    elif kind == "X":
                        dve.wait_ge(x_hi, m * DC + (DC + g + 1))
                        nc.vector.tensor_tensor(xl[:, g, :], xst[:, g % XS, :], f32(xh[:, g, :]),
                                                ALU.subtract).then_inc(xt_ready, 1)
                    elif kind == "A":
                        dve.wait_ge(a_hi, m * NU + u + 1)
                        nc.vector.tensor_tensor(Al[u % 2][:].rearrange("p h t -> p (h t)"), psc[u % 2][:, :],
                                                f32(Ah[u % 2][:].rearrange("p h t -> p (h t)")),
                                                ALU.subtract).then_inc(sc_free, 1)
                    elif kind == "N":
                        gn = ((u + 1) % NU) // NCH
                        dve.wait_ge(s_hi, m * NU + u + 1)
                        nc.vector.tensor_tensor(Sl[:, :], pst[:, gn * HD:(gn + 1) * HD], f32(Sh[:, :]),
                                                ALU.subtract).then_inc(s_lo, 1)
                    elif kind == "O":
                        dve.wait_ge(num_done, m * NU + u + 1)
                        dve.wait_ge(num_out[u % 2], m * (8 * NU) + 16 * (u // 2) + 16)
                        nc.vector.tensor_copy(no[u % 2][:].rearrange("p h t -> p (h t)"),
                                              pnum[u % 2][:, :]).then_inc(num_free, 1)
                    elif kind == "Y":
                        dve.wait_ge(d_done, m * H + (d * H + (g + 1) * G + 1))
                        dve.wait_ge(den_out, m * (16 * KV) + (d * 16 * KV + 16 * g + 16))
                        nc.vector.tensor_copy(dn[:, :], pden[0:G, :]).then_inc(den_free, 1)

            bodies(dve, body)

        @block.gpsimd
        def _(pool):
            def body(m, events):
                for e in events:
                    kind, g, c, d = e
                    s = (g * (G + 1) + c) % NT
                    if kind == "S":
                        if (g, c) == (0, 0):
                            pool.wait_ge(cs_in, m * 32 + (d * 32 + 32))
                        pool.wait_ge(shifted, rope_number(e, m) + 1)
                        nc.gpsimd.tensor_tensor(tb[s][:, :], tb[s][:, :], sinb[:, :], ALU.mult).then_inc(sin_done, 1)
                    elif kind == "L":
                        src = Kf if c == 0 else tb[s]
                        pool.wait_ge(hi_done, rope_number(e, m) + 1)
                        nc.gpsimd.tensor_tensor(Ql[g % 2][:, c, :], src[:, :], f32(Qh[g % 2][:, c, :]),
                                                ALU.subtract).then_inc(lo_done, 1)
                    elif kind == "P":
                        pool.wait_ge(p_hi, product_number(e, m) + 1)
                        nc.gpsimd.tensor_tensor(Pl[:, :], ta[s][:, :], f32(Ph[:, :]), ALU.subtract).then_inc(p_lo, 1)
                    elif kind == "A":
                        u = g * NCH + c
                        pool.wait_ge(sc_free, m * NU + u + 3)
                        nc.gpsimd.sem_inc(passed, 1)
                        for a in (Ah[u % 2], Al[u % 2]):
                            ins = nc.gpsimd.affine_select(out=a[:, :, :], in_=a[:, :, :], compare_op=ALU.is_ge, fill=0.0,
                                                          base=0, pattern=[[0, G], [1, CH]], channel_multiplier=-1)
                        ins.then_inc(a_ready, 1)

            bodies(pool, body)

        @block.sync
        def _(sp):
            def load_x(m, blocks, ahead, nxt):
                for c in blocks:
                    sp.wait_ge(xt_ready, m * DC + (DC + ahead))
                    sp.dma_start(xst[:, c % XS, :], xT[(m + nxt) % NM, :, c, :]).then_inc(xst_in[c], 16)

            def body(m, events):
                last = isinstance(m, int)
                for u in range(NU):
                    g, c = divmod(u, NCH)
                    if u == 10 and not last:
                        load_x(m, range(XS, DC), DC - XS, 1)
                        sp.wait_ge(sin_done, m * NR + NR)
                        sp.wait_ge(bank_free, job_number("J", KV - 1, G, m, 0) + 3)
                        sp.dma_start(cosb[:, :], cosT[:, bass.ts(m + 1, MT)]).then_inc(cs_in, 16)
                        sp.dma_start(sinb[:, :], sinT[:, bass.ts(m + 1, MT)]).then_inc(cs_in, 16)
                    if u == 12 and not last:
                        load_x(m, range(XS), DC, 2)
                    sp.wait_ge(num_free, m * NU + u + 3)
                    sp.dma_start(num_d[m * NCH + c, :, g * G:(g + 1) * G, :], no[u % 2][:, :, :]).then_inc(num_out[u % 2], 16)
                    if c == 0:
                        chunks = slice(m * NCH, (m + 1) * NCH) if last else bass.ds(m * NCH, NCH)
                        sp.wait_ge(den_free, m * KV + (g + 2))
                        sp.dma_start(den_d[chunks, g * G:(g + 1) * G, :].rearrange("c h t -> h c t"),
                                     dn[:, :].rearrange("h (c t) -> h c t", c=NCH)).then_inc(den_out, 16)

            load_x(-1, range(XS, DC), DC - XS, 1)
            load_x(-1, range(XS), DC, 2)
            with sp.Fori(0, NM - 1) as m:
                body(m, EVENTS)
            body(NM - 1, EVENTS)
            sp.wait_ge(num_out[0], NM * NU * 8 + 16)
            sp.wait_ge(num_out[1], NM * NU * 8 + 16)
            sp.wait_ge(den_out, NM * KV * 16 + 16)
            for c in range(XS):
                sp.wait_ge(xst_in[c], 16 * (NM + 1))


def phase_b(nc, x, wo, su, consts, num_d, den_d, rden_d, x1_d, x2_d):
    ctx = ExitStack()
    NC = T // CH
    WP = 4
    with ctx:
        def sb(name, shape, dt=F32):
            return ctx.enter_context(nc.sbuf_tensor(name, shape, dt))

        def sem(name):
            return ctx.enter_context(nc.semaphore(name))

        woh, wol = sb("woh", [P, H, D], F32R), sb("wol", [P, H, D], F32R)
        stage = [sb(f"stage_b{i}", [P, H // WP, D]) for i in range(2)]
        da = sb("da", [P, T * H // P])
        nt = [sb(f"nt{i}", [P, H, CH]) for i in range(2)]
        rrow = [sb(f"rrow{i}", [1, H * CH]) for i in range(2)]
        rb = [sb(f"rb{i}", [P, H * CH]) for i in range(2)]
        xr = [sb(f"xr{i}", [P, D]) for i in range(2)]
        oh = [sb(f"oh{i}", [P, H, CH], F32R) for i in range(2)]
        ol = [sb(f"ol{i}", [P, H, CH], F32R) for i in range(2)]
        x1 = [sb(f"x1{i}", [P, D]) for i in range(2)]
        stats, mv, ve, rstd = sb("stats", [P, 6]), sb("mv", [P, 2]), sb("ve", [P, 1]), sb("rstd", [P, 1])
        xs, xb, xc = sb("xs", [P, DC, MT]), sb("xb", [P, DC, MT]), sb("xc", [P, DC, MT])
        xsh, xsl = sb("xsh", [P, DC, MT], F32R), sb("xsl", [P, DC, MT], F32R)
        x2 = sb("x2", [P, DC, MT])
        suc = sb("suc", [P, DC])
        identb, had, hadr = sb("identb", [P, P]), sb("had", [P, P]), sb("hadr", [P, P], F32R)
        neghalf = sb("neghalf", [P, 1])
        py = [ctx.enter_context(nc.psum_tensor(f"py{i}", [P, D], F32)) for i in range(2)]
        pt = [ctx.enter_context(nc.psum_tensor(f"pt{i}", [P, DC, CH], F32)) for i in range(2)]
        ph = [ctx.enter_context(nc.psum_tensor(f"ph{i}", [P, MT], F32)) for i in range(DC)]
        x_v = x.rearrange("(n p) d -> n p d", p=CH)
        x1_v = x1_d.rearrange("(n p) d -> n p d", p=CH)

        passed, passed_pool = sem("passed_b"), sem("passed_b_pool")
        w_in = [sem("wo_in0"), sem("wo_in1")]
        id_in, had_in, su_in, had_ready = sem("id_in"), sem("had_in"), sem("su_in"), sem("had_ready")
        w_hi, w_lo = sem("wo_hi"), sem("wo_lo")
        d_in, d_step, d_out = sem("d_in"), sem("d_step"), sem("d_out")
        nt_in = [sem("nt_in0"), sem("nt_in1")]
        row_in = [sem("row_in0"), sem("row_in1")]
        xr_in = [sem("xr_in0"), sem("xr_in1")]
        rb_done = sem("rb_done")
        o_done, o_hi, o_lo = sem("o_done"), sem("o_hi"), sem("o_lo")
        y_done = sem("y_done")
        r_done = sem("r_done")
        ln_step, rstd_done, x1_ready = sem("ln_step"), sem("rstd_done"), sem("x1_ready")
        x1_out = [sem("x1_out0"), sem("x1_out1")]
        tr_done = sem("tr_done")
        tr_free = sem("tr_free")
        bf_step, xs_hi = sem("bf_step"), sem("xs_hi")
        xs_lo = sem("xs_lo")
        had_done = sem("had_done")
        had_free = sem("had_free")
        x2_out = sem("x2_out")

        def heads(a, i):
            return a[:, i * (H // WP):(i + 1) * (H // WP)].rearrange("p h n -> p (h n)")

        def columns_lo(eng, ops, m1):
            eng.wait_ge(xs_hi, m1)
            ops.tensor_tensor(xsl[:].rearrange("p c t -> p (c t)"), xc[:].rearrange("p c t -> p (c t)"),
                              f32(xsh[:].rearrange("p c t -> p (c t)")), ALU.subtract).then_inc(xs_lo, 1)

        def load_numerators(sp, n, s):
            row = rden_d[n:n + 1, :] if isinstance(n, int) else rden_d[bass.ds(n, 1), :]
            sp.dma_start(rrow[s][:, :], row).then_inc(row_in[s], 16)
            sp.dma_start(nt[s][:, :, :], num_d[n]).then_inc(nt_in[s], 16)

        block = ctx.enter_context(nc.Block())

        def before(m, j, k):
            return (j - k) % NCH, m * NCH + j - k

        @block.tensor
        def _(pe):
            def transposes(jp, n):
                s = jp % 2
                pe.wait_ge(x1_ready, n + 1)
                pe.wait_ge(tr_free, n + 1)
                for c in range(DC):
                    last = nc.tensor.transpose(pt[s][:, c, :], x1[s][:, c * P:(c + 1) * P], identb[:, :])
                last.then_inc(tr_done, 1)

            def transform(m1):
                pe.wait_ge(xs_lo, m1 + 1)
                pe.wait_ge(had_free, m1 * DC)
                for c in range(DC):
                    nc.tensor.matmul(ph[c][:, :], hadr[:, :], xsh[:, c, :], start=True, stop=False)
                    last = nc.tensor.matmul(ph[c][:, :], hadr[:, :], xsl[:, c, :], start=False, stop=True)
                    last.then_inc(had_done, 1)

            def step(m, j, first):
                n = m * NCH + j
                s = j % 2
                pe.wait_ge(o_lo, n + 1)
                pe.wait_ge(r_done, n + 1)
                k = 0
                for h in range(H):
                    if first and j == 0 and h % (H // WP) == 0:
                        pe.wait_ge(w_lo, h // (H // WP) + 1)
                    for a, b in ((oh, woh), (oh, wol), (ol, woh)):
                        last = nc.tensor.matmul(py[s][:, :], a[s][:, h, :], b[:, h, :], start=(k == 0), stop=(k == 3 * H - 1))
                        k += 1
                    if h == 11:
                        if j or not first:
                            transposes(*before(m, j, 1))
                        if j == 2 and not first:
                            transform(m)
                last.then_inc(y_done, 1)

            pe.wait_ge(id_in, 16)
            pe.wait_ge(had_ready, 1)
            for j in range(NCH):
                step(0, j, True)
            with pe.Fori(1, NM) as m:
                for j in range(NCH):
                    step(m, j, False)
            transposes(NCH - 1, NC - 1)
            transform(NM)

        @block.scalar
        def _(act):
            def columns(jp, n, stage1):
                s = jp % 2
                act.wait_ge(tr_done, n + 1)
                if stage1 is not None:
                    act.wait_ge(bf_step, stage1)
                for c in range(DC):
                    last = nc.scalar.activation(xs[:, c, jp * CH:(jp + 1) * CH], pt[s][:, c, :], ACT.Copy,
                                                scale=suc[:, c:c + 1])
                last.then_inc(tr_free, 1)

            def split(m1):
                act.wait_ge(bf_step, m1 * 4)
                act.wait_ge(had_free, m1 * DC)
                nc.scalar.activation(xsh[:].rearrange("p c t -> p (c t)"), xc[:].rearrange("p c t -> p (c t)"),
                                     ACT.Copy).then_inc(xs_hi, 1)

            def write_x2(m1, mt):
                act.wait_ge(x2_out, m1 * 16)
                for c in range(DC):
                    act.wait_ge(had_done, m1 * DC - DC + c + 1)
                    last = nc.scalar.activation(x2[:, c, :], ph[c][:, :], ACT.Copy, scale=float(D) ** -0.5)
                    last.then_inc(had_free, 1)
                act.wait_ge(had_free, m1 * DC + DC)
                act.dma_start(x2_d[mt], x2[:, :, :]).then_inc(x2_out, 16)

            def weights_hi(i):
                act.wait_ge(w_in[i % 2], 16 * (i // 2) + 16)
                nc.scalar.activation(heads(woh, i), stage[i % 2][:].rearrange("p h n -> p (h n)"), ACT.Copy).then_inc(w_hi, 1)

            def step(m, j, first):
                n = m * NCH + j
                s = j % 2
                act.wait_ge(o_done, n + 1)
                act.wait_ge(y_done, n + 1)
                nc.scalar.activation(oh[s][:].rearrange("p h t -> p (h t)"), nt[s][:].rearrange("p h t -> p (h t)"),
                                     ACT.Copy).then_inc(o_hi, 1)
                if j == 2 and not first:
                    split(m)
                if j >= 2 or not first:
                    columns(*before(m, j, 2), m * 4 - 2 if j == 2 and not first else None)
                if j == 3 and not first:
                    write_x2(m, m - 1)

            for i in range(WP):
                weights_hi(i)
                if i == 1:
                    step(0, 0, True)
            act.wait_ge(su_in, 16)
            for j in range(1, NCH):
                step(0, j, True)
            with act.Fori(1, NM) as m:
                for j in range(NCH):
                    step(m, j, False)
            for k in (2, 1):
                columns(NCH - k, NC - k, None)
            split(NM)
            write_x2(NM, NM - 1)
            act.wait_ge(x2_out, 16 * NM + 16)

        @block.vector
        def _(dve):
            def norm(jp, n, m_of_n):
                s = jp % 2
                dve.wait_ge(y_done, n + 3)
                dve.wait_ge(x1_out[s], m_of_n * 32 + (jp // 2) * 16)
                dve.wait_ge(xr_in[s], m_of_n * 32 + (jp // 2) * 16 + 16)
                nc.vector.tensor_tensor(x1[s][:, :], py[s][:, :], xr[s][:, :], ALU.add).then_inc(r_done, 1)
                dve.wait_ge(r_done, n + 3)
                nc.vector.bn_stats(stats[:, :], x1[s][:, :]).then_inc(ln_step, 1)
                dve.wait_ge(ln_step, n * 3 + 1)
                nc.vector.sem_inc(passed, 1)
                nc.vector.bn_aggr(mv[:, :], stats[:, :]).then_inc(ln_step, 1)
                dve.wait_ge(ln_step, n * 3 + 2)
                nc.vector.tensor_scalar_add(ve[:, :], mv[:, 1:2], EPS).then_inc(ln_step, 1)
                dve.wait_ge(rstd_done, n + 1)
                nc.vector.tensor_scalar(x1[s][:, :], x1[s][:, :], mv[:, 0:1], rstd[:, 0:1], ALU.subtract,
                                        ALU.mult).then_inc(x1_ready, 1)

            def butterflies(m1):
                dve.wait_ge(tr_free, m1 * NCH + 2)
                base = m1 * 4 - 4
                for k, (src, dst, v) in enumerate(((xs, xb, "p (a b) t -> p b a t"), (xb, xc, "p (b a) t -> p b a t"))):
                    i, o = src[:].rearrange(v, b=2), dst[:].rearrange(v, b=2)
                    if k:
                        dve.wait_ge(bf_step, base + 2)
                        dve.wait_ge(xs_lo, m1)
                    nc.vector.tensor_tensor(o[:, 0], i[:, 0], i[:, 1], ALU.add).then_inc(bf_step, 1)
                    nc.vector.tensor_tensor(o[:, 1], i[:, 0], i[:, 1], ALU.subtract).then_inc(bf_step, 1)

            def weights_lo(i):
                dve.wait_ge(w_hi, i + 1)
                nc.vector.tensor_tensor(heads(wol, i), stage[i % 2][:].rearrange("p h n -> p (h n)"), f32(heads(woh, i)),
                                        ALU.subtract).then_inc(w_lo, 1)

            def divide(m, j):
                n = m * NCH + j
                s = j % 2
                dve.wait_ge(nt_in[s], m * 32 + (j // 2) * 16 + 16)
                dve.wait_ge(rb_done, n + 1)
                nc.vector.tensor_tensor(nt[s][:].rearrange("p h t -> p (h t)"), nt[s][:].rearrange("p h t -> p (h t)"),
                                        rb[s][:, :], ALU.mult).then_inc(o_done, 1)

            def lower_part(m, j):
                n = m * NCH + j
                s = j % 2
                dve.wait_ge(o_hi, n + 1)
                nc.vector.tensor_tensor(ol[s][:].rearrange("p h t -> p (h t)"), nt[s][:].rearrange("p h t -> p (h t)"),
                                        f32(oh[s][:].rearrange("p h t -> p (h t)")), ALU.subtract).then_inc(o_lo, 1)

            def step(m, j, first):
                if j != 2 or first:
                    divide(m, j)
                if j >= 2 or not first:
                    norm(*before(m, j, 2), m if j >= 2 else m - 1)
                lower_part(m, j)
                if j == 1 and not first:
                    divide(m, 2)
                    butterflies(m)

            dve.wait_ge(d_in, 16)
            nc.vector.tensor_scalar_add(da[:, :], da[:, :], 1e-6).then_inc(d_step, 1)
            dve.wait_ge(d_step, 1)
            nc.vector.reciprocal(da[:, :], da[:, :]).then_inc(d_step, 1)
            dve.wait_ge(had_in, 16)
            nc.vector.tensor_copy(hadr[:, :], had[:, :]).then_inc(had_ready, 1)
            for i in range(WP):
                weights_lo(i)
                if i == 1:
                    step(0, 0, True)
            for j in range(1, NCH):
                step(0, j, True)
            with dve.Fori(1, NM) as m:
                for j in range(NCH):
                    step(m, j, False)
            for k in (2, 1):
                norm(NCH - k, NC - k, NM - 1)
            butterflies(NM)
            columns_lo(dve, nc.vector, NM)

        @block.gpsimd
        def _(pool):
            def inverse_root(n):
                pool.wait_ge(ln_step, n * 3 + 3)
                nc.gpsimd.tensor_tensor(rstd[:, :], ve[:, :], neghalf[:, :], ALU.pow).then_inc(rstd_done, 1)

            def factors(m, j, first):
                n = m * NCH + j
                s = j % 2
                pool.wait_ge(row_in[s], m * 32 + (j // 2) * 16 + 16)
                if j >= 2 or not first:
                    pool.wait_ge(o_done, n - 1)
                nc.gpsimd.sem_inc(passed_pool, 1)
                nc.gpsimd.partition_broadcast(rb[s][:, :], rrow[s][:, :]).then_inc(rb_done, 1)

            def step(m, j, first):
                if j != 3:
                    factors(m, j, first)
                if j >= 2 or not first:
                    inverse_root(before(m, j, 2)[1])
                if j == 2:
                    factors(m, 3, first)
                if j == 2 and not first:
                    columns_lo(pool, nc.gpsimd, m)

            for s, ahead in ((y_done, 2), (r_done, 2), (tr_free, 2), (had_free, DC), (xs_lo, 1), (x2_out, 16)):
                nc.gpsimd.sem_inc(s, ahead)
            nc.gpsimd.memset(neghalf[:], -0.5).then_inc(passed_pool, 1)
            pool.wait_ge(passed_pool, 1)
            for j in range(NCH):
                step(0, j, True)
            with pool.Fori(1, NM) as m:
                for j in range(NCH):
                    step(m, j, False)
            for k in (2, 1):
                inverse_root(NC - k)

        @block.sync
        def _(sp):
            def load_weights(i):
                sp.dma_start(stage[i % 2][:, :, :], wo[:, i * (H // WP):(i + 1) * (H // WP)]).then_inc(w_in[i % 2], 16)

            def write_x1(jp, n):
                sp.wait_ge(x1_ready, n + 1)
                sp.dma_start(x1_v[n], x1[jp % 2][:, :]).then_inc(x1_out[jp % 2], 16)

            def step(m, j, first):
                n = m * NCH + j
                s = j % 2
                sp.wait_ge(o_lo, n + 1)
                load_numerators(sp, (n + 2) % NC, s)
                if j >= 2 or not first:
                    sp.wait_ge(r_done, n + 1)
                sp.dma_start(xr[s][:, :], x_v[n]).then_inc(xr_in[s], 16)
                if j >= 2 or not first:
                    write_x1(*before(m, j, 2))

            sp.dma_start(da[:, :], den_d.rearrange("n h t -> (n h t)").rearrange("(p q) -> p q", p=P)).then_inc(d_in, 16)
            load_weights(0)
            sp.wait_ge(d_step, 2)
            sp.dma_start(rden_d.rearrange("n k -> (n k)").rearrange("(p q) -> p q", p=P), da[:, :]).then_inc(d_out, 16)
            sp.dma_start(identb[:, :], consts[:, 0:P]).then_inc(id_in, 16)
            sp.dma_start(had[:, :], consts[:, P:2 * P]).then_inc(had_in, 16)
            sp.dma_start(suc[:, :], su).then_inc(su_in, 16)
            sp.wait_ge(d_out, 16)
            load_numerators(sp, 0, 0)
            load_weights(1)
            load_numerators(sp, 1, 1)
            for i in range(2, WP):
                sp.wait_ge(w_lo, i - 1)
                load_weights(i)
            for j in range(NCH):
                step(0, j, True)
            with sp.Fori(1, NM) as m:
                for j in range(NCH):
                    step(m, j, False)
            for k in (2, 1):
                write_x1(NCH - k, NC - k)
            for s in range(2):
                sp.wait_ge(x1_out[s], NM * 32)
                sp.wait_ge(nt_in[s], NM * 32 + 16)
                sp.wait_ge(row_in[s], NM * 32 + 16)


def phase_c(nc, wg, wu, wsg, wsu, wd_d, x1_d, x2_d, out):
    ctx = ExitStack()
    with ctx:
        def sb(name, shape, dt=F32, c=ctx):
            return c.enter_context(nc.sbuf_tensor(name, shape, dt))

        def sem(name):
            return ctx.enter_context(nc.semaphore(name))

        wgh, wgl = sb("wgh", [P, FB, DC, P], F32R), sb("wgl", [P, FB, DC, P], F32R)
        wuh, wul = sb("wuh", [P, FB, DC, P], F32R), sb("wul", [P, FB, DC, P], F32R)
        wdf = sb("wdf", [P, FB, D])
        NS = 4
        stage = sb("stage_c", [P, NS, DC * P])
        x2st = sb("x2st", [P, DC, MT])
        x2h, x2l = sb("x2h", [P, DC, MT], F32R), sb("x2l", [P, DC, MT], F32R)
        sg, su2 = sb("sg", [P, FB]), sb("su2", [P, FB])
        neghalf = sb("neghalfc", [P, 1])
        pgu = [ctx.enter_context(nc.psum_tensor(f"pgu{i}", [P, MT], F32)) for i in range(4)]
        pyc = [ctx.enter_context(nc.psum_tensor(f"pyc{i}", [P, D], F32)) for i in range(NCH)]
        x1_v = x1_d.rearrange("(n p) d -> n p d", p=CH)
        out_v = out.rearrange("(n p) d -> n p d", p=CH)

        parts = [[a[:, f].rearrange("p c n -> p (c n)") for a in w] for f in range(FB) for w in ((wg, wgh, wgl), (wu, wuh, wul))]
        w_in = [sem(f"wc_in{i}") for i in range(NS)]
        wd_in = [sem(f"wd_in{i}") for i in range(4)]
        w_hi, w_lo, sc_in, sc_step = sem("wc_hi"), sem("wc_lo"), sem("scale_in"), sem("scale_step")
        passed, set_up = sem("passed_c"), sem("set_up_c")
        x2_in = [sem(f"x2_in{i}") for i in range(DC)]
        x2_hi, x2_lo = sem("x2_hi"), sem("x2_lo")
        gu_done = sem("gu_done")
        gu_free = sem("gu_free")
        tanh_done, h_hi = sem("tanh_done"), sem("h_hi")
        h_lo = sem("h_lo")
        wd_hi, wd_lo = sem("wd_hi"), sem("wd_lo")
        d_done = sem("down_done")
        yb_done = sem("yb_done")
        y_free = sem("y_free")
        lnc_step, rc_done, o_ready = sem("lnc_step"), sem("rc_done"), sem("o_ready")
        x1_in = [sem(f"x1_in{i}") for i in range(NCH)]
        o_out = [sem(f"o_out{i}") for i in range(NCH)]

        wdh, wdl = [sb(f"wdh{i}", [P, D], F32R) for i in range(2)], [sb(f"wdl{i}", [P, D], F32R) for i in range(2)]
        th = [sb(f"th{i}", [P, MT]) for i in range(2)]
        hh, hl = [sb(f"hh{i}", [P, MT], F32R) for i in range(2)], [sb(f"hl{i}", [P, MT], F32R) for i in range(2)]
        x1r = [sb(f"x1r{i}", [P, D]) for i in range(NCH)]
        stats, mv, ve, rstd = sb("statsc", [P, 6]), sb("mvc", [P, 2]), sb("vec", [P, 1]), sb("rstdc", [P, 1])

        block = ctx.enter_context(nc.Block())

        @block.tensor
        def _(pe):
            def project(f, up, m, first):
                n = m * 2 * FB + 2 * f + up
                bank = pgu[2 * (f % 2) + up]
                wh, wl = (wuh, wul) if up else (wgh, wgl)
                pe.wait_ge(gu_free, n + 1)
                if first:
                    pe.wait_ge(w_lo, 2 * f + up + 1)
                k = 0
                for c in range(DC):
                    if f == 0 and not up:
                        pe.wait_ge(x2_lo, m * DC + c + 1)
                    for w, x in ((wh, x2h), (wh, x2l), (wl, x2h)):
                        last = nc.tensor.matmul(bank[:, :], w[:, f, c, :], x[:, c, :], start=(k == 0), stop=(k == 11))
                        k += 1
                last.then_inc(gu_done, 1)

            def down(f, m):
                s = f % 2
                pe.wait_ge(h_lo, m * FB + f + 3)
                pe.wait_ge(wd_lo, m * FB + f + 1)
                for t in range(NCH):
                    if f == 0:
                        pe.wait_ge(y_free, m * NCH + t + 1)
                    tok = slice(t * CH, (t + 1) * CH)
                    for k, (a, b) in enumerate(((hh, wdh), (hh, wdl), (hl, wdh))):
                        last = nc.tensor.matmul(pyc[t][:, :], a[s][:, tok], b[s][:, :], start=(f == 0 and k == 0),
                                                stop=(f == FB - 1 and k == 2))
                    if f == FB - 1 and t < NCH - 1:
                        last.then_inc(yb_done, 1)
                if f == FB - 1:
                    last.then_inc(yb_done, 1)
                else:
                    last.then_inc(d_done, 1)

            def tile(m, first):
                project(0, 0, m, first)
                if not first:
                    down(FB - 1, m - 1)
                project(0, 1, m, first)
                for f in range(1, FB):
                    project(f, 0, m, first)
                    project(f, 1, m, first)
                    down(f - 1, m)

            tile(0, True)
            with pe.Fori(1, NM) as m:
                tile(m, False)
            down(FB - 1, NM - 1)

        def used_before(eng, m, f):
            if f >= 2:
                eng.wait_ge(d_done, m * (FB - 1) + f - 1 + 2)
            elif f == 0:
                eng.wait_ge(d_done, m * (FB - 1) + 2)
            else:
                eng.wait_ge(yb_done, m * NCH)

        @block.scalar
        def _(act):
            def weights_hi(f):
                for i in (2 * f, 2 * f + 1):
                    act.wait_ge(w_in[i % NS], 16 * (i // NS + 1))
                    nc.scalar.activation(parts[i][1], stage[:, i % NS, :], ACT.Copy).then_inc(w_hi, 1)

            def tile(m, first):
                for f in range(FB):
                    s = f % 2
                    n = m * 2 * FB + 2 * f
                    if first and f + 1 < FB:
                        weights_hi(f + 1)
                    act.wait_ge(gu_done, n + 1)
                    act.wait_ge(h_lo, m * FB + f + 1)
                    nc.scalar.activation(th[s][:, :], pgu[2 * s][:, :], ACT.Tanh, scale=sg[:, f:f + 1]).then_inc(tanh_done, 1)
                    if f != 1 or not first:
                        used_before(act, m, f)
                    if first and f % 4 == 0:
                        act.wait_ge(wd_in[f // 4], 16)
                    nc.scalar.activation(wdh[s][:, :], wdf[:, f, :], ACT.Copy).then_inc(wd_hi, 1)
                    if f == FB - 1:
                        for c in range(DC):
                            act.wait_ge(x2_in[c], m * 16 + 32)
                            act.wait_ge(gu_done, m * 2 * FB + 2 * FB)
                            nc.scalar.activation(x2h[:, c, :], x2st[:, c, :], ACT.Copy).then_inc(x2_hi, 1)
                    act.wait_ge(gu_free, n + 2 + 4)
                    nc.scalar.activation(hh[s][:, :], th[s][:, :], ACT.Copy).then_inc(h_hi, 1)

            weights_hi(0)
            for c in range(DC):
                act.wait_ge(x2_in[c], 16)
                nc.scalar.activation(x2h[:, c, :], x2st[:, c, :], ACT.Copy).then_inc(x2_hi, 1)
            act.wait_ge(sc_step, 2)
            tile(0, True)
            with act.Fori(1, NM) as m:
                tile(m, False)

        @block.vector
        def _(dve):
            def weights_lo(f):
                for i in (2 * f, 2 * f + 1):
                    dve.wait_ge(w_hi, i + 1)
                    nc.vector.tensor_tensor(parts[i][2], stage[:, i % NS, :], f32(parts[i][1]), ALU.subtract).then_inc(w_lo, 1)

            def residual(m, t):
                n = m * NCH + t
                dve.wait_ge(yb_done, n + 1)
                dve.wait_ge(x1_in[t], m * 16 + 16)
                nc.vector.tensor_tensor(x1r[t][:, :], pyc[t][:, :], x1r[t][:, :], ALU.add).then_inc(y_free, 1)

            def norm(m, t):
                n = m * NCH + t
                dve.wait_ge(y_free, n + 1 + 4)
                nc.vector.bn_stats(stats[:, :], x1r[t][:, :]).then_inc(lnc_step, 1)
                dve.wait_ge(lnc_step, n * 3 + 1)
                nc.vector.sem_inc(passed, 1)
                nc.vector.bn_aggr(mv[:, :], stats[:, :]).then_inc(lnc_step, 1)
                dve.wait_ge(lnc_step, n * 3 + 2)
                nc.vector.tensor_scalar_add(ve[:, :], mv[:, 1:2], EPS).then_inc(lnc_step, 1)
                dve.wait_ge(rc_done, n + 1)
                nc.vector.tensor_scalar(x1r[t][:, :], x1r[t][:, :], mv[:, 0:1], rstd[:, 0:1], ALU.subtract,
                                        ALU.mult).then_inc(o_ready, 1)

            def tile(m, first):
                for f in range(FB):
                    s = f % 2
                    n = m * 2 * FB + 2 * f
                    if first and f + 1 < FB:
                        weights_lo(f + 1)
                    dve.wait_ge(tanh_done, m * FB + f + 1)
                    nc.vector.scalar_tensor_tensor(out=th[s][:, :], in0=th[s][:, :], scalar=1.0, in1=pgu[2 * s][:, :],
                                                   op0=ALU.add, op1=ALU.mult).then_inc(gu_free, 1)
                    dve.wait_ge(wd_hi, m * FB + f + 1)
                    nc.vector.tensor_tensor(wdl[s][:, :], wdf[:, f, :], f32(wdh[s][:, :]), ALU.subtract).then_inc(wd_lo, 1)
                    if f == 0 and not first:
                        for t in range(NCH):
                            residual(m - 1, t)
                    dve.wait_ge(gu_done, n + 2)
                    dve.wait_ge(gu_free, n + 1 + 4)
                    nc.vector.scalar_tensor_tensor(out=th[s][:, :], in0=pgu[2 * s + 1][:, :], scalar=su2[:, f:f + 1],
                                                   in1=th[s][:, :], op0=ALU.mult, op1=ALU.mult).then_inc(gu_free, 1)
                    if f == FB - 1:
                        for c in range(DC):
                            dve.wait_ge(x2_hi, m * DC + c + DC + 1)
                            nc.vector.tensor_tensor(x2l[:, c, :], x2st[:, c, :], f32(x2h[:, c, :]),
                                                    ALU.subtract).then_inc(x2_lo, 1)
                    dve.wait_ge(h_hi, m * FB + f + 1)
                    nc.vector.tensor_tensor(hl[s][:, :], th[s][:, :], f32(hh[s][:, :]), ALU.subtract).then_inc(h_lo, 1)
                    if f < NCH and not first:
                        norm(m - 1, f)

            dve.wait_ge(sc_in, 32)
            nc.vector.tensor_scalar_mul(sg[:, :], sg[:, :], 0.5).then_inc(sc_step, 1)
            dve.wait_ge(sc_step, 1)
            nc.vector.tensor_tensor(su2[:, :], su2[:, :], sg[:, :], ALU.mult).then_inc(sc_step, 1)
            dve.wait_ge(sc_step, 2)
            weights_lo(0)
            for c in range(DC):
                dve.wait_ge(x2_hi, c + 1)
                nc.vector.tensor_tensor(x2l[:, c, :], x2st[:, c, :], f32(x2h[:, c, :]), ALU.subtract).then_inc(x2_lo, 1)
            tile(0, True)
            with dve.Fori(1, NM) as m:
                tile(m, False)
            for t in range(NCH):
                residual(NM - 1, t)
                norm(NM - 1, t)

        @block.gpsimd
        def _(pool):
            for s, ahead in ((gu_free, 4), (h_lo, 2), (d_done, 2), (y_free, 4)):
                nc.gpsimd.sem_inc(s, ahead)
            nc.gpsimd.memset(neghalf[:], -0.5).then_inc(set_up, 1)
            pool.wait_ge(set_up, 1)
            with pool.Fori(0, NM) as m:
                for t in range(NCH):
                    pool.wait_ge(lnc_step, m * (3 * NCH) + 3 * t + 3)
                    nc.gpsimd.tensor_tensor(rstd[:, :], ve[:, :], neghalf[:, :], ALU.pow).then_inc(rc_done, 1)

        @block.sync
        def _(sp):
            def load_weights(f):
                for i in (2 * f, 2 * f + 1):
                    if i >= NS:
                        sp.wait_ge(w_lo, i - NS + 1)
                    sp.dma_start(stage[:, i % NS, :], (wu if i % 2 else wg)[:, f].rearrange("p c n -> p (c n)"))\
                        .then_inc(w_in[i % NS], 16)

            def load_down(q):
                b = slice(q * FB // 4, (q + 1) * FB // 4)
                sp.dma_start(wdf[:, b, :], wd_d[:, b, :]).then_inc(wd_in[q], 16)

            def write_out(m, t):
                sp.wait_ge(o_ready, m * NCH + t + 1)
                sp.dma_start(out_v[m * NCH + t], x1r[t][:, :]).then_inc(o_out[t], 16)

            def load_x2(m, q):
                sp.wait_ge(x2_lo, m * DC + q + 1)
                sp.dma_start(x2st[:, q, :], x2_d[(m + 1) % NM, :, q, :]).then_inc(x2_in[q], 16)

            def tile(m, first):
                for q in range(DC):
                    load_x2(m, q)
                if not first:
                    for t in range(NCH):
                        write_out(m - 1, t)
                for t in range(NCH):
                    if not first:
                        sp.wait_ge(o_out[t], m * 16)
                    sp.dma_start(x1r[t][:, :], x1_v[m * NCH + t]).then_inc(x1_in[t], 16)

            sp.dma_start(x2st[:, 0, :], x2_d[0, :, 0, :]).then_inc(x2_in[0], 16)
            load_weights(0)
            for c in range(1, DC):
                sp.dma_start(x2st[:, c, :], x2_d[0, :, c, :]).then_inc(x2_in[c], 16)
            sp.dma_start(sg[:, :], wsg).then_inc(sc_in, 16)
            sp.dma_start(su2[:, :], wsu).then_inc(sc_in, 16)
            load_weights(1)
            load_down(0)
            for f in range(2, FB):
                load_weights(f)
                if f % 4 == 2 and f > 2:
                    load_down(f // 4)
            tile(0, True)
            with sp.Fori(1, NM) as m:
                tile(m, False)
            for t in range(NCH):
                write_out(NM - 1, t)
            for t in range(NCH):
                sp.wait_ge(o_out[t], 16 * NM)
            for q in range(DC):
                sp.wait_ge(x2_in[q], 16 * (NM + 1))


def kernel(L0_attn_x, L0_attn_Wq, L0_attn_Wk, L0_attn_Wv, L0_attn_Wo, L0_ffn_SU_ug, L0_ffn_SU_dp,
           L0_ffn_Wscale_ug, L0_ffn_Wscale_dp, L0_ffn_W_up, L0_ffn_W_gate, L0_ffn_W_down):
    import concourse.bacc as bacc
    from concourse.bass_utils import run_bass_kernel_spmd

    lay = np.ascontiguousarray
    x = np.asarray(L0_attn_x).reshape(T, D)

    def cols(v, n):
        return lay(np.asarray(v).reshape(n, P).T)

    inv_freq = (np.float32(1.0) / np.power(np.float32(10000.0), np.arange(0, HD, 2, dtype=np.float32) / np.float32(HD)))
    freqs = np.outer(np.arange(T, dtype=np.float32), inv_freq.astype(np.float32)).T
    cos, sin = np.cos(freqs), np.sin(freqs)
    had = np.ones((1, 1), np.float32)
    while had.shape[0] < P:
        had = np.block([[had, had], [had, -had]])
    arrays = {
        "xT": lay(x.reshape(NM, MT, DC, P).transpose(0, 3, 2, 1)),
        "x": lay(x),
        "wq": lay(np.asarray(L0_attn_Wq).reshape(H, HD, DC, P).transpose(3, 0, 2, 1)),
        "wk": lay(np.asarray(L0_attn_Wk).reshape(KV, HD, DC, P).transpose(3, 0, 2, 1)),
        "wv": lay(np.asarray(L0_attn_Wv).reshape(KV * HD, DC, P).transpose(2, 1, 0)),
        "wo": lay(np.asarray(L0_attn_Wo).reshape(D, H, HD).transpose(2, 1, 0)),
        "wg": lay(np.asarray(L0_ffn_W_gate).reshape(FB, P, DC, P).transpose(3, 0, 2, 1)),
        "wu": lay(np.asarray(L0_ffn_W_up).reshape(FB, P, DC, P).transpose(3, 0, 2, 1)),
        "wd": lay(np.asarray(L0_ffn_W_down).reshape(D, FB, P).transpose(2, 1, 0)),
        "su": cols(L0_ffn_SU_ug, DC),
        "sd": cols(L0_ffn_SU_dp, FB),
        "wsu": cols(np.asarray(L0_ffn_Wscale_ug)[:F], FB),
        "wsg": cols(np.asarray(L0_ffn_Wscale_ug)[F:], FB),
        "wsd": lay(np.asarray(L0_ffn_Wscale_dp).reshape(1, D)),
        "cosT": lay(np.concatenate([cos, cos]).astype(np.float32)),
        "sinT": lay(np.concatenate([-sin, sin]).astype(np.float32)),
        "consts": lay(np.concatenate([np.eye(P, dtype=np.float32), had], axis=1)),
    }
    nc = bacc.Bacc("TRN2", target_bir_lowering=False, num_devices=1, dynamic_dma_scratch_size=1024)
    a = {}
    feed = {}
    for name, v in arrays.items():
        feed[f"in_{name}"] = v
        a[name] = nc.dram_tensor(f"in_{name}", v.shape, F32, kind="ExternalInput").ap()
    out = nc.dram_tensor("out", [T, D], F32, kind="ExternalOutput").ap()

    def scratch(name, shape):
        return nc.dram_tensor(name, shape, F32).ap()

    num_d = scratch("num_scratch", [T // CH, P, H, CH])
    den_d = scratch("den_scratch", [T // CH, H, CH])
    rden_d = scratch("rden_scratch", [T // CH, H * CH])
    x1_d = scratch("x1_scratch", [T, D])
    x2_d = scratch("x2_scratch", [NM, P, DC, MT])
    wd_d = scratch("wd_scratch", [P, FB, D])
    phase_a(nc, a["xT"], a["wq"], a["wk"], a["wv"], a["cosT"], a["sinT"], a["consts"], a["wd"], a["sd"], a["wsd"],
            num_d, den_d, wd_d)
    phase_b(nc, a["x"], a["wo"], a["su"], a["consts"], num_d, den_d, rden_d, x1_d, x2_d)
    phase_c(nc, a["wg"], a["wu"], a["wsg"], a["wsu"], wd_d, x1_d, x2_d, out)
    r = run_bass_kernel_spmd(nc, [feed], core_ids=[0])
    return r.results[0]["out"].reshape(1, T, D)
```
